# Optimizing a Trainium2 kernel written in Bass

```python
import numpy as np
import jax
import jax.numpy as jnp

def _softmax(x, axis=-1):
    return jax.nn.softmax(x, axis=axis)

def _gelu(x):
    return jax.nn.gelu(x, approximate=True)

def _silu(x):
    return jax.nn.silu(x)

def _sigmoid(x):
    return jax.nn.sigmoid(x)

def _layernorm(x, axis=-1, eps=1e-05):
    m = jnp.mean(x, axis=axis, keepdims=True)
    v = jnp.var(x, axis=axis, keepdims=True)
    return (x - m) / jnp.sqrt(v + eps)

def _scatter_add(tgt, idx, src, axis=0):
    return tgt.at[idx].add(src)

def _segment_sum(src, seg, n):
    return jax.ops.segment_sum(src, seg, n)
kernel_name = 'mk_sandwich_d4_jaxref_r8_54d252'

def setup_inputs(seed: int=0):
    np.random.seed(seed)
    _w = jnp.asarray

    def _L0_attn_setup():
        import jax, jax.numpy as jnp
        import numpy as np
        DIM = 128
        B, S = (8, 256)
        LN_EPS = 1e-05
        key = jax.random.key(seed)
        k1, k2, k3 = jax.random.split(key, 3)
        x = jax.random.normal(k1, (B, S, DIM), dtype=jnp.float32)
        w_qkv = jax.random.normal(k2, (3 * DIM, DIM), dtype=jnp.float32) * np.sqrt(2.0 / (DIM + 3 * DIM))
        w_fc = jax.random.normal(k3, (DIM, DIM), dtype=jnp.float32) * np.sqrt(2.0 / (DIM + DIM))
        b_fc = jnp.zeros((DIM,), dtype=jnp.float32)
        gamma = jnp.ones((DIM,), dtype=jnp.float32)
        beta = jnp.zeros((DIM,), dtype=jnp.float32)
        return {'x': x, 'w_qkv': w_qkv, 'w_fc': w_fc, 'b_fc': b_fc, 'gamma': gamma, 'beta': beta}
    _L0_attn_in = _L0_attn_setup()

    def _L0_ffn_setup():
        import jax, jax.numpy as jnp
        import numpy as np
        B, N, D = (4, 256, 128)
        SPARSITY = 0.01
        key = jax.random.key(seed)
        k1, k2, k3 = jax.random.split(key, 3)
        x = jax.random.normal(k1, (B, N, D), dtype=jnp.float32)
        spatial = jax.random.normal(k2, (D, D), dtype=jnp.float32) * 0.02
        freq = jnp.fft.fft(spatial, axis=-1)
        k = int(D * SPARSITY)
        mag = jnp.abs(freq)
        kth = jax.lax.top_k(mag, k)[0][:, -1:]
        w_sparse = jnp.where(mag >= kth, freq, 0.0 + 0j)
        bias = jax.random.normal(k3, (D,), dtype=jnp.float32) * 0.01
        return {'x': x, 'w_freq_real': jnp.real(w_sparse).astype(jnp.float32), 'w_freq_imag': jnp.imag(w_sparse).astype(jnp.float32), 'bias': bias}
    _L0_ffn_in = _L0_ffn_setup()

    def _L1_attn_setup():
        import jax, jax.numpy as jnp
        import numpy as np
        B_SZ, SEQ, D_MODEL = (2, 64, 128)
        EXPAND, HEAD_DIM = (2, 64)
        D_INNER = EXPAND * D_MODEL
        N_HEADS = D_INNER // HEAD_DIM
        D_STATE = 64
        EPS = 1e-06
        PROJ_DIM = 2 * D_INNER + 2 * N_HEADS * D_STATE + N_HEADS

        def _rope(x, theta):
            x0, x1 = (x[..., 0::2], x[..., 1::2])
            c, s = (jnp.cos(theta), jnp.sin(theta))
            y = jnp.stack([x0 * c - x1 * s, x0 * s + x1 * c], axis=-1)
            return y.reshape(x.shape)
        key = jax.random.key(seed)
        k = jax.random.split(key, 5)
        return {'hidden': jax.random.normal(k[0], (B_SZ, SEQ, D_MODEL), jnp.float32), 'W_in': 0.02 * jax.random.normal(k[1], (D_MODEL, PROJ_DIM), jnp.float32), 'dt_bias': 0.5 * jax.random.normal(k[2], (N_HEADS,), jnp.float32), 'A_log': 0.5 * jax.random.normal(k[3], (N_HEADS,), jnp.float32), 'norm_weight': jnp.ones((D_INNER,), jnp.float32), 'W_out': 0.02 * jax.random.normal(k[4], (D_INNER, D_MODEL), jnp.float32)}
    _L1_attn_in = _L1_attn_setup()

    def _L1_ffn_setup():
        import jax, jax.numpy as jnp
        import numpy as np
        D = 128
        E = 8
        H = 256
        TOP_K = 2
        ALPHA = 0.5
        LN_EPS = 1e-05

        def _experts_all(x, W1, b1, W2, b2):
            h = jax.nn.relu(jnp.einsum('bld,edh->eblh', x, W1) + b1[:, None, None, :])
            return jnp.einsum('eblh,ehd->ebld', h, W2) + b2[:, None, None, :]

        def _selected_expert(x, expert_idx, W1, b1, W2, b2):
            oh = jax.nn.one_hot(expert_idx, E, dtype=x.dtype)
            return jnp.einsum('ebld,ble->bld', _experts_all(x, W1, b1, W2, b2), oh)

        def _layer_norm(x, gamma, beta):
            mu = jnp.mean(x, axis=-1, keepdims=True)
            var = jnp.mean(jnp.square(x - mu), axis=-1, keepdims=True)
            return (x - mu) * jax.lax.rsqrt(var + LN_EPS) * gamma + beta
        key = jax.random.key(seed)
        ks = jax.random.split(key, 8)
        x = jax.random.normal(ks[0], (2, 256, D), dtype=jnp.float32)
        gate_W = jax.random.normal(ks[1], (D, E), dtype=jnp.float32) * 0.02
        gate_b = jnp.zeros((E,), dtype=jnp.float32)
        W1 = jax.random.normal(ks[2], (E, D, H), dtype=jnp.float32) * 0.02
        b1 = jnp.zeros((E, H), dtype=jnp.float32)
        W2 = jax.random.normal(ks[3], (E, H, D), dtype=jnp.float32) * 0.02
        b2 = jnp.zeros((E, D), dtype=jnp.float32)
        ln_gamma = jnp.ones((D,), dtype=jnp.float32)
        ln_beta = jnp.zeros((D,), dtype=jnp.float32)
        return {'x': x, 'gate_W': gate_W, 'gate_b': gate_b, 'W1': W1, 'b1': b1, 'W2': W2, 'b2': b2, 'ln_gamma': ln_gamma, 'ln_beta': ln_beta}
    _L1_ffn_in = _L1_ffn_setup()

    def _L2_attn_setup():
        import jax, jax.numpy as jnp
        import numpy as np
        B, T, C, H = (4, 256, 128, 16)
        D = C // H

        def _wkv_parallel(k, v, exp_w, exp_u):
            Tn = k.shape[1]
            exp_k = jnp.exp(k)
            exp_ek_v = exp_k * v
            t_idx = jnp.arange(Tn, dtype=k.dtype)
            log_alpha = jnp.log(exp_w)
            alpha_pow = jnp.exp(t_idx[None, :, None, None] * log_alpha)
            alpha_next_pow = alpha_pow * exp_w
            f_a = exp_ek_v / alpha_next_pow
            f_b = exp_k.sum(-1, keepdims=True) / alpha_next_pow
            cs_a = jnp.cumsum(f_a, axis=1)
            cs_b = jnp.cumsum(f_b, axis=1)
            zero_a = jnp.zeros_like(cs_a[:, :1])
            zero_b = jnp.zeros_like(cs_b[:, :1])
            excl_a = jnp.concatenate([zero_a, cs_a[:, :-1]], axis=1)
            excl_b = jnp.concatenate([zero_b, cs_b[:, :-1]], axis=1)
            state_a = jnp.nan_to_num(alpha_pow * excl_a, nan=0.0, posinf=0.0)
            state_b = jnp.nan_to_num(alpha_pow * excl_b, nan=0.0, posinf=0.0)
            exp_u_k = exp_u * exp_k
            num = state_a + exp_u_k * v
            den = jnp.maximum(state_b + exp_u_k.sum(-1, keepdims=True), 1e-06)
            return num / den
        key = jax.random.key(seed)
        ks = jax.random.split(key, 10)
        s = 1.0 / np.sqrt(C)
        return {'x': jax.random.normal(ks[0], (B, T, C), jnp.float32), 'mix_k': jax.random.uniform(ks[1], (1, 1, C), jnp.float32), 'mix_v': jax.random.uniform(ks[2], (1, 1, C), jnp.float32), 'mix_r': jax.random.uniform(ks[3], (1, 1, C), jnp.float32), 'W_key': jax.random.normal(ks[4], (C, C), jnp.float32) * s, 'W_value': jax.random.normal(ks[5], (C, C), jnp.float32) * s, 'W_receptance': jax.random.normal(ks[6], (C, C), jnp.float32) * s, 'W_output': jax.random.normal(ks[7], (C, C), jnp.float32) * s, 'time_decay': jax.random.normal(ks[8], (H,), jnp.float32) - 5.0, 'time_first': jax.random.normal(ks[9], (H,), jnp.float32)}
    _L2_attn_in = _L2_attn_setup()

    def _L2_ffn_setup():
        import jax, jax.numpy as jnp
        import numpy as np
        HIDDEN = 128
        INTER = 512
        key = jax.random.key(seed)
        k1, k2, k3, k4, k5 = jax.random.split(key, 5)
        hidden_states = jax.random.normal(k1, (4, 256, HIDDEN), dtype=jnp.float32)
        W1 = jax.random.normal(k2, (HIDDEN, INTER), dtype=jnp.float32) * (1.0 / np.sqrt(HIDDEN))
        b1 = jax.random.normal(k3, (INTER,), dtype=jnp.float32) * 0.02
        W2 = jax.random.normal(k4, (INTER, HIDDEN), dtype=jnp.float32) * (1.0 / np.sqrt(INTER))
        b2 = jax.random.normal(k5, (HIDDEN,), dtype=jnp.float32) * 0.02
        return {'hidden_states': hidden_states, 'W1': W1, 'b1': b1, 'W2': W2, 'b2': b2}
    _L2_ffn_in = _L2_ffn_setup()

    def _L3_attn_setup():
        import jax, jax.numpy as jnp
        import numpy as np
        N_HEADS = 16
        key = jax.random.key(seed)
        k_x, k_q, k_k, k_v, k_o = jax.random.split(key, 5)
        N, S, D = (8, 512, 128)
        scale = 0.02
        return {'x': jax.random.normal(k_x, (N, S, D), dtype=jnp.float32), 'Wq': jax.random.normal(k_q, (D, D), dtype=jnp.float32) * scale, 'Wk': jax.random.normal(k_k, (D, D), dtype=jnp.float32) * scale, 'Wv': jax.random.normal(k_v, (D, D), dtype=jnp.float32) * scale, 'Wo': jax.random.normal(k_o, (D, D), dtype=jnp.float32) * scale, 'bo': jnp.zeros((D,), dtype=jnp.float32)}
    _L3_attn_in = _L3_attn_setup()

    def _L3_ffn_setup():
        import jax, jax.numpy as jnp
        import numpy as np
        SQRT_2_PI = 0.7978845608028654
        GELU_COEF = 0.044715
        LN_EPS = 1e-06
        TOP_K = 2

        def gelu_kernel(x):
            inner = SQRT_2_PI * (x + GELU_COEF * x ** 3)
            return 0.5 * x * (1.0 + jnp.tanh(inner))
        key = jax.random.key(seed)
        ks = jax.random.split(key, 8)
        B, S, D, F, E = (2, 256, 128, 512, 8)
        s = lambda d: 1.0 / np.sqrt(d)
        return {'x': jax.random.normal(ks[0], (B, S, D), jnp.float32), 'Wr1': jax.random.normal(ks[1], (D, D // 2), jnp.float32) * s(D), 'br1': jnp.zeros((D // 2,), jnp.float32), 'ln_scale': jnp.ones((D // 2,), jnp.float32), 'ln_bias': jnp.zeros((D // 2,), jnp.float32), 'Wr2': jax.random.normal(ks[2], (D // 2, E), jnp.float32) * s(D // 2), 'br2': jnp.zeros((E,), jnp.float32), 'W1': jax.random.normal(ks[3], (E, D, 2 * F), jnp.float32) * s(D), 'b1': jnp.zeros((E, 2 * F), jnp.float32), 'W2': jax.random.normal(ks[4], (E, F, D), jnp.float32) * s(F), 'b2': jnp.zeros((E, D), jnp.float32)}
    _L3_ffn_in = _L3_ffn_setup()
    _d = {'L0_attn_x': _L0_attn_in['x'], 'L0_attn_w_qkv': _L0_attn_in['w_qkv'], 'L0_attn_w_fc': _L0_attn_in['w_fc'], 'L0_attn_b_fc': _L0_attn_in['b_fc'], 'L0_attn_gamma': _L0_attn_in['gamma'], 'L0_attn_beta': _L0_attn_in['beta'], 'L0_ffn_w_freq_real': _L0_ffn_in['w_freq_real'], 'L0_ffn_w_freq_imag': _L0_ffn_in['w_freq_imag'], 'L0_ffn_bias': _L0_ffn_in['bias'], 'L1_attn_W_in': _L1_attn_in['W_in'], 'L1_attn_dt_bias': _L1_attn_in['dt_bias'], 'L1_attn_A_log': _L1_attn_in['A_log'], 'L1_attn_norm_weight': _L1_attn_in['norm_weight'], 'L1_attn_W_out': _L1_attn_in['W_out'], 'L1_ffn_gate_W': _L1_ffn_in['gate_W'], 'L1_ffn_gate_b': _L1_ffn_in['gate_b'], 'L1_ffn_W1': _L1_ffn_in['W1'], 'L1_ffn_b1': _L1_ffn_in['b1'], 'L1_ffn_W2': _L1_ffn_in['W2'], 'L1_ffn_b2': _L1_ffn_in['b2'], 'L1_ffn_ln_gamma': _L1_ffn_in['ln_gamma'], 'L1_ffn_ln_beta': _L1_ffn_in['ln_beta'], 'L2_attn_mix_k': _L2_attn_in['mix_k'], 'L2_attn_mix_v': _L2_attn_in['mix_v'], 'L2_attn_mix_r': _L2_attn_in['mix_r'], 'L2_attn_W_key': _L2_attn_in['W_key'], 'L2_attn_W_value': _L2_attn_in['W_value'], 'L2_attn_W_receptance': _L2_attn_in['W_receptance'], 'L2_attn_W_output': _L2_attn_in['W_output'], 'L2_attn_time_decay': _L2_attn_in['time_decay'], 'L2_attn_time_first': _L2_attn_in['time_first'], 'L2_ffn_W1': _L2_ffn_in['W1'], 'L2_ffn_b1': _L2_ffn_in['b1'], 'L2_ffn_W2': _L2_ffn_in['W2'], 'L2_ffn_b2': _L2_ffn_in['b2'], 'L3_attn_Wq': _L3_attn_in['Wq'], 'L3_attn_Wk': _L3_attn_in['Wk'], 'L3_attn_Wv': _L3_attn_in['Wv'], 'L3_attn_Wo': _L3_attn_in['Wo'], 'L3_attn_bo': _L3_attn_in['bo'], 'L3_ffn_Wr1': _L3_ffn_in['Wr1'], 'L3_ffn_br1': _L3_ffn_in['br1'], 'L3_ffn_ln_scale': _L3_ffn_in['ln_scale'], 'L3_ffn_ln_bias': _L3_ffn_in['ln_bias'], 'L3_ffn_Wr2': _L3_ffn_in['Wr2'], 'L3_ffn_br2': _L3_ffn_in['br2'], 'L3_ffn_W1': _L3_ffn_in['W1'], 'L3_ffn_b1': _L3_ffn_in['b1'], 'L3_ffn_W2': _L3_ffn_in['W2'], 'L3_ffn_b2': _L3_ffn_in['b2']}
    _x0 = _d['L0_attn_x']
    _d['L0_attn_x'] = jax.random.normal(jax.random.fold_in(jax.random.key(seed), 1), (2, 1024, 128), dtype=_x0.dtype)
    del _x0
    return _d

def reference(L0_attn_x, L0_attn_w_qkv, L0_attn_w_fc, L0_attn_b_fc, L0_attn_gamma, L0_attn_beta, L0_ffn_w_freq_real, L0_ffn_w_freq_imag, L0_ffn_bias, L1_attn_W_in, L1_attn_dt_bias, L1_attn_A_log, L1_attn_norm_weight, L1_attn_W_out, L1_ffn_gate_W, L1_ffn_gate_b, L1_ffn_W1, L1_ffn_b1, L1_ffn_W2, L1_ffn_b2, L1_ffn_ln_gamma, L1_ffn_ln_beta, L2_attn_mix_k, L2_attn_mix_v, L2_attn_mix_r, L2_attn_W_key, L2_attn_W_value, L2_attn_W_receptance, L2_attn_W_output, L2_attn_time_decay, L2_attn_time_first, L2_ffn_W1, L2_ffn_b1, L2_ffn_W2, L2_ffn_b2, L3_attn_Wq, L3_attn_Wk, L3_attn_Wv, L3_attn_Wo, L3_attn_bo, L3_ffn_Wr1, L3_ffn_br1, L3_ffn_ln_scale, L3_ffn_ln_bias, L3_ffn_Wr2, L3_ffn_br2, L3_ffn_W1, L3_ffn_b1, L3_ffn_W2, L3_ffn_b2):

    def _L0_attn_ref(x, w_qkv, w_fc, b_fc, gamma, beta):
        import jax, jax.numpy as jnp
        import numpy as np
        DIM = 128
        B, S = (8, 256)
        LN_EPS = 1e-05
        scaling = DIM ** (-0.5)
        qkv = jnp.einsum('bsd,ed->bse', x, w_qkv)
        q, k, v = jnp.split(qkv, 3, axis=-1)
        att = jax.nn.softmax(jnp.einsum('bqd,bkd->bqk', q, k) * scaling, axis=-1)
        y = jnp.einsum('bqk,bvd->bqd', att, v)
        y = jnp.einsum('bqd,ed->bqe', y, w_fc) + b_fc
        h = x + y
        mu = jnp.mean(h, axis=-1, keepdims=True)
        var = jnp.var(h, axis=-1, keepdims=True)
        return (h - mu) * jax.lax.rsqrt(var + LN_EPS) * gamma + beta

    def _L0_ffn_ref(x, w_freq_real, w_freq_imag, bias):
        import jax, jax.numpy as jnp
        import numpy as np
        B, N, D = (4, 256, 128)
        SPARSITY = 0.01
        w = jax.lax.complex(w_freq_real, w_freq_imag)
        x_freq = jnp.fft.fft(x, axis=-1)
        y_freq = jnp.einsum('bnd,do->bno', x_freq, w)
        y = jnp.real(jnp.fft.ifft(y_freq, axis=-1))
        return y + bias

    def _L1_attn_ref(hidden, W_in, dt_bias, A_log, norm_weight, W_out):
        import jax, jax.numpy as jnp
        import numpy as np
        B_SZ, SEQ, D_MODEL = (2, 64, 128)
        EXPAND, HEAD_DIM = (2, 64)
        D_INNER = EXPAND * D_MODEL
        N_HEADS = D_INNER // HEAD_DIM
        D_STATE = 64
        EPS = 1e-06
        PROJ_DIM = 2 * D_INNER + 2 * N_HEADS * D_STATE + N_HEADS

        def _rope(x, theta):
            x0, x1 = (x[..., 0::2], x[..., 1::2])
            c, s = (jnp.cos(theta), jnp.sin(theta))
            y = jnp.stack([x0 * c - x1 * s, x0 * s + x1 * c], axis=-1)
            return y.reshape(x.shape)
        b, l, _ = hidden.shape
        proj = hidden @ W_in
        hn = N_HEADS * D_STATE
        z = proj[..., :D_INNER]
        xr = proj[..., D_INNER:2 * D_INNER].reshape(b, l, N_HEADS, HEAD_DIM)
        Bm = proj[..., 2 * D_INNER:2 * D_INNER + hn].reshape(b, l, N_HEADS, D_STATE)
        Cm = proj[..., 2 * D_INNER + hn:2 * D_INNER + 2 * hn].reshape(b, l, N_HEADS, D_STATE)
        dt = jax.nn.softplus(proj[..., -N_HEADS:] + dt_bias)
        A = -jnp.exp(A_log)
        alpha = jnp.exp(dt * A)
        beta = 0.5 * dt * alpha
        gamma = 0.5 * dt
        half = D_STATE // 2
        inv_freq = 1.0 / 10000.0 ** (jnp.arange(half, dtype=jnp.float32) / half)
        theta = jnp.cumsum(dt, axis=1)[..., None] * inv_freq
        Bm = _rope(Bm, theta)
        Cm = _rope(Cm, theta)
        Bp = jnp.pad(Bm[:, :-1], ((0, 0), (1, 0), (0, 0), (0, 0)))
        xp = jnp.pad(xr[:, :-1], ((0, 0), (1, 0), (0, 0), (0, 0)))
        tl = lambda t: jnp.moveaxis(t, 1, 0)
        xs = (tl(xr), tl(Bm), tl(Cm), tl(Bp), tl(xp), tl(alpha), tl(beta), tl(gamma))
        h0 = jnp.zeros((b, N_HEADS, D_STATE, HEAD_DIM), hidden.dtype)

        def step(h, inp):
            x_t, B_t, C_t, Bprev, xprev, a, bt, g = inp
            h = a[..., None, None] * h + bt[..., None, None] * jnp.einsum('bhn,bhp->bhnp', Bprev, xprev) + g[..., None, None] * jnp.einsum('bhn,bhp->bhnp', B_t, x_t)
            y = jnp.einsum('bhn,bhnp->bhp', C_t, h)
            return (h, y)
        _, ys = jax.lax.scan(step, h0, xs)
        y = jnp.moveaxis(ys, 0, 1).reshape(b, l, D_INNER)
        y = y * jax.nn.silu(z)
        rms = jnp.sqrt(jnp.mean(y * y, axis=-1, keepdims=True) + EPS)
        y = y / rms * norm_weight
        return y @ W_out

    def _L1_ffn_ref(x, gate_W, gate_b, W1, b1, W2, b2, ln_gamma, ln_beta):
        import jax, jax.numpy as jnp
        import numpy as np
        D = 128
        E = 8
        H = 256
        TOP_K = 2
        ALPHA = 0.5
        LN_EPS = 1e-05

        def _experts_all(x, W1, b1, W2, b2):
            h = jax.nn.relu(jnp.einsum('bld,edh->eblh', x, W1) + b1[:, None, None, :])
            return jnp.einsum('eblh,ehd->ebld', h, W2) + b2[:, None, None, :]

        def _selected_expert(x, expert_idx, W1, b1, W2, b2):
            oh = jax.nn.one_hot(expert_idx, E, dtype=x.dtype)
            return jnp.einsum('ebld,ble->bld', _experts_all(x, W1, b1, W2, b2), oh)

        def _layer_norm(x, gamma, beta):
            mu = jnp.mean(x, axis=-1, keepdims=True)
            var = jnp.mean(jnp.square(x - mu), axis=-1, keepdims=True)
            return (x - mu) * jax.lax.rsqrt(var + LN_EPS) * gamma + beta
        residual = x
        gate_logits = jnp.einsum('bld,de->ble', x, gate_W) + gate_b
        gate_weights = jax.nn.softmax(gate_logits, axis=-1)
        topk_vals, topk_idx = jax.lax.top_k(gate_weights, TOP_K)
        boost = jax.lax.stop_gradient(x)
        outs = []
        for i in range(TOP_K):
            eo = _selected_expert(boost, topk_idx[:, :, i], W1, b1, W2, b2)
            outs.append(eo)
            if i < TOP_K - 1:
                boost = boost + ALPHA * jax.lax.stop_gradient(eo)
        fused = sum((topk_vals[:, :, i:i + 1] * outs[i] for i in range(TOP_K)))
        return _layer_norm(residual + fused, ln_gamma, ln_beta)

    def _L2_attn_ref(x, mix_k, mix_v, mix_r, W_key, W_value, W_receptance, W_output, time_decay, time_first):
        import jax, jax.numpy as jnp
        import numpy as np
        B, T, C, H = (4, 256, 128, 16)
        D = C // H

        def _wkv_parallel(k, v, exp_w, exp_u):
            Tn = k.shape[1]
            exp_k = jnp.exp(k)
            exp_ek_v = exp_k * v
            t_idx = jnp.arange(Tn, dtype=k.dtype)
            log_alpha = jnp.log(exp_w)
            alpha_pow = jnp.exp(t_idx[None, :, None, None] * log_alpha)
            alpha_next_pow = alpha_pow * exp_w
            f_a = exp_ek_v / alpha_next_pow
            f_b = exp_k.sum(-1, keepdims=True) / alpha_next_pow
            cs_a = jnp.cumsum(f_a, axis=1)
            cs_b = jnp.cumsum(f_b, axis=1)
            zero_a = jnp.zeros_like(cs_a[:, :1])
            zero_b = jnp.zeros_like(cs_b[:, :1])
            excl_a = jnp.concatenate([zero_a, cs_a[:, :-1]], axis=1)
            excl_b = jnp.concatenate([zero_b, cs_b[:, :-1]], axis=1)
            state_a = jnp.nan_to_num(alpha_pow * excl_a, nan=0.0, posinf=0.0)
            state_b = jnp.nan_to_num(alpha_pow * excl_b, nan=0.0, posinf=0.0)
            exp_u_k = exp_u * exp_k
            num = state_a + exp_u_k * v
            den = jnp.maximum(state_b + exp_u_k.sum(-1, keepdims=True), 1e-06)
            return num / den
        Bn, Tn, Cn = x.shape
        x_prev = jnp.pad(x, ((0, 0), (1, 0), (0, 0)))[:, :-1]
        k = (x * mix_k + x_prev * (1.0 - mix_k)) @ W_key.T
        v = (x * mix_v + x_prev * (1.0 - mix_v)) @ W_value.T
        r = jax.nn.sigmoid((x * mix_r + x_prev * (1.0 - mix_r)) @ W_receptance.T)
        k4 = k.reshape(Bn, Tn, H, D)
        v4 = v.reshape(Bn, Tn, H, D)
        exp_w = jnp.exp(-jnp.exp(time_decay)).reshape(1, 1, H, 1)
        exp_u = jnp.exp(time_first).reshape(1, 1, H, 1)
        wkv = _wkv_parallel(k4, v4, exp_w, exp_u).reshape(Bn, Tn, Cn)
        return r * wkv @ W_output.T

    def _L2_ffn_ref(hidden_states, W1, b1, W2, b2):
        import jax, jax.numpy as jnp
        import numpy as np
        HIDDEN = 128
        INTER = 512
        h = jax.nn.relu(jnp.einsum('bsh,hi->bsi', hidden_states, W1) + b1)
        return jnp.einsum('bsi,ih->bsh', h, W2) + b2

    def _L3_attn_ref(x, Wq, Wk, Wv, Wo, bo):
        import jax, jax.numpy as jnp
        import numpy as np
        N_HEADS = 16
        N, S, D = x.shape
        H = N_HEADS
        hd = D // H
        q = (x @ Wq.T).reshape(N, S, H, hd).transpose(0, 2, 1, 3)
        k = (x @ Wk.T).reshape(N, S, H, hd).transpose(0, 2, 1, 3)
        v = (x @ Wv.T).reshape(N, S, H, hd).transpose(0, 2, 1, 3)
        att = jnp.einsum('nqhd,nkhd->nhqk', q, k)
        att = jax.nn.softmax(att / jnp.sqrt(jnp.asarray(hd, x.dtype)), axis=3)
        out = jnp.einsum('nhqk,nkhd->nqhd', att, v).reshape(N, S, D)
        return out @ Wo.T + bo

    def _L3_ffn_ref(x, Wr1, br1, ln_scale, ln_bias, Wr2, br2, W1, b1, W2, b2):
        import jax, jax.numpy as jnp
        import numpy as np
        SQRT_2_PI = 0.7978845608028654
        GELU_COEF = 0.044715
        LN_EPS = 1e-06
        TOP_K = 2

        def gelu_kernel(x):
            inner = SQRT_2_PI * (x + GELU_COEF * x ** 3)
            return 0.5 * x * (1.0 + jnp.tanh(inner))
        E = W1.shape[0]
        h = jnp.einsum('bsd,dk->bsk', x, Wr1) + br1
        mu = jnp.mean(h, axis=-1, keepdims=True)
        var = jnp.mean((h - mu) ** 2, axis=-1, keepdims=True)
        h = (h - mu) * jax.lax.rsqrt(var + LN_EPS) * ln_scale + ln_bias
        h = gelu_kernel(h)
        router_logits = jnp.einsum('bsk,ke->bse', h, Wr2) + br2
        routing_probs = jax.nn.softmax(router_logits, axis=-1)
        top_k_probs, top_k_indices = jax.lax.top_k(routing_probs, TOP_K)
        top_k_probs = top_k_probs / jnp.sum(top_k_probs, axis=-1, keepdims=True)
        expert_mask = jnp.sum(jax.nn.one_hot(top_k_indices, E, dtype=x.dtype) * top_k_probs[..., None], axis=-2)
        output = jnp.zeros_like(x)
        for e in range(E):
            x12 = jnp.einsum('bsd,df->bsf', x, W1[e]) + b1[e]
            x1, x2 = jnp.split(x12, 2, axis=-1)
            g = x1 * gelu_kernel(x2)
            y = jnp.einsum('bsf,fd->bsd', g, W2[e]) + b2[e]
            output = output + y * expert_mask[:, :, e][:, :, None]
        return output
    x = L0_attn_x
    x = x + _layernorm(_L0_attn_ref(_layernorm(x, axis=-1), L0_attn_w_qkv, L0_attn_w_fc, L0_attn_b_fc, L0_attn_gamma, L0_attn_beta), axis=-1)
    x = x + _layernorm(_L0_ffn_ref(_layernorm(x, axis=-1), L0_ffn_w_freq_real, L0_ffn_w_freq_imag, L0_ffn_bias), axis=-1)
    x = x + _layernorm(_L1_attn_ref(_layernorm(x, axis=-1), L1_attn_W_in, L1_attn_dt_bias, L1_attn_A_log, L1_attn_norm_weight, L1_attn_W_out), axis=-1)
    x = x + _layernorm(_L1_ffn_ref(_layernorm(x, axis=-1), L1_ffn_gate_W, L1_ffn_gate_b, L1_ffn_W1, L1_ffn_b1, L1_ffn_W2, L1_ffn_b2, L1_ffn_ln_gamma, L1_ffn_ln_beta), axis=-1)
    x = x + _layernorm(_L2_attn_ref(_layernorm(x, axis=-1), L2_attn_mix_k, L2_attn_mix_v, L2_attn_mix_r, L2_attn_W_key, L2_attn_W_value, L2_attn_W_receptance, L2_attn_W_output, L2_attn_time_decay, L2_attn_time_first), axis=-1)
    x = x + _layernorm(_L2_ffn_ref(_layernorm(x, axis=-1), L2_ffn_W1, L2_ffn_b1, L2_ffn_W2, L2_ffn_b2), axis=-1)
    x = x + _layernorm(_L3_attn_ref(_layernorm(x, axis=-1), L3_attn_Wq, L3_attn_Wk, L3_attn_Wv, L3_attn_Wo, L3_attn_bo), axis=-1)
    x = x + _layernorm(_L3_ffn_ref(_layernorm(x, axis=-1), L3_ffn_Wr1, L3_ffn_br1, L3_ffn_ln_scale, L3_ffn_ln_bias, L3_ffn_Wr2, L3_ffn_br2, L3_ffn_W1, L3_ffn_b1, L3_ffn_W2, L3_ffn_b2), axis=-1)
    return x

_drawn_inputs = setup_inputs


def setup_inputs(seed=0):
    import zlib

    import numpy as np

    out = dict(_drawn_inputs(seed))
    spreads = {'L0_attn_b_fc': (0.0, 0.351),
     'L0_attn_gamma': (1.0, 0.2),
     'L0_attn_beta': (0.0, 0.1),
     'L1_attn_norm_weight': (1.0, 0.2),
     'L1_ffn_gate_b': (0.0, 0.468),
     'L1_ffn_b1': (0.0, 0.8),
     'L1_ffn_b2': (0.0, 0.356),
     'L1_ffn_ln_gamma': (1.0, 0.2),
     'L1_ffn_ln_beta': (0.0, 0.1),
     'L3_attn_bo': (0.0, 0.1),
     'L3_ffn_br1': (0.0, 0.1),
     'L3_ffn_ln_scale': (1.0, 0.2),
     'L3_ffn_ln_bias': (0.0, 0.1),
     'L3_ffn_br2': (0.0, 0.1),
     'L3_ffn_b1': (0.0, 0.1),
     'L3_ffn_b2': (0.0, 0.1)}
    factors = {'L1_ffn_gate_W': 3.026,
     'L1_ffn_W1': 3.717,
     'L1_ffn_W2': 4.204,
     'L2_ffn_b1': 2.772,
     'L3_attn_Wq': 5.331,
     'L3_attn_Wk': 6.46}
    for name, (base, spread) in spreads.items():
        noise = np.random.default_rng([zlib.crc32(name.encode()), seed]).standard_normal(out[name].shape)
        drawn = base * np.exp(spread * noise) if base else spread * noise
        out[name] = jnp.asarray(drawn.astype(out[name].dtype))
    for name, factor in factors.items():
        out[name] = (out[name] * factor).astype(out[name].dtype)
    return out
```

```python
import concourse.bass as bass
from concourse import mybir
from contextlib import ExitStack
import numpy as np

F32 = mybir.dt.float32
F32R = mybir.dt.float32r
BF16 = mybir.dt.bfloat16
U32 = mybir.dt.uint32
ALU = mybir.AluOpType
ACT = mybir.ActivationFunctionType
AX = mybir.AxisListType

B, S, D = 2, 1024, 128
P = 128
NT_TILES = B * S // P
TPB = S // P
GT = 4
G = NT_TILES // GT
GW = GT * P
TOK = B * S
STAGES = 8


def columns(widths):
    at, out = 0, {}
    for name, w in widths:
        out[name] = (at, w)
        at += w
    return out, at


H1, N1, P1 = 4, 64, 64
E8 = 8
HID1 = 256
HID2 = 512
F3 = 512
KR = 64
NH3, HD3 = 16, 8

PACK, PACK_W = columns([
    ("ident", 128), ("ones", 128),
    ("wq0", 128), ("wk0", 128), ("wv0", 128), ("wfc", 128), ("bfc", 128), ("gam0", 128), ("bet0", 128),
    ("wr", 128), ("wi", 128), ("cos", 128), ("sin", 128), ("nsin", 128), ("fbias", 128),
    ("win", 1028), ("nw", 2), ("wout", 256), ("dtb", H1), ("alog", H1), ("freq", 32),
    ("upper", 128), ("below", 128), ("shift", 128), ("first", 128), ("mask", 128),
    ("gw", E8), ("gb", E8), ("rank", E8), ("b1m", 16), ("lng", 128), ("lnb", 128),
    ("mk", 1), ("mv", 1), ("mr", 1), ("wkey", 128), ("wval", 128), ("wrec", 128), ("wo2", 128),
    ("td", 1), ("tf", 1), ("blocks", 128), ("time", 1024),
    ("w1f", HID2), ("b1f", 4), ("w2f", 4 * 128), ("b2f", 128),
    ("wq3", 128), ("wk3", 128), ("wv3", 128), ("wo3", 128), ("bo3", 128),
    ("wr1", KR), ("br1", KR), ("lns", KR), ("lnbi", KR), ("wr2", E8), ("br2", E8), ("b1g", 64),
])


def program(nc, x_in, pack, b2s, l1w1, l1w2, l3w1, l3w2, out):
    ctx = ExitStack()
    with ctx:
        sb = lambda n, s, d=F32: ctx.enter_context(nc.sbuf_tensor(n, s, d))
        sem = lambda n: ctx.enter_context(nc.semaphore(n))
        X = sb("X", [P, NT_TILES, D])
        XN = sb("XN", [P, NT_TILES, D])
        NT = [sb(f"NT{i}", [P, TOK]) for i in range(2)]
        XS = sb("XS", [P, GT, D])
        W = sb("W", [P, PACK_W])
        W2S = sb("W2S", [E8, 2 * D])
        STAT = sb("STAT", [P, GT, 6])
        MV = sb("MV", [P, GT, 2])
        VPE = sb("VPE", [P, GT])
        RSTD = sb("RSTD", [P, GT])
        MHALF = sb("MHALF", [P, 64])
        PS = [ctx.enter_context(nc.psum_tensor(f"PS{i}", [P, 512], F32)) for i in range(8)]

        def w(name, a=0, n=None, rows=P):
            at, width = PACK[name]
            return W[0:rows, at + a:at + a + (width - a if n is None else n)]

        c = Common()
        c.nc, c.X, c.XN, c.NT, c.XS, c.w, c.PS, c.W2S = nc, X, XN, NT, XS, w, PS, W2S
        c.STAT, c.MV, c.VPE, c.RSTD, c.MHALF = STAT, MV, VPE, RSTD, MHALF
        c.out = out
        c.var_ready, c.rstd_ready = sem("var_ready"), sem("rstd_ready")
        c.xs_ready, c.xs_copied, c.xs_transposed, c.nt_ready = (
            sem("xs_ready"), sem("xs_copied"), sem("xs_transposed"), sem("nt_ready"))
        c.out_stored = sem("out_stored")
        c.dve = Chain(sem("dve_steps"))
        c.n_var, c.n_front = 0, 0
        loads(c, x_in, pack, b2s)
        if STAGES >= 1:
            l0_attn(c)
        if STAGES >= 2:
            l0_ffn(c)
        if STAGES >= 3:
            l1_attn(c)
        if STAGES >= 4:
            l1_ffn(c, l1w1, l1w2)
        if STAGES >= 5:
            l2_attn(c)
        if STAGES >= 6:
            l2_ffn(c)
        if STAGES >= 7:
            l3_attn(c)
        if STAGES >= 8:
            l3_ffn(c, l3w1, l3w2)
        if STAGES < 8:
            with nc.Block() as block:
                @block.sync
                def _(sp):
                    sp.dma_start(out.rearrange("t p d -> p t d"), X[:, :, :]).then_inc(c.out_stored, 16)
                    sp.wait_ge(c.out_stored, 16)


class Common:
    pass


def cleared(nc, name, used):
    s = nc.alloc_semaphore(name)
    used.append(s)
    return s


class Chain:

    def __init__(self, sem):
        self.sem, self.n = sem, 0

    def link(self, eng, ins):
        self.n += 1
        ins.then_inc(self.sem, 1)
        eng.wait_ge(self.sem, self.n)


def statistics(c, v, tiles, eps):
    nc, n = c.nc, len(tiles)
    for j, t in enumerate(tiles):
        last = nc.vector.bn_stats(c.STAT[:, j, :], t)
    c.dve.link(v, last)
    for j in range(n):
        last = nc.vector.bn_aggr(c.MV[:, j, :], c.STAT[:, j, :])
    c.dve.link(v, last)
    c.n_var += 1
    nc.vector.tensor_scalar(c.VPE[:, 0:n], c.MV[:, 0:n, 1], eps, None, ALU.add).then_inc(c.var_ready, 1)
    v.wait_ge(c.rstd_ready, c.n_var)


def normalise(c, v, outs, tiles):
    for j, (o, t) in enumerate(zip(outs, tiles)):
        last = c.nc.vector.tensor_scalar(o, t, c.MV[:, j, 0:1], c.RSTD[:, j:j + 1], ALU.subtract, ALU.mult)
    return last


def front(c, v, g):
    if c.n_front:
        v.wait_ge(c.xs_transposed, c.n_front)
        v.wait_ge(c.xs_copied, c.n_front)
    tiles = [c.X[:, GT * g + j, :] for j in range(GT)]
    statistics(c, v, tiles, 1e-5)
    normalise(c, v, [c.XS[:, j, :] for j in range(GT)], tiles).then_inc(c.xs_ready, 1)
    c.n_front += 1


def tail(c, v, g, Y):
    residual(c, v, g, Y)
    front(c, v, g)


def residual(c, v, g, Y):
    tiles = [Y[:, j, :] for j in range(GT)]
    statistics(c, v, tiles, 1e-5)
    c.dve.link(v, normalise(c, v, tiles, tiles))
    c.dve.link(v, c.nc.vector.tensor_tensor(c.X[:, GT * g:GT * g + GT, :], c.X[:, GT * g:GT * g + GT, :],
                                            Y[:, 0:GT, :], ALU.add))


def rstds(c, pool, first, count, n=GT):
    for k in range(first, first + count):
        pool.wait_ge(c.var_ready, k + 1)
        c.nc.gpsimd.tensor_tensor(c.RSTD[:, 0:n], c.VPE[:, 0:n], c.MHALF[:, 0:n], ALU.pow)\
            .then_inc(c.rstd_ready, 1)


def keep_xn(c, pool, k, g):
    pool.wait_ge(c.xs_ready, k + 1)
    c.nc.gpsimd.tensor_copy(c.XN[:, GT * g:GT * g + GT, :], c.XS[:, :, :]).then_inc(c.xs_copied, 1)


def transpose_xs(c, pe, k, bank):
    pe.wait_ge(c.xs_ready, k + 1)
    if k:
        pe.wait_ge(c.nt_ready, k)
    for j in range(GT):
        last = c.nc.tensor.transpose(bank[:, P * j:P * j + P], c.XS[:, j, :], c.w("ident"))
    last.then_inc(c.xs_transposed, 1)


def copy_nt(c, act, k, g, nt, bank):
    act.wait_ge(c.xs_transposed, k + 1)
    c.nc.scalar.activation(nt[:, GW * g:GW * g + GW], bank[:, :], ACT.Copy).then_inc(c.nt_ready, 1)


def loads(c, x_in, pack, b2s):
    nc = c.nc
    with ExitStack() as ctx:
        x_loaded = [ctx.enter_context(nc.semaphore(f"x_loaded{g}")) for g in range(G)]
        w_loaded = ctx.enter_context(nc.semaphore("w_loaded"))
        const_ready = ctx.enter_context(nc.semaphore("const_ready"))
        with nc.Block() as block:
            @block.sync
            def _(sp):
                for g in range(G):
                    sp.dma_start(c.X[:, GT * g:GT * g + GT, :],
                                 x_in[GT * g:GT * g + GT].rearrange("t p d -> p t d")).then_inc(x_loaded[g], 16)
                sp.dma_start(c.W2S[:, :], b2s).then_inc(w_loaded, 16)
                sp.wait_ge(w_loaded, 32)

            @block.scalar
            def _(act):
                act.dma_start(c.w("ident", 0, PACK_W), pack).then_inc(w_loaded, 16)
                for g in range(G):
                    copy_nt(c, act, g, g, c.NT[0], c.PS[7])

            @block.tensor
            def _(pe):
                pe.wait_ge(w_loaded, 32)
                for g in range(G):
                    transpose_xs(c, pe, g, c.PS[7])

            @block.gpsimd
            def _(pool):
                nc.gpsimd.memset(c.MHALF[:, :], -0.5).then_inc(const_ready, 1)
                pool.wait_ge(const_ready, 1)
                for g in range(G):
                    rstds(c, pool, g, 1)
                    keep_xn(c, pool, g, g)

            @block.vector
            def _(v):
                for g in range(G):
                    v.wait_ge(x_loaded[g], 16)
                    front(c, v, g)


def l0_attn(c):
    nc, w, PS = c.nc, c.w, c.PS
    SCALE = D ** -0.5
    base = c.n_front
    nv0 = c.n_var
    with ExitStack() as ctx:
        sb = lambda n, s, d=F32: ctx.enter_context(nc.sbuf_tensor(n, s, d))
        sem = lambda n: ctx.enter_context(nc.semaphore(n))
        KT, QT = sb("a0_KT", [P, TOK]), sb("a0_QT", [P, TOK])
        MX, NB, L, AS = sb("a0_MX", [P, 16, 2]), sb("a0_NB", [P, 16]), sb("a0_L", [P, 16]), sb("a0_AS", [P, 16])
        MXC, LH = sb("a0_MXC", [P, 16]), sb("a0_LH", [P, 16, 2])
        NSUM, VS, VB, FB = sb("a0_NS", [P, B]), sb("a0_VS", [P, B]), sb("a0_VB", [P, B, D]), sb("a0_FB", [P, B, D])
        Y = sb("a0_Y", [P, GT, D])
        EJ = sb("a0_E", [P, S])
        qk_done, qk_copied = sem("qk_done"), sem("qk_copied")
        l_half = sem("l_half")
        scores_ready, bias_ready, exp_done = sem("scores_ready"), sem("bias_ready"), sem("exp_done")
        nsum_ready, v_ready, vb_ready, f_ready, fb_ready = (
            sem("nsum_ready"), sem("v_ready"), sem("vb_ready"), sem("f_ready"), sem("fb_ready"))
        dve = c.dve
        with nc.Block() as block:
            @block.tensor
            def _(pe):
                for g in range(G):
                    if g:
                        pe.wait_ge(qk_copied, 2 * g)
                    for j, name in enumerate(("wq0", "wk0")):
                        nc.tensor.matmul(PS[j][:, :], w(name), c.NT[0][:, GW * g:GW * g + GW],
                                         start=True, stop=True).then_inc(qk_done, 1)
                pe.wait_ge(nsum_ready, 1)
                nc.tensor.matmul(PS[2][:, 0:B], w("wv0"), NSUM[:, :], start=True, stop=True).then_inc(v_ready, 1)
                pe.wait_ge(vb_ready, 1)
                for b in range(B):
                    last = nc.tensor.matmul(PS[3][:, b * D:b * D + D], VB[:, b, :], w("wfc"), start=True, stop=True)
                last.then_inc(f_ready, 1)
                pe.wait_ge(qk_copied, 2 * G)
                for t in range(NT_TILES):
                    b, s = t // TPB, t % 2
                    if t >= 2:
                        pe.wait_ge(exp_done, t - 1)
                    for half in range(2):
                        last = nc.tensor.matmul(PS[(0, 4)[s] + half][:, :], QT[:, P * t:P * t + P],
                                                KT[:, S * b + 512 * half:S * b + 512 * half + 512],
                                                start=True, stop=True)
                    last.then_inc(scores_ready, 1)
                for g in range(G):
                    transpose_xs(c, pe, base + g, PS[7])

            @block.scalar
            def _(act):
                for g in range(G):
                    for j, dst in enumerate((QT, KT)):
                        act.wait_ge(qk_done, 2 * g + j + 1)
                        nc.scalar.activation(dst[:, GW * g:GW * g + GW], PS[j][:, :], ACT.Copy).then_inc(qk_copied, 1)
                for t in range(NT_TILES):
                    act.wait_ge(bias_ready, t + 1)
                    if t >= 1:
                        act.wait_ge(exp_done, t)
                    for half in range(2):
                        k = (0, 4)[t % 2] + half
                        if half:
                            act.wait_ge(l_half, t + 1)
                        ins = nc.scalar.activation(EJ[:, 512 * half:512 * half + 512], PS[k][:, :], ACT.Exp,
                                                   bias=NB[:, t:t + 1], scale=SCALE,
                                                   accum_out=LH[:, t, half:half + 1])
                        ins.then_inc(exp_done if half else l_half, 1)
                for g in range(G):
                    copy_nt(c, act, base + g, g, c.NT[1], PS[7])

            @block.gpsimd
            def _(pool):
                rstds_seq = nv0
                for g in range(G):
                    rstds(c, pool, rstds_seq, 3)
                    rstds_seq += 3
                    keep_xn(c, pool, base + g, g)

            @block.vector
            def _(v):
                for b in range(B):
                    last = nc.vector.reduce_sum(NSUM[:, b:b + 1], c.NT[0][:, S * b:S * b + S], axis=AX.X)
                last.then_inc(nsum_ready, 1)
                v.wait_ge(v_ready, 1)
                dve.link(v, nc.vector.tensor_copy(VS[:, :], PS[2][:, 0:B]))
                nc.vector.tensor_copy(VB[:, :, :], VS[:, :].unsqueeze(2).to_broadcast([P, B, D])).then_inc(vb_ready, 1)
                v.wait_ge(f_ready, 1)
                dve.link(v, nc.vector.tensor_copy(FB[:, :, :], PS[3][:, 0:B * D].rearrange("p (b d) -> p b d", b=B)))
                for t in range(NT_TILES):
                    v.wait_ge(scores_ready, t + 1)
                    for half in range(2):
                        last = nc.vector.reduce_max(MX[:, t, half:half + 1], PS[(0, 4)[t % 2] + half][:, :], axis=AX.X)
                    dve.link(v, last)
                    dve.link(v, nc.vector.reduce_max(MXC[:, t:t + 1], MX[:, t, :], axis=AX.X))
                    nc.vector.tensor_scalar(NB[:, t:t + 1], MXC[:, t:t + 1], -SCALE, None, ALU.mult).then_inc(bias_ready, 1)
                v.wait_ge(exp_done, NT_TILES)
                dve.link(v, nc.vector.reduce_sum(L[:, :], LH[:, :, :], axis=AX.X))
                dve.link(v, nc.vector.reciprocal(AS[:, :], L[:, :]))
                dve.link(v, nc.vector.tensor_tensor(AS[:, :], AS[:, :], L[:, :], ALU.mult))
                for g in range(G):
                    b = g // 2
                    ngr = c.XN[:, GT * g:GT * g + GT, :]
                    dve.link(v, nc.vector.tensor_tensor(Y[:, :, :], ngr, rep(w("bfc"), GT), ALU.add))
                    for j in range(GT):
                        t = GT * g + j
                        last = nc.vector.scalar_tensor_tensor(Y[:, j, :], FB[:, b, :], AS[:, t:t + 1], Y[:, j, :],
                                                              ALU.mult, ALU.add)
                    dve.link(v, last)
                    tiles = [Y[:, j, :] for j in range(GT)]
                    statistics(c, v, tiles, 1e-5)
                    dve.link(v, normalise(c, v, tiles, tiles))
                    dve.link(v, nc.vector.tensor_tensor(Y[:, :, :], Y[:, :, :], rep(w("gam0"), GT), ALU.mult))
                    dve.link(v, nc.vector.tensor_tensor(Y[:, :, :], Y[:, :, :], rep(w("bet0"), GT), ALU.add))
                    tail(c, v, g, Y)


def rep(ap, n):
    return ap.unsqueeze(1).to_broadcast([ap.shape[0], n, ap.shape[1]])


def project_tail(c, name, products, bias, nt_out, before=None):
    nc, w, PS = c.nc, c.w, c.PS
    base, nv0 = c.n_front, c.n_var
    with ExitStack() as ctx:
        Y = ctx.enter_context(nc.sbuf_tensor(name + "_Y", [P, GT, D], F32))
        y_made = ctx.enter_context(nc.semaphore(name + "_y_made"))
        y_read = ctx.enter_context(nc.semaphore(name + "_y_read"))
        with nc.Block() as block:
            @block.tensor
            def _(pe):
                for g in range(G + 1):
                    if g < G:
                        if g >= 2:
                            pe.wait_ge(y_read, g - 1)
                        products(pe, g, PS[g % 2]).then_inc(y_made, 1)
                    if g:
                        transpose_xs(c, pe, base + g - 1, PS[7])

            @block.scalar
            def _(act):
                for g in range(G):
                    copy_nt(c, act, base + g, g, nt_out, PS[7])

            @block.gpsimd
            def _(pool):
                for g in range(G):
                    rstds(c, pool, nv0 + 2 * g, 2)
                    keep_xn(c, pool, base + g, g)

            @block.vector
            def _(v):
                for g in range(G):
                    v.wait_ge(y_made, g + 1)
                    made = PS[g % 2][:, :].rearrange("p (t d) -> p t d", t=GT)
                    if bias:
                        ins = nc.vector.tensor_tensor(Y[:, :, :], made, rep(w(bias), GT), ALU.add)
                    else:
                        ins = nc.vector.tensor_copy(Y[:, :, :], made)
                    ins.then_inc(y_read, 1)
                    v.wait_ge(y_read, g + 1)
                    tail(c, v, g, Y)


def l0_ffn(c):
    nc, w, PS = c.nc, c.w, c.PS
    with ExitStack() as ctx:
        sb = lambda n, s, d=F32: ctx.enter_context(nc.sbuf_tensor(n, s, d))
        sem = lambda n: ctx.enter_context(nc.semaphore(n))
        AB, M = sb("f0_AB", [P, 2, D]), sb("f0_M", [P, D])
        ab_made, ab_copied, m_made, m_copied = sem("ab_made"), sem("ab_copied"), sem("m_made"), sem("m_copied")
        with nc.Block() as block:
            @block.tensor
            def _(pe):
                mm = nc.tensor.matmul
                mm(PS[0][:, 0:D], w("wr"), w("cos"), start=True, stop=False)
                mm(PS[0][:, 0:D], w("wi"), w("sin"), start=False, stop=True)
                mm(PS[1][:, 0:D], w("wi"), w("cos"), start=True, stop=False)
                mm(PS[1][:, 0:D], w("wr"), w("nsin"), start=False, stop=True).then_inc(ab_made, 1)
                pe.wait_ge(ab_copied, 2)
                mm(PS[2][:, 0:D], AB[:, 0, :], w("cos"), start=True, stop=False)
                mm(PS[2][:, 0:D], AB[:, 1, :], w("nsin"), start=False, stop=True).then_inc(m_made, 1)

            @block.scalar
            def _(act):
                act.wait_ge(ab_made, 1)
                for k in range(2):
                    nc.scalar.activation(AB[:, k, :], PS[k][:, 0:D], ACT.Copy).then_inc(ab_copied, 1)
                act.wait_ge(m_made, 1)
                nc.scalar.activation(M[:, :], PS[2][:, 0:D], ACT.Copy, scale=1.0 / D).then_inc(m_copied, 1)
                act.wait_ge(m_copied, 1)

        def products(pe, g, bank):
            for j in range(GT):
                t = GT * g + j
                last = nc.tensor.matmul(bank[:, P * j:P * j + P], c.NT[1][:, P * t:P * t + P], M[:, :],
                                        start=True, stop=True)
            return last
        project_tail(c, "f0", products, "fbias", c.NT[0])


def l1_attn(c):
    nc, w, PS = c.nc, c.w, c.PS
    dve = c.dve
    NTI = c.NT[0]
    TH = NT_TILES * H1
    used = []
    with ExitStack() as ctx:
        sb = lambda n, s, d=F32: ctx.enter_context(nc.sbuf_tensor(n, s, d))
        sem = lambda n: ctx.enter_context(nc.semaphore(n))
        SIN, COS = sb("s_SIN", [P, NT_TILES, H1 * 32]), sb("s_COS", [P, NT_TILES, H1 * 32])
        DT, DTA = sb("s_DT", [P, TH]), sb("s_DTA", [P, TH])
        EC, ETP = sb("s_EC", [P, TH]), sb("s_ETP", [P, NT_TILES, 2])
        WS, WED, CD = sb("s_WS", [P, TH]), sb("s_WED", [P, TH]), sb("s_CD", [P, TH])
        YT = sb("s_YT", [P, 2, TOK])
        with ExitStack() as ctx1:
            sb1 = lambda n, s, d=F32: ctx1.enter_context(nc.sbuf_tensor(n, s, d))
            sem1 = lambda n: cleared(nc, n, used)
            RAW, AB, EX, LN = (sb1(n, [P, TH]) for n in ("s_RAW", "s_AB", "s_EX", "s_LN"))
            NEGA, CAR, TOTA, ET = sb1("s_NEGA", [P, H1]), sb1("s_CAR", [P, TH]), sb1("s_TOTA", [P, TH]), sb1("s_ET", [P, TH])
            TOT, CUM = sb1("s_TOT", [P, TH]), sb1("s_CUM", [P, TH])
            ANG, TURN = sb1("s_ANG", [P, TH, 32]), sb1("s_TURN", [P, TH, 32])
            dt_made, ab_ready, soft_ready, a_ready, dt_ready, sums_made = (sem1(n) for n in (
                "dt_made", "ab_ready", "soft_ready", "a_ready", "dt_ready", "sums_made"))
            decay_ready, decays, ang_ready, sin_ready, ex_ready = (sem1(n) for n in (
                "decay_ready", "decays", "ang_ready", "sin_ready", "ex_ready"))
            with nc.Block() as block:
                @block.tensor
                def _(pe):
                    mm = nc.tensor.matmul
                    for t in range(NT_TILES):
                        last = mm(PS[0][:, H1 * t:H1 * t + H1], NTI[:, P * t:P * t + P], w("win", 1024, H1),
                                  start=True, stop=True)
                    last.then_inc(dt_made, 1)
                    pe.wait_ge(dt_ready, 1)
                    for k, (lhs, rhs) in enumerate((("upper", DT), ("ones", DT), ("upper", DTA), ("ones", DTA))):
                        mm(PS[1 + k][:, 0:TH], w(lhs), rhs[:, :], start=True, stop=True)
                    mm(PS[5][:, 0:TH], w("shift"), DT[:, :], start=True, stop=False)
                    mm(PS[5][:, 0:TH - H1], w("first"), DT[:, H1:TH], start=False, stop=True).then_inc(sums_made, 1)

                @block.scalar
                def _(act):
                    nc.scalar.activation(NEGA[:, :], w("alog"), ACT.Exp).then_inc(a_ready, 1)
                    act.wait_ge(ab_ready, 1)
                    nc.scalar.activation(EX[:, :], AB[:, :], ACT.Exp, scale=-1.0).then_inc(ex_ready, 1)
                    act.wait_ge(ex_ready, 1)
                    nc.scalar.activation(LN[:, :], EX[:, :], ACT.Ln, bias=1.0).then_inc(soft_ready, 1)
                    act.wait_ge(decay_ready, 1)
                    nc.scalar.activation(EC[:, :], PS[3][:, 0:TH], ACT.Exp).then_inc(decays, 1)
                    nc.scalar.activation(ET[:, :], TOTA[:, :], ACT.Exp).then_inc(decays, 1)
                    nc.scalar.activation(WED[:, :], AB[:, :], ACT.Exp).then_inc(decays, 1)
                    act.wait_ge(ang_ready, 1)
                    nc.scalar.activation(SIN[:, :, :], ANG[:, :, :].rearrange("p (t h) f -> p t (h f)", h=H1), ACT.Sin)\
                        .then_inc(sin_ready, 1)
                    nc.scalar.activation(COS[:, :, :], ANG[:, :, :].rearrange("p (t h) f -> p t (h f)", h=H1), ACT.Sin,
                                         scale=0.5).then_inc(sin_ready, 1)

                @block.vector
                def _(v):
                    tt, ts, stt = nc.vector.tensor_tensor, nc.vector.tensor_scalar, nc.vector.scalar_tensor_tensor
                    v.wait_ge(dt_made, 1)
                    th = lambda a: a[:, :].rearrange("p (t h) -> p t h", h=H1)
                    dve.link(v, tt(th(RAW), PS[0][:, 0:TH].rearrange("p (t h) -> p t h", h=H1),
                                   rep(w("dtb"), NT_TILES), ALU.add))
                    stt(AB[:, :], RAW[:, :], -1.0, RAW[:, :], ALU.mult, ALU.max).then_inc(ab_ready, 1)
                    v.wait_ge(soft_ready, 1)
                    dve.link(v, stt(DT[:, :], RAW[:, :], 0.0, LN[:, :], ALU.max, ALU.add))
                    v.wait_ge(a_ready, 1)
                    dve.link(v, ts(NEGA[:, :], NEGA[:, :], -1.0, None, ALU.mult))
                    tt(th(DTA), th(DT), rep(NEGA[:, :], NT_TILES), ALU.mult).then_inc(dt_ready, 1)
                    v.wait_ge(sums_made, 1)
                    dve.link(v, nc.vector.tensor_copy(TOTA[:, :], PS[4][:, 0:TH]))
                    dve.link(v, tt(AB[:, :], TOTA[:, :], PS[3][:, 0:TH], ALU.subtract))
                    nc.vector.tensor_copy(TOT[:, :], PS[2][:, 0:TH]).then_inc(decay_ready, 1)
                    v.wait_ge(decay_ready, 1)
                    bc = lambda a, k: a[:, :].rearrange("p (b c h) -> p b c h", b=B, h=H1)[:, :, k, :]
                    dve.link(v, nc.vector.memset(bc(CAR, 0), 0.0))
                    for k in range(1, TPB):
                        dve.link(v, tt(bc(CAR, k), bc(CAR, k - 1), bc(TOT, k - 1), ALU.add))
                    dve.link(v, tt(CUM[:, :], CAR[:, :], PS[1][:, 0:TH], ALU.add))
                    ts_magic = 12582912.0
                    dve.link(v, tt(ANG[:, :, :], CUM[:, :].unsqueeze(2).to_broadcast([P, TH, 32]),
                                   rep(w("freq"), TH), ALU.mult))
                    dve.link(v, ts(TURN[:, :, :], ANG[:, :, :], 1.0 / (2 * np.pi), ts_magic, ALU.mult, ALU.add))
                    dve.link(v, ts(TURN[:, :, :], TURN[:, :, :], ts_magic, None, ALU.subtract))
                    for part in turn_parts():
                        dve.link(v, stt(ANG[:, :, :], TURN[:, :, :], -part, ANG[:, :, :], ALU.mult, ALU.add))
                    lim = float(np.nextafter(np.float32(np.pi), np.float32(0)))
                    ts(ANG[:, :, :], ANG[:, :, :], lim, -lim, ALU.min, ALU.max).then_inc(ang_ready, 1)
                    dve.link(v, ts(CD[:, :], PS[5][:, 0:TH], 0.5, None, ALU.mult))
                    dve.link(v, stt(WS[:, :], DT[:, :], 0.5, CD[:, :], ALU.mult, ALU.add))
                    v.wait_ge(decays, 3)
                    dve.link(v, tt(WED[:, :], WED[:, :], WS[:, :], ALU.mult))
                    for r in range(2):
                        last = nc.vector.tensor_copy(ETP[64 * r:64 * r + 64, :, :],
                                                     th(ET)[64 * r:64 * r + 64, :, r::2])
                    dve.link(v, last)
                    v.wait_ge(sin_ready, 2)
                    dve.link(v, tt(COS[:, :, :], COS[:, :, :], COS[:, :, :], ALU.mult))
                    dve.link(v, ts(COS[:, :, :], COS[:, :, :], -2.0, 1.0, ALU.mult, ALU.add))

        with ExitStack() as ctx1:
            sb1 = lambda n, s, d=F32: ctx1.enter_context(nc.sbuf_tensor(n, s, d))
            sem1 = lambda n: cleared(nc, n, used)
            two = lambda n, s: [sb1(f"{n}{i}", s) for i in range(2)]
            ZX, EZ = two("s_ZX", [P, 512]), two("s_EZ", [P, 256])
            PR = sb1("s_PR", [P, 4, 256])
            R = two("s_R", [P, 2, H1, 2, 32])
            CS = sb1("s_CS", [P, H1, 64])
            SL = sb1("s_SL", [P, H1, P])
            TB, TC = two("s_TB", [P, 512]), two("s_TC", [P, 256])
            ED = two("s_ED", [P, 512])
            XW, XD = two("s_XW", [P, H1, 64]), two("s_XD", [P, H1, 64])
            CB, CC = sb1("s_CB", [P, H1, 64]), two("s_CC", [P, H1])
            GE, H = sb1("s_GE", [P, 512]), sb1("s_H", [P, 2, P])
            YG, SG, SS, RR, XC = (sb1("s_YG", [P, 256]), sb1("s_SG", [P, 256]), sb1("s_SS", [P, 1]),
                                  sb1("s_RR", [P, 1]), sb1("s_XC", [P, 256]))
            SQ = sb1("s_SQ", [P, 256])
            (proj_made, zx_copied, ez_ready, prods_ready, rot_ready, cs_ready, sl_ready, decay_made, decay_read,
             turned, turned_copied, g_made, ge_ready, xw_ready, y_made, y_read, h_ready, yg_ready, ss_ready,
             rr_ready, yn_ready, yt_made, yt_copied, cc_ready, h_zero, sg_ready, rr_in, g_half) = (
                sem1("ssd_" + n) for n in (
                    "proj_made", "zx_copied", "ez_ready", "prods_ready", "rot_ready", "cs_ready", "sl_ready",
                    "decay_made", "decay_read", "turned", "turned_copied", "g_made", "ge_ready", "xw_ready",
                    "y_made", "y_read", "h_ready", "yg_ready", "ss_ready", "rr_ready", "yn_ready", "yt_made",
                    "yt_copied", "cc_ready", "h_zero", "sg_ready", "rr_in", "g_half"))
            zb, bb, db, tb, tcb, gb, yb, ob = PS[0], PS[1], PS[2], PS[3], PS[4], PS[5], PS[6], PS[7]
            BCV = bb[:, :].rearrange("p (c h e f) -> p (c h) e f", c=2, h=H1, e=2)
            rsel = lambda r, k: r[:, k, :, :, :].rearrange("p h e f -> p h (e f)")
            steps = range(NT_TILES + 1)
            with nc.Block() as block:
                @block.tensor
                def _(pe):
                    mm, tr = nc.tensor.matmul, nc.tensor.transpose
                    for i in steps:
                        if i < NT_TILES:
                            t = i
                            if t:
                                pe.wait_ge(zx_copied, t)
                                pe.wait_ge(ez_ready, t)
                                pe.wait_ge(prods_ready, t)
                            for k, bank in enumerate((zb, bb)):
                                last = mm(bank[:, :], NTI[:, P * t:P * t + P], w("win", 512 * k, 512),
                                          start=True, stop=True)
                            last.then_inc(proj_made, 1)
                            pe.wait_ge(sl_ready, t + 1)
                            if t:
                                pe.wait_ge(decay_read, t)
                            for h in range(H1):
                                last = mm(db[:, P * h:P * h + P], SL[:, h, :], w("upper"), start=True, stop=False)
                                last = mm(db[:, P * h:P * h + P], w("ident"), w("mask"), start=False, stop=True)
                            last.then_inc(decay_made, 1)
                            pe.wait_ge(rot_ready, t + 1)
                            pe.wait_ge(cs_ready, t + 1)
                            if t:
                                pe.wait_ge(turned_copied, 2 * t)
                            for k in range(2):
                                for pair in range(2):
                                    tr(tb[:, 256 * k + P * pair:256 * k + P * pair + P],
                                       rsel(R[t % 2], k)[:, 2 * pair:2 * pair + 2, :].rearrange("p h n -> p (h n)"),
                                       w("ident"))
                            for pair in range(2):
                                last = tr(tcb[:, P * pair:P * pair + P],
                                          CS[:, 2 * pair:2 * pair + 2, :].rearrange("p h n -> p (h n)"), w("ident"))
                            last.then_inc(turned, 1)
                        if i:
                            t = i - 1
                            pe.wait_ge(turned_copied, 2 * t + 2)
                            if t:
                                pe.wait_ge(ge_ready, t)
                            for h in (0, 2, 1, 3):
                                r, q = 64 * (h % 2), P * (h // 2)
                                if h == 1:
                                    last.then_inc(g_half, 1)
                                    pe.wait_ge(g_half, t + 1)
                                last = mm(gb[:, P * h:P * h + P], TB[t % 2][r:r + 64, q:q + P],
                                          TB[t % 2][r:r + 64, 256 + q:256 + q + P], start=True, stop=True)
                            last.then_inc(g_made, 1)
                            pe.wait_ge(ge_ready, t + 1)
                            pe.wait_ge(xw_ready, t + 1)
                            if t:
                                pe.wait_ge(y_read, t)
                                pe.wait_ge(h_ready, t)
                            first = True
                            if t % TPB:
                                for pair in range(2):
                                    mm(yb[:, P * pair:P * pair + P], TC[t % 2][:, P * pair:P * pair + P], H[:, pair, :],
                                       start=first, stop=False, skip_group_check=True)
                                    first = False
                            for h in range(H1):
                                mm(yb[:, 64 * h:64 * h + 64], GE[:, P * h:P * h + P], XW[t % 2][:, h, :],
                                   start=first, stop=True, skip_group_check=True)
                                first = False
                            for pair in range(2):
                                last = mm(yb[:, 256 + P * pair:256 + P * pair + P],
                                          rsel(R[t % 2], 0)[:, 2 * pair:2 * pair + 2, :].rearrange("p h n -> p (h n)"),
                                          XD[t % 2][:, 2 * pair:2 * pair + 2, :].rearrange("p h n -> p (h n)"),
                                          start=False, stop=True, skip_group_check=True)
                            last.then_inc(y_made, 1)
                            pe.wait_ge(yn_ready, t + 1)
                            if t:
                                pe.wait_ge(yt_copied, t)
                            for pair in range(2):
                                last = tr(ob[:, P * pair:P * pair + P], YG[:, P * pair:P * pair + P], w("ident"))
                            last.then_inc(yt_made, 1)

                @block.scalar
                def _(act):
                    av = nc.scalar.activation
                    for i in steps:
                        if i < NT_TILES:
                            t = i
                            act.wait_ge(proj_made, t + 1)
                            if t >= 2:
                                act.wait_ge(yg_ready, t - 1)
                                act.wait_ge(xw_ready, t - 1)
                                act.wait_ge(sg_ready, t - 1)
                            av(ZX[t % 2][:, :], zb[:, :], ACT.Copy).then_inc(zx_copied, 1)
                            av(EZ[t % 2][:, :], zb[:, 0:256], ACT.Exp, scale=-1.0).then_inc(ez_ready, 1)
                            act.wait_ge(decay_made, t + 1)
                            if t >= 2:
                                act.wait_ge(ge_ready, t - 1)
                            av(ED[t % 2][:, :], db[:, :], ACT.Exp).then_inc(decay_read, 1)
                            act.wait_ge(turned, t + 1)
                            if t >= 2:
                                act.wait_ge(y_made, t - 1)
                            av(TB[t % 2][:, :], tb[:, :], ACT.Copy).then_inc(turned_copied, 1)
                            av(TC[t % 2][:, :], tcb[:, 0:256], ACT.Copy).then_inc(turned_copied, 1)
                        if i:
                            t = i - 1
                            act.wait_ge(yg_ready, t + 1)
                            if t:
                                act.wait_ge(ss_ready, t)
                                act.wait_ge(rr_in, t)
                            av(SQ[:, :], YG[:, :], ACT.Square, accum_out=SS[:, :]).then_inc(ss_ready, 1)
                            act.wait_ge(yt_made, t + 1)
                            for pair in range(2):
                                last = av(YT[:, pair, P * t:P * t + P], ob[:, P * pair:P * pair + P], ACT.Copy,
                                          scale=w("nw", pair, 1))
                            last.then_inc(yt_copied, 1)

                @block.gpsimd
                def _(pool):
                    gt = nc.gpsimd.tensor_tensor
                    for i in steps:
                        if i < NT_TILES:
                            t, hs = i, slice(H1 * i, H1 * i + H1)
                            if t:
                                pool.wait_ge(decay_made, t)
                            gt(SL[:, :, :], rep(w("below"), H1), DTA[:, hs].unsqueeze(2).to_broadcast([P, H1, P]),
                               ALU.mult).then_inc(sl_ready, 1)
                            pool.wait_ge(prods_ready, t + 1)
                            if t >= 2:
                                pool.wait_ge(y_made, t - 1)
                                pool.wait_ge(cc_ready, t - 1)
                            pr = lambda k: PR[:, k, :].rearrange("p (c f) -> p c f", f=32)
                            ro = lambda e: R[t % 2][:, :, :, e, :].rearrange("p c h f -> p (c h) f")
                            gt(ro(0), pr(0), pr(1), ALU.subtract)
                            gt(ro(1), pr(2), pr(3), ALU.add).then_inc(rot_ready, 1)
                            pool.wait_ge(rot_ready, t + 1)
                            if t:
                                pool.wait_ge(turned, t)
                            gt(CS[:, :, :], rsel(R[t % 2], 1), EC[:, hs].unsqueeze(2).to_broadcast([P, H1, 64]),
                               ALU.mult).then_inc(cs_ready, 1)
                            pool.wait_ge(zx_copied, t + 1)
                            if t >= 2:
                                pool.wait_ge(y_made, t - 1)
                            xh = ZX[t % 2][:, 256:512].rearrange("p (h n) -> p h n", h=H1)
                            gt(XW[t % 2][:, :, :], xh, WS[:, hs].unsqueeze(2).to_broadcast([P, H1, 64]), ALU.mult)
                            gt(XD[t % 2][:, :, :], xh, WED[:, hs].unsqueeze(2).to_broadcast([P, H1, 64]), ALU.mult)\
                                .then_inc(xw_ready, 1)
                        if i:
                            t = i - 1
                            pool.wait_ge(rr_in, t + 1)
                            gt(RR[:, :], SS[:, :], c.MHALF[:, 0:1], ALU.pow).then_inc(rr_ready, 1)

                @block.vector
                def _(v):
                    tt, ts, stt = nc.vector.tensor_tensor, nc.vector.tensor_scalar, nc.vector.scalar_tensor_tensor
                    nc.vector.memset(H[:, :, :], 0.0).then_inc(h_zero, 1)
                    v.wait_ge(h_zero, 1)
                    for i in steps:
                        if i < NT_TILES:
                            t, hs = i, slice(H1 * i, H1 * i + H1)
                            v.wait_ge(proj_made, t + 1)
                            if t:
                                v.wait_ge(rot_ready, t)
                            cs, sn = (a[:, t, :].rearrange("p (h f) -> p h f", h=H1) for a in (COS, SIN))
                            for k, (e, tr) in enumerate(((0, cs), (1, sn), (0, sn), (1, cs))):
                                for cc in range(2):
                                    last = tt(PR[:, k, P * cc:P * cc + P].rearrange("p (h f) -> p h f", h=H1),
                                              BCV[:, H1 * cc:H1 * cc + H1, e, :], tr, ALU.mult)
                            last.then_inc(prods_ready, 1)
                            v.wait_ge(prods_ready, t + 1)
                            v.wait_ge(rot_ready, t + 1)
                            dve.link(v, tt(CB[:, :, :], rsel(R[t % 2], 0), rsel(R[t % 2], 1), ALU.mult))
                            dve.link(v, nc.vector.reduce_sum(CC[t % 2][:, :], CB[:, :, :], axis=AX.X))
                            tt(CC[t % 2][:, :], CC[t % 2][:, :], CD[:, hs], ALU.mult).then_inc(cc_ready, 1)
                            v.wait_ge(cc_ready, t + 1)
                        if i:
                            t = i - 1
                            v.wait_ge(g_made, t + 1)
                            v.wait_ge(decay_read, t + 1)
                            if t:
                                v.wait_ge(y_made, t)
                            tt(GE[:, :], gb[:, :], ED[t % 2][:, :], ALU.mult).then_inc(ge_ready, 1)
                            v.wait_ge(ez_ready, t + 1)
                            v.wait_ge(zx_copied, t + 1)
                            dve.link(v, ts(SG[:, :], EZ[t % 2][:, :], 1.0, None, ALU.add))
                            dve.link(v, nc.vector.reciprocal(SG[:, :], SG[:, :]))
                            tt(SG[:, :], SG[:, :], ZX[t % 2][:, 0:256], ALU.mult).then_inc(sg_ready, 1)
                            xh = ZX[t % 2][:, 256:512].rearrange("p (h n) -> p h n", h=H1)
                            dve.link(v, tt(XC[:, :].rearrange("p (h n) -> p h n", h=H1), xh,
                                           CC[t % 2][:, :].unsqueeze(2).to_broadcast([P, H1, 64]), ALU.mult))
                            v.wait_ge(y_made, t + 1)
                            if t:
                                v.wait_ge(yt_made, t)
                            tt(YG[:, :], yb[:, 0:256], XC[:, :], ALU.subtract).then_inc(y_read, 1)
                            for pair in range(2):
                                for r in range(2):
                                    rows, cols = slice(64 * r, 64 * r + 64), slice(64 * r, 64 * r + 64)
                                    src = yb[rows, 256 + P * pair + 64 * r:256 + P * pair + 64 * r + 64]
                                    if t % TPB == 0:
                                        last = nc.vector.tensor_copy(H[rows, pair, cols], src)
                                    else:
                                        last = stt(H[rows, pair, cols], H[rows, pair, cols],
                                                   ETP[rows, t, pair:pair + 1], src, ALU.mult, ALU.add)
                            last.then_inc(h_ready, 1)
                            v.wait_ge(y_read, t + 1)
                            v.wait_ge(sg_ready, t + 1)
                            tt(YG[:, :], YG[:, :], SG[:, :], ALU.mult).then_inc(yg_ready, 1)
                            v.wait_ge(ss_ready, t + 1)
                            if t:
                                v.wait_ge(rr_ready, t)
                            ts(SS[:, :], SS[:, :], 1.0 / 256, 1e-6, ALU.mult, ALU.add).then_inc(rr_in, 1)
                            v.wait_ge(rr_ready, t + 1)
                            ts(YG[:, :], YG[:, :], RR[:, 0:1], None, ALU.mult).then_inc(yn_ready, 1)

        def products(pe, g, bank):
            for j in range(GT):
                t = GT * g + j
                for k in range(2):
                    last = nc.tensor.matmul(bank[:, P * j:P * j + P], YT[:, k, P * t:P * t + P], w("wout", D * k, D),
                                            start=(k == 0), stop=(k == 1))
            return last
        nc.clear_and_free_semaphores(used)
        nc.all_engine_barrier()
        project_tail(c, "s1", products, None, c.NT[1])


def turn_parts():
    a = 6.28125
    b = float(np.float32(np.round((2 * np.pi - a) * 2 ** 20) / 2 ** 20))
    return a, b, 2 * np.pi - a - b


def softmax_top2(c, v, LG, T, probs_exp):
    nc, w, link = c.nc, c.w, c.dve.link
    tt, ts, stt = nc.vector.tensor_tensor, nc.vector.tensor_scalar, nc.vector.scalar_tensor_tensor
    n = NT_TILES
    bc = lambda a: a[:, :].unsqueeze(2).to_broadcast([P, n, E8])
    rmax = lambda o, a: link(v, nc.vector.reduce_max(o[:, :], a[:, :, :], axis=AX.X))
    exp_wanted, exp_done = probs_exp
    rmax(T.MX, LG)
    tt(T.A[:, :, :], LG[:, :, :], bc(T.MX), ALU.subtract).then_inc(exp_wanted, 1)
    v.wait_ge(exp_done, 1)
    link(v, nc.vector.reduce_sum(T.MX[:, :], T.PB[:, :, :], axis=AX.X))
    link(v, nc.vector.reciprocal(T.MX[:, :], T.MX[:, :]))
    link(v, tt(T.PB[:, :, :], T.PB[:, :, :], bc(T.MX), ALU.mult))
    for oh, m in ((T.OH1, T.M1), (T.OH2, T.M2)):
        rmax(m, T.PB)
        link(v, tt(T.A[:, :, :], T.PB[:, :, :], bc(m), ALU.is_equal))
        link(v, tt(T.A[:, :, :], T.A[:, :, :], rep(w("rank"), n), ALU.mult))
        rmax(T.MX, T.A)
        link(v, tt(oh[:, :, :], T.A[:, :, :], bc(T.MX), ALU.is_equal))
        if oh is T.OH1:
            link(v, stt(T.PB[:, :, :], oh[:, :, :], -2.0, T.PB[:, :, :], ALU.mult, ALU.add))


def choice_tiles(sb, tag):
    T = Common()
    T.A, T.PB, T.OH1, T.OH2 = (sb(f"{tag}_{n}", [P, NT_TILES, E8]) for n in ("A", "PB", "OH1", "OH2"))
    T.MX, T.M1, T.M2 = (sb(f"{tag}_{n}", [P, NT_TILES]) for n in ("MX", "M1", "M2"))
    return T


def start_outputs(c, tag, OH, ACC, b2, boost=None):
    nc, w, PS = c.nc, c.w, c.PS
    with ExitStack() as ctx:
        OHT = ctx.enter_context(nc.sbuf_tensor(tag + "_OHT", [E8, TOK], F32))
        sem = lambda n: ctx.enter_context(nc.semaphore(tag + n))
        oh_turned, oh_copied, b_made, b_copied, bo_ready, bo_turned, bo_copied = (sem(n) for n in (
            "_oh_turned", "_oh_copied", "_b_made", "_b_copied", "_bo_ready", "_bo_turned", "_bo_copied"))
        with nc.Block() as block:
            @block.tensor
            def _(pe):
                for g in range(G):
                    for j in range(GT):
                        last = nc.tensor.transpose(PS[g][0:E8, P * j:P * j + P], OH[:, GT * g + j, :], w("ident"))
                    last.then_inc(oh_turned, 1)
                for g in range(G):
                    pe.wait_ge(oh_copied, g + 1)
                    for j in range(GT):
                        t = GT * g + j
                        last = nc.tensor.matmul(PS[4 + g % 2][:, P * j:P * j + P], OHT[:, P * t:P * t + P], b2,
                                                start=True, stop=True)
                    last.then_inc(b_made, 1)
                    pe.wait_ge(b_copied, g + 1)
                if boost:
                    for g in range(G):
                        pe.wait_ge(bo_ready, g + 1)
                        if g >= 2:
                            pe.wait_ge(bo_copied, g - 1)
                        for j in range(GT):
                            last = nc.tensor.transpose(PS[6 + g % 2][:, P * j:P * j + P], boost[1][:, GT * g + j, :],
                                                       w("ident"))
                        last.then_inc(bo_turned, 1)

            @block.scalar
            def _(act):
                for g in range(G):
                    act.wait_ge(oh_turned, g + 1)
                    nc.scalar.activation(OHT[:, GW * g:GW * g + GW], PS[g][0:E8, :], ACT.Copy).then_inc(oh_copied, 1)
                for g in range(G):
                    act.wait_ge(b_made, g + 1)
                    nc.scalar.activation(ACC[:, GT * g:GT * g + GT, :],
                                         PS[4 + g % 2][:, :].rearrange("p (t d) -> p t d", t=GT), ACT.Copy)\
                        .then_inc(b_copied, 1)
                if boost:
                    for g in range(G):
                        act.wait_ge(bo_turned, g + 1)
                        nc.scalar.activation(boost[0][:, GW * g:GW * g + GW], PS[6 + g % 2][:, :], ACT.Copy)\
                            .then_inc(bo_copied, 1)

            @block.vector
            def _(v):
                if boost:
                    for g in range(G):
                        gs = slice(GT * g, GT * g + GT)
                        nc.vector.scalar_tensor_tensor(boost[1][:, gs, :], boost[2][:, gs, :], 0.5, c.XN[:, gs, :],
                                                       ALU.mult, ALU.add).then_inc(bo_ready, 1)


def start_sums(c, tag, OH, ACC, b2, MT, sums, split):
    nc, w, PS = c.nc, c.w, c.PS
    with ExitStack() as ctx:
        OHT = c.NT[0][0:E8, :]
        REST = ctx.enter_context(nc.sbuf_tensor(tag + "_REST", [E8, TOK], F32)) if split else None
        MID = ctx.enter_context(nc.sbuf_tensor(tag + "_MID", [E8, TOK], BF16)) if split else None
        oh_turned, oh_copied, b_made, b_copied = sums
        with nc.Block() as block:
            @block.tensor
            def _(pe):
                for g in range(G):
                    for j in range(GT):
                        last = nc.tensor.transpose(PS[g][0:E8, P * j:P * j + P], OH[:, GT * g + j, :], w("ident"))
                    last.then_inc(oh_turned, 1)
                for g in range(G):
                    pe.wait_ge(oh_copied, g + 1)
                    nc.tensor.matmul(PS[4 + g][:, :], b2, OHT[:, GW * g:GW * g + GW], start=True, stop=True)\
                        .then_inc(b_made, 1)

            @block.scalar
            def _(act):
                for g in range(G):
                    act.wait_ge(oh_turned, g + 1)
                    nc.scalar.activation(OHT[:, GW * g:GW * g + GW], PS[g][0:E8, :], ACT.Copy).then_inc(oh_copied, 1)
                for g in range(G):
                    act.wait_ge(b_made, g + 1)
                    nc.scalar.activation(ACC[:, GW * g:GW * g + GW], PS[4 + g][:, :], ACT.Copy).then_inc(b_copied, 1)

            @block.vector
            def _(v):
                cp, tt, link = nc.vector.tensor_copy, nc.vector.tensor_tensor, c.dve.link
                v.wait_ge(oh_copied, G)
                if not split:
                    cp(MT[:, :], OHT[:, :])
                else:
                    link(v, nc.vector.memset(MT[:, :].bitcast(U32), 0))
                    link(v, cp(MT[0:E8, :], OHT[:, :]))
                    link(v, tt(REST[:, :], OHT[:, :], MT[0:E8, :], ALU.subtract))
                    link(v, cp(MID[:, :], REST[:, :]))
                    cp(MT[32:32 + E8, :], MID[:, :])
                    link(v, tt(REST[:, :], REST[:, :], MID[:, :], ALU.subtract))
                    cp(MT[64:64 + E8, :], REST[:, :])


def expert_masks(c, v, SEL, SELF, rows):
    nc, w, link = c.nc, c.w, c.dve.link
    link(v, nc.vector.tensor_copy(SELF[0:rows, :], w("ident", 0, E8)[0:rows, :]))
    for part in range(32, rows, 32):
        link(v, nc.vector.tensor_tensor(SELF[0:rows, :], SELF[0:rows, :], w("ident", part, E8)[0:rows, :], ALU.add))
    link(v, nc.vector.tensor_copy(SEL[:, :, :], SELF[0:rows, :].unsqueeze(2).to_broadcast([rows, E8, P])))


def load_experts(c, sp, W1, W2, w1_dram, w2_dram, loaded):
    for e in range(E8):
        sp.dma_start(W1[:, e, :], w1_dram[e]).then_inc(loaded[e], 16)
        sp.dma_start(W2[:, e, :, :], w2_dram[e]).then_inc(loaded[e], 16)


def l1_ffn(c, w1_dram, w2_dram):
    nc, w, PS = c.nc, c.w, c.PS
    dve = c.dve
    NTI = c.NT[1]
    with ExitStack() as ctx:
        sb = lambda n, s, d=F32: ctx.enter_context(nc.sbuf_tensor(n, s, d))
        sem = lambda n: ctx.enter_context(nc.semaphore(n))
        W1, W2 = sb("m_W1", [P, E8, HID1]), sb("m_W2", [P, E8, 2, D])
        T, LG = choice_tiles(sb, "m"), sb("m_LG", [P, NT_TILES, E8])
        ACC = [sb(f"m_ACC{i}", [P, NT_TILES, D]) for i in range(2)]
        BO, BT = sb("m_BO", [P, NT_TILES, D]), sb("m_BT", [P, TOK])
        HT = [sb(f"m_HT{i}", [P, 2, GW]) for i in range(2)]
        loaded = [sem(f"m_loaded{e}") for e in range(E8)]
        lg_made, exp_wanted, exp_done = sem("m_lg_made"), sem("m_exp_wanted"), sem("m_exp_done")
        with nc.Block() as block:
            @block.sync
            def _(sp):
                load_experts(c, sp, W1, W2, w1_dram, w2_dram, loaded)

            @block.tensor
            def _(pe):
                for t in range(NT_TILES):
                    last = nc.tensor.matmul(PS[0][:, E8 * t:E8 * t + E8], NTI[:, P * t:P * t + P], w("gw"),
                                            start=True, stop=True)
                last.then_inc(lg_made, 1)

            @block.scalar
            def _(act):
                act.wait_ge(exp_wanted, 1)
                nc.scalar.activation(T.PB[:, :, :], T.A[:, :, :], ACT.Exp).then_inc(exp_done, 1)

            @block.vector
            def _(v):
                v.wait_ge(lg_made, 1)
                dve.link(v, nc.vector.tensor_tensor(LG[:, :, :],
                                                    PS[0][:, 0:NT_TILES * E8].rearrange("p (t e) -> p t e", e=E8),
                                                    rep(w("gb"), NT_TILES), ALU.add))
                softmax_top2(c, v, LG, T, (exp_wanted, exp_done))

        start_outputs(c, "m0", T.OH1, ACC[0], c.W2S[:, 0:D])
        expert_round(c, "m0", NTI, W1, W2, loaded, T.OH1, ACC[0], HT)
        start_outputs(c, "m1", T.OH2, ACC[1], c.W2S[:, 0:D], (BT, BO, ACC[0]))
        expert_round(c, "m1", BT, W1, W2, loaded, T.OH2, ACC[1], HT)

        base, nv0 = c.n_front, c.n_var
        with nc.Block() as block:
            @block.tensor
            def _(pe):
                for g in range(G):
                    transpose_xs(c, pe, base + g, PS[7])

            @block.scalar
            def _(act):
                for g in range(G):
                    copy_nt(c, act, base + g, g, c.NT[0], PS[7])

            @block.gpsimd
            def _(pool):
                for g in range(G):
                    rstds(c, pool, nv0 + 3 * g, 3)
                    keep_xn(c, pool, base + g, g)

            @block.vector
            def _(v):
                Y = BO
                for g in range(G):
                    gs = slice(GT * g, GT * g + GT)
                    for r, (m, src) in enumerate(((T.M1, c.XN), (T.M2, Y))):
                        for t in range(GT * g, GT * g + GT):
                            last = nc.vector.scalar_tensor_tensor(Y[:, t, :], ACC[r][:, t, :], m[:, t:t + 1],
                                                                  src[:, t, :], ALU.mult, ALU.add)
                        dve.link(v, last)
                    tiles = [Y[:, t, :] for t in range(GT * g, GT * g + GT)]
                    statistics(c, v, tiles, 1e-5)
                    dve.link(v, normalise(c, v, tiles, tiles))
                    dve.link(v, nc.vector.tensor_tensor(Y[:, gs, :], Y[:, gs, :], rep(w("lng"), GT), ALU.mult))
                    dve.link(v, nc.vector.tensor_tensor(Y[:, gs, :], Y[:, gs, :], rep(w("lnb"), GT), ALU.add))
                    tail(c, v, g, Y[:, gs, :])


def expert_round(c, tag, IN, W1, W2, loaded, OH, ACC, HT):
    nc, w, PS = c.nc, c.w, c.PS
    n = E8 * G
    with ExitStack() as ctx:
        sem = lambda s: ctx.enter_context(nc.semaphore(tag + s))
        h_made, h_ready, y_made, y_read = sem("_h_made"), sem("_h_ready"), sem("_y_made"), sem("_y_read")
        with nc.Block() as block:
            @block.tensor
            def _(pe):
                for i in range(n + 1):
                    if i < n:
                        e, g = divmod(i, G)
                        if g == 0:
                            pe.wait_ge(loaded[e], 32)
                        if i >= 2:
                            pe.wait_ge(h_ready, 2 * (i - 1))
                        for k in range(2):
                            nc.tensor.matmul(PS[2 * (i % 2) + k][:, :], W1[:, e, P * k:P * k + P],
                                             IN[:, GW * g:GW * g + GW], start=True, stop=True).then_inc(h_made, 1)
                    if i:
                        e = (i - 1) // G
                        pe.wait_ge(h_ready, 2 * i)
                        if i >= 3:
                            pe.wait_ge(y_read, i - 2)
                        for j in range(GT):
                            for k in range(2):
                                last = nc.tensor.matmul(PS[4 + (i - 1) % 2][:, P * j:P * j + P],
                                                        HT[(i - 1) % 2][:, k, P * j:P * j + P], W2[:, e, k, :],
                                                        start=(k == 0), stop=(k == 1))
                        last.then_inc(y_made, 1)

            @block.scalar
            def _(act):
                for i in range(n):
                    e = i // G
                    if i >= 2:
                        act.wait_ge(y_made, i - 1)
                    for k in range(2):
                        act.wait_ge(h_made, 2 * i + k + 1)
                        nc.scalar.activation(HT[i % 2][:, k, :], PS[2 * (i % 2) + k][:, :], ACT.Relu,
                                             bias=w("b1m", 2 * e + k, 1)).then_inc(h_ready, 1)

            @block.vector
            def _(v):
                for i in range(n):
                    e, g = divmod(i, G)
                    v.wait_ge(y_made, i + 1)
                    if i:
                        v.wait_ge(y_read, i)
                    for j in range(GT):
                        t = GT * g + j
                        last = nc.vector.scalar_tensor_tensor(ACC[:, t, :], PS[4 + i % 2][:, P * j:P * j + P],
                                                              OH[:, t, e:e + 1], ACC[:, t, :], ALU.mult, ALU.add)
                    last.then_inc(y_read, 1)


def l2_attn(c):
    nc, w, PS = c.nc, c.w, c.PS
    dve = c.dve
    NTI = c.NT[0]
    FMAX = float(np.finfo(np.float32).max)
    with ExitStack() as ctx:
        sb = lambda n, s, d=F32: ctx.enter_context(nc.sbuf_tensor(n, s, d))
        sem = lambda n: ctx.enter_context(nc.semaphore(n))
        OT = sb("r_OT", [P, TOK])
        with ExitStack() as ctx1:
            sb1 = lambda n, s, d=F32: ctx1.enter_context(nc.sbuf_tensor(n, s, d))
            sem1 = lambda n: ctx1.enter_context(nc.semaphore("r_" + n))
            NP = sb1("r_NP", [P, B, S + 1])
            WM = sb1("r_WM", [P, 3, 2, D])
            OM = sb1("r_OM", [P, 3])
            LA, EU, EW = sb1("r_LA", [P, 1]), sb1("r_EU", [P, 1]), sb1("r_EW", [P, 1])
            AP, RN = sb1("r_AP", [P, S]), sb1("r_RN", [P, S])
            ONE = sb1("r_ONE", [P, S])
            EK, EKV, SK, RR = (sb1("r_" + n, [P, TOK]) for n in ("EK", "EKV", "SK", "RR"))
            F_, CSUM = sb1("r_F", [P, S]), sb1("r_CS", [P, S + 1])
            ST, STN, MK, DEN = sb1("r_ST", [P, S]), sb1("r_STN", [P, S]), sb1("r_MK", [P, S], U32), sb1("r_DEN", [P, S])
            (np_ready, wm_ready, kvr_made, ek_ready, ekv_ready, er_ready, sk_made, sk_ready, td_ready, la_ready, ap_ready,
             const_ready) = (sem1(n) for n in (
                 "np_ready", "wm_ready", "kvr_made", "ek_ready", "ekv_ready", "er_ready", "sk_made", "sk_ready",
                 "td_ready", "la_ready", "ap_ready", "const_ready"))
            with nc.Block() as block:
                @block.tensor
                def _(pe):
                    mm = nc.tensor.matmul
                    pe.wait_ge(np_ready, 1)
                    pe.wait_ge(wm_ready, 1)
                    for g in range(G + 1):
                        if g < G:
                            b, at = g // 2, GW * (g % 2)
                            if g:
                                pe.wait_ge(ek_ready, g)
                                pe.wait_ge(ekv_ready, g)
                                pe.wait_ge(er_ready, g)
                            for k in range(3):
                                mm(PS[k][:, :], WM[:, k, 0, :], NP[:, b, 1 + at:1 + at + GW], start=True, stop=False)
                                mm(PS[k][:, :], WM[:, k, 1, :], NP[:, b, at:at + GW], start=False, stop=True)\
                                    .then_inc(kvr_made, 1)
                        if g:
                            q = g - 1
                            pe.wait_ge(ek_ready, q + 1)
                            if q >= 2:
                                pe.wait_ge(sk_ready, q - 1)
                            mm(PS[3 + q % 2][:, :], w("blocks"), EK[:, GW * q:GW * q + GW], start=True, stop=True)\
                                .then_inc(sk_made, 1)

                @block.scalar
                def _(act):
                    av = nc.scalar.activation
                    av(LA[:, :], w("td"), ACT.Exp)
                    av(EU[:, :], w("tf"), ACT.Exp).then_inc(td_ready, 1)
                    act.wait_ge(la_ready, 1)
                    av(EW[:, :], LA[:, :], ACT.Exp)
                    av(AP[:, :], w("time"), ACT.Exp, scale=LA[:, 0:1]).then_inc(ap_ready, 1)
                    for g in range(G):
                        gs = slice(GW * g, GW * g + GW)
                        act.wait_ge(kvr_made, 3 * g + 1)
                        av(EK[:, gs], PS[0][:, :], ACT.Exp).then_inc(ek_ready, 1)
                        act.wait_ge(kvr_made, 3 * g + 3)
                        av(RR[:, gs], PS[2][:, :], ACT.Exp, scale=-1.0).then_inc(er_ready, 1)
                        act.wait_ge(sk_made, g + 1)
                        av(SK[:, gs], PS[3 + g % 2][:, :], ACT.Copy).then_inc(sk_ready, 1)

                @block.gpsimd
                def _(pool):
                    nc.gpsimd.memset(ONE[:, :], 1.0)
                    nc.gpsimd.memset(CSUM[:, 0:1], 0.0).then_inc(const_ready, 1)
                    nc.gpsimd.memset(NP[:, :, 0:1], 0.0)
                    for b in range(B):
                        last = nc.gpsimd.tensor_copy(NP[:, b, 1:1 + S], NTI[:, S * b:S * b + S])
                    last.then_inc(np_ready, 1)

                @block.vector
                def _(v):
                    tt, ts, stt = nc.vector.tensor_tensor, nc.vector.tensor_scalar, nc.vector.scalar_tensor_tensor
                    dve.link(v, ts(OM[:, :], w("mk", 0, 3), -1.0, 1.0, ALU.mult, ALU.add))
                    for k, (m, wn) in enumerate((("mk", "wkey"), ("mv", "wval"), ("mr", "wrec"))):
                        ts(WM[:, k, 0, :], w(wn), w(m), None, ALU.mult)
                        last = ts(WM[:, k, 1, :], w(wn), OM[:, k:k + 1], None, ALU.mult)
                    last.then_inc(wm_ready, 1)
                    v.wait_ge(td_ready, 1)
                    ts(LA[:, :], LA[:, :], -1.0, None, ALU.mult).then_inc(la_ready, 1)
                    v.wait_ge(ap_ready, 1)
                    dve.link(v, ts(RN[:, :], AP[:, :], EW[:, 0:1], None, ALU.mult))
                    dve.link(v, nc.vector.reciprocal(RN[:, :], RN[:, :]))
                    for g in range(G):
                        gs = slice(GW * g, GW * g + GW)
                        v.wait_ge(kvr_made, 3 * g + 2)
                        v.wait_ge(ek_ready, g + 1)
                        tt(EKV[:, gs], PS[1][:, :], EK[:, gs], ALU.mult).then_inc(ekv_ready, 1)
                    v.wait_ge(ekv_ready, G)
                    v.wait_ge(er_ready, G)
                    v.wait_ge(sk_ready, G)
                    v.wait_ge(const_ready, 1)
                    for b in range(B):
                        bs = slice(S * b, S * b + S)
                        for src, state in ((EKV, "a"), (SK, "b")):
                            dve.link(v, tt(F_[:, :], src[:, bs], RN[:, :], ALU.mult))
                            dve.link(v, nc.vector.tensor_tensor_scan(CSUM[:, 1:1 + S], ONE[:, :], F_[:, :], 0.0,
                                                                     ALU.mult, ALU.add))
                            dve.link(v, tt(ST[:, :], AP[:, :], CSUM[:, 0:S], ALU.mult))
                            ts(MK[:, :], ST[:, :], FMAX, None, ALU.is_le)
                            ts(F_[:, :], ST[:, :], -FMAX, None, ALU.max)
                            dve.link(v, nc.vector.memset(STN[:, :], 0.0))
                            dve.link(v, nc.vector.copy_predicated(STN[:, :], MK[:, :], F_[:, :]))
                            if state == "a":
                                dve.link(v, stt(EKV[:, bs], EKV[:, bs], EU[:, 0:1], STN[:, :], ALU.mult, ALU.add))
                            else:
                                dve.link(v, stt(DEN[:, :], SK[:, bs], EU[:, 0:1], STN[:, :], ALU.mult, ALU.add))
                        dve.link(v, ts(DEN[:, :], DEN[:, :], 1e-6, None, ALU.max))
                        dve.link(v, ts(RR[:, bs], RR[:, bs], 1.0, None, ALU.add))
                        dve.link(v, nc.vector.reciprocal(DEN[:, :], DEN[:, :]))
                        dve.link(v, nc.vector.reciprocal(RR[:, bs], RR[:, bs]))
                        dve.link(v, tt(EKV[:, bs], EKV[:, bs], DEN[:, :], ALU.mult))
                        dve.link(v, tt(OT[:, bs], EKV[:, bs], RR[:, bs], ALU.mult))

        def products(pe, g, bank):
            for j in range(GT):
                t = GT * g + j
                last = nc.tensor.matmul(bank[:, P * j:P * j + P], OT[:, P * t:P * t + P], w("wo2"),
                                        start=True, stop=True)
            return last
        project_tail(c, "r1", products, None, c.NT[1])


def l2_ffn(c):
    nc, w, PS = c.nc, c.w, c.PS
    NTI = c.NT[1]
    KC = HID2 // P
    with ExitStack() as ctx:
        HT = ctx.enter_context(nc.sbuf_tensor("g_HT", [P, KC, TOK], F32))
        h_made, h_ready = ctx.enter_context(nc.semaphore("g_h_made")), ctx.enter_context(nc.semaphore("g_h_ready"))
        with nc.Block() as block:
            @block.tensor
            def _(pe):
                for i in range(G * KC):
                    g, k = divmod(i, KC)
                    if i >= 4:
                        pe.wait_ge(h_ready, i - 3)
                    nc.tensor.matmul(PS[i % 4][:, :], w("w1f", P * k, P), NTI[:, GW * g:GW * g + GW],
                                     start=True, stop=True).then_inc(h_made, 1)

            @block.scalar
            def _(act):
                for i in range(G * KC):
                    g, k = divmod(i, KC)
                    act.wait_ge(h_made, i + 1)
                    nc.scalar.activation(HT[:, k, GW * g:GW * g + GW], PS[i % 4][:, :], ACT.Relu,
                                         bias=w("b1f", k, 1)).then_inc(h_ready, 1)

        def products(pe, g, bank):
            for j in range(GT):
                t = GT * g + j
                for k in range(KC):
                    last = nc.tensor.matmul(bank[:, P * j:P * j + P], HT[:, k, P * t:P * t + P], w("w2f", D * k, D),
                                            start=(k == 0), stop=(k == KC - 1))
            return last
        project_tail(c, "g1", products, "b2f", c.NT[0])


def l3_attn(c):
    nc, w, PS = c.nc, c.w, c.PS
    dve = c.dve
    NH, HD = NH3, HD3
    M = D // HD
    R = S // M
    NTM = c.NT[0][:, :].rearrange("c (b r m) -> c m b r", b=B, m=M)
    OT = c.NT[0]
    with ExitStack() as ctx:
        sb = lambda n_, s, d=F32: ctx.enter_context(nc.sbuf_tensor("h_" + n_, s, d))
        sem = lambda n_: ctx.enter_context(nc.semaphore("h_" + n_))
        two = lambda n_, s: [sb(f"{n_}{i}", s) for i in range(2)]
        OUT = sb("OUT", [P, NH, M, HD])
        QKV, PR = two("QKV", [P, 3, NH, HD]), two("PR", [P, NH, NH, HD])
        SCR, E, PV = two("SCR", [P, NH, NH]), two("E", [P, NH, NH]), sb("PV", [P, NH, HD, NH])
        MX, SM = sb("MX", [P, NH]), sb("SM", [P, NH])
        (made, copied, prod_ready, prod_read, scr_ready, e_ready, e_read, done, turned, ot_copied) = (
            sem(n_) for n_ in ("made", "copied", "prod_ready", "prod_read", "scr_ready", "e_ready", "e_read", "done",
                               "turned", "ot_copied"))
        over = lambda a: a.unsqueeze(2).to_broadcast([P, NH, NH])
        with nc.Block() as block:
            @block.tensor
            def _(pe):
                for m in range(M):
                    if m >= 2:
                        pe.wait_ge(copied, m - 1)
                    nc.tensor.matmul(PS[m % 2][:, 0:3 * D], NTM[:, m, :, :], w("wq3", 0, 3 * D),
                                     start=True, stop=True).then_inc(made, 1)
                pe.wait_ge(done, M)
                for h in range(NH):
                    if h >= 4:
                        pe.wait_ge(ot_copied, h - 3)
                    nc.tensor.transpose(PS[2 + h % 4][:, 0:P], OUT[:, h, :, :].rearrange("p m d -> p (m d)"), w("ident"))\
                        .then_inc(turned, 1)

            @block.scalar
            def _(act):
                for m in range(M + 1):
                    if m < M:
                        act.wait_ge(made, m + 1)
                        if m >= 2:
                            act.wait_ge(prod_ready, m - 1)
                            act.wait_ge(done, m - 1)
                        nc.scalar.activation(QKV[m % 2][:, :, :, :].rearrange("p k h d -> p (k h d)"),
                                             PS[m % 2][:, 0:3 * D], ACT.Copy).then_inc(copied, 1)
                    if m:
                        q = m - 1
                        act.wait_ge(scr_ready, q + 1)
                        if q >= 2:
                            act.wait_ge(e_read, q - 1)
                        nc.scalar.activation(E[q % 2][:, :, :], SCR[q % 2][:, :, :], ACT.Exp, scale=HD ** -0.5)\
                            .then_inc(e_ready, 1)
                for h in range(NH):
                    act.wait_ge(turned, h + 1)
                    nc.scalar.activation(OT[:, :].rearrange("c (b x) -> c b x", b=B)[:, :, R * h:R * h + R],
                                         PS[2 + h % 4][:, 0:P].rearrange("c (b r) -> c b r", b=B), ACT.Copy)\
                        .then_inc(ot_copied, 1)

            @block.gpsimd
            def _(pool):
                for m in range(M):
                    s = m % 2
                    pool.wait_ge(copied, m + 1)
                    if m >= 2:
                        pool.wait_ge(prod_read, m - 1)
                    nc.gpsimd.tensor_tensor(PR[s][:, :, :, :],
                                            QKV[s][:, 0, :, :].unsqueeze(2).to_broadcast([P, NH, NH, HD]),
                                            QKV[s][:, 1, :, :].unsqueeze(1).to_broadcast([P, NH, NH, HD]), ALU.mult)\
                        .then_inc(prod_ready, 1)

            @block.vector
            def _(v):
                tt = nc.vector.tensor_tensor
                for m in range(M + 1):
                    if m < M:
                        s = m % 2
                        v.wait_ge(prod_ready, m + 1)
                        if m >= 2:
                            v.wait_ge(e_ready, m - 1)
                        nc.vector.reduce_sum(SCR[s][:, :, :], PR[s][:, :, :, :], axis=AX.X).then_inc(prod_read, 1)
                        v.wait_ge(prod_read, m + 1)
                        dve.link(v, nc.vector.reduce_max(MX[:, :], SCR[s][:, :, :], axis=AX.X))
                        tt(SCR[s][:, :, :], SCR[s][:, :, :], over(MX[:, :]), ALU.subtract).then_inc(scr_ready, 1)
                    if m:
                        q, s = m - 1, (m - 1) % 2
                        v.wait_ge(e_ready, q + 1)
                        if q:
                            v.wait_ge(done, q)
                        dve.link(v, nc.vector.reduce_sum(SM[:, :], E[s][:, :, :], axis=AX.X))
                        dve.link(v, tt(PV[:, :, :, :], E[s][:, :, :].unsqueeze(2).to_broadcast([P, NH, HD, NH]),
                                       QKV[s][:, 2, :, :].rearrange("p k d -> p d k").unsqueeze(1)
                                       .to_broadcast([P, NH, HD, NH]), ALU.mult))
                        nc.vector.reduce_sum(OUT[:, :, q, :], PV[:, :, :, :], axis=AX.X).then_inc(e_read, 1)
                        dve.link(v, nc.vector.reciprocal(SM[:, :], SM[:, :]))
                        v.wait_ge(e_read, q + 1)
                        tt(OUT[:, :, q, :], OUT[:, :, q, :], SM[:, :].unsqueeze(2).to_broadcast([P, NH, HD]),
                           ALU.mult).then_inc(done, 1)

        def products(pe, g, bank):
            for j in range(GT):
                t = GT * g + j
                last = nc.tensor.matmul(bank[:, P * j:P * j + P], OT[:, P * t:P * t + P], w("wo3"),
                                        start=True, stop=True)
            return last
        project_tail(c, "h1", products, "bo3", c.NT[1])


def l3_ffn(c, w1_dram, w2_dram):
    nc, w, PS = c.nc, c.w, c.PS
    dve = c.dve
    NTI = c.NT[1]
    KC = F3 // P
    n = E8 * G
    with ExitStack() as ctx:
        sb = lambda n_, s, d=F32: ctx.enter_context(nc.sbuf_tensor(n_, s, d))
        sem = lambda n_: ctx.enter_context(nc.semaphore("x_" + n_))
        W1, W2 = sb("x_W1", [P, 2, 2 * F3]), sb("x_W2", [P, 2, KC * D])
        WU = [sb(f"x_WU{i}", [P, 2, 2 * F3], F32R) for i in range(2)]
        WD = [sb(f"x_WD{i}", [P, 2, KC * D], F32R) for i in range(2)]
        NS = sb("x_NS", [P, 2, TOK], F32R)
        T, LG = choice_tiles(sb, "x"), sb("x_LG", [P, NT_TILES, E8])
        HR, HRT = sb("x_HR", [P, NT_TILES, KR]), c.NT[0][0:KR, :]
        ACC = c.XN[:, :, :].rearrange("p t d -> p (t d)")
        MROWS = 64 + E8
        MT, SEL, SELF = sb("x_MT", [MROWS, TOK], BF16), sb("x_SEL", [MROWS, E8, P], BF16), sb("x_SELF", [MROWS, E8])
        MB = [sb(f"x_MB{i}", [P, GW]) for i in range(2)]
        Z = [sb(f"x_Z{i}", [P, GW]) for i in range(2)]
        RST, RMV, RV, RRS = (sb("x_RST", [P, NT_TILES, 6]), sb("x_RMV", [P, NT_TILES, 2]),
                             sb("x_RV", [P, NT_TILES]), sb("x_RRS", [P, NT_TILES]))
        GE = [sb(f"x_GE{i}", [P, GW]) for i in range(4)]
        GF = [sb(f"x_GF{i}", [P, GW]) for i in range(4)]
        GS = [sb(f"x_GS{i}", [P, 2, KC, GW], F32R) for i in range(2)]
        loaded = [sem(f"loaded{e}") for e in range(E8)]
        w_high, w_low, n_high, n_low = sem("w_high"), sem("w_low"), sem("n_high"), sem("n_low")

        def load(sp, e):
            sp.dma_start(W1[:, e % 2, :], w1_dram[e]).then_inc(loaded[e], 16)
            sp.dma_start(W2[:, e % 2, :], w2_dram[e].rearrange("p k d -> p (k d)")).then_inc(loaded[e], 16)

        def weights_high(act, e):
            act.wait_ge(loaded[e], 32)
            for raw, part in ((W1, WU), (W2, WD)):
                nc.scalar.activation(part[e % 2][:, 0, :], raw[:, e % 2, :], ACT.Copy).then_inc(w_high, 1)

        def weights_low(eng, tensor_tensor, e):
            for k, (raw, part) in enumerate(((W1, WU), (W2, WD))):
                eng.wait_ge(w_high, 2 * e + k + 1)
                tensor_tensor(part[e % 2][:, 1, :], raw[:, e % 2, :], part[e % 2][:, 0, :].bitcast(F32),
                                        ALU.subtract).then_inc(w_low, 1)
        (r_made, rv_ready, rr_ready, hr_ready, gelu_ready, r_turned, r_copied, lg_made, exp_wanted, exp_done) = (
            sem(n_) for n_ in ("r_made", "rv_ready", "rr_ready", "hr_ready", "gelu_ready", "r_turned", "r_copied",
                               "lg_made", "exp_wanted", "exp_done"))
        with nc.Block() as block:
            @block.sync
            def _(sp):
                for e in range(2):
                    load(sp, e)

            @block.tensor
            def _(pe):
                for t in range(NT_TILES):
                    last = nc.tensor.matmul(PS[t // 8][:, KR * (t % 8):KR * (t % 8) + KR], NTI[:, P * t:P * t + P],
                                            w("wr1"), start=True, stop=True)
                last.then_inc(r_made, 1)
                pe.wait_ge(gelu_ready, 1)
                for g in range(G):
                    for j in range(GT):
                        last = nc.tensor.transpose(PS[2 + g][0:KR, P * j:P * j + P], HR[:, GT * g + j, :], w("ident"))
                    last.then_inc(r_turned, 1)
                pe.wait_ge(r_copied, G)
                for t in range(NT_TILES):
                    last = nc.tensor.matmul(PS[6][:, E8 * t:E8 * t + E8], HRT[:, P * t:P * t + P], w("wr2", rows=KR),
                                            start=True, stop=True)
                last.then_inc(lg_made, 1)

            @block.scalar
            def _(act):
                for g in range(G):
                    nc.scalar.activation(NS[:, 0, GW * g:GW * g + GW], NTI[:, GW * g:GW * g + GW], ACT.Copy)\
                        .then_inc(n_high, 1)
                act.wait_ge(hr_ready, 1)
                nc.scalar.activation(HR[:, :, :], HR[:, :, :], ACT.Gelu_apprx_tanh).then_inc(gelu_ready, 1)
                for g in range(G):
                    act.wait_ge(r_turned, g + 1)
                    nc.scalar.activation(HRT[:, GW * g:GW * g + GW], PS[2 + g][0:KR, :], ACT.Copy).then_inc(r_copied, 1)
                for e in range(2):
                    weights_high(act, e)
                act.wait_ge(exp_wanted, 1)
                nc.scalar.activation(T.PB[:, :, :], T.A[:, :, :], ACT.Exp).then_inc(exp_done, 1)

            @block.gpsimd
            def _(pool):
                pool.wait_ge(rv_ready, 1)
                nc.gpsimd.tensor_tensor(RRS[:, :], RV[:, :], c.MHALF[:, 0:NT_TILES], ALU.pow).then_inc(rr_ready, 1)
                for g in range(G):
                    gs = slice(GW * g, GW * g + GW)
                    pool.wait_ge(n_high, g + 1)
                    nc.gpsimd.tensor_tensor(NS[:, 1, gs], NTI[:, gs], NS[:, 0, gs].bitcast(F32), ALU.subtract)\
                        .then_inc(n_low, 1)
                for e in range(2):
                    weights_low(pool, nc.gpsimd.tensor_tensor, e)

            @block.vector
            def _(v):
                tt, ts = nc.vector.tensor_tensor, nc.vector.tensor_scalar
                v.wait_ge(r_made, 1)
                for k in range(2):
                    last = tt(HR[:, 8 * k:8 * k + 8, :], PS[k][:, :].rearrange("p (t r) -> p t r", r=KR),
                              rep(w("br1"), 8), ALU.add)
                dve.link(v, last)
                for t in range(NT_TILES):
                    last = nc.vector.bn_stats(RST[:, t, :], HR[:, t, :])
                dve.link(v, last)
                for t in range(NT_TILES):
                    last = nc.vector.bn_aggr(RMV[:, t, :], RST[:, t, :])
                dve.link(v, last)
                ts(RV[:, :], RMV[:, :, 1], 1e-6, None, ALU.add).then_inc(rv_ready, 1)
                v.wait_ge(rr_ready, 1)
                for t in range(NT_TILES):
                    last = ts(HR[:, t, :], HR[:, t, :], RMV[:, t, 0:1], RRS[:, t:t + 1], ALU.subtract, ALU.mult)
                dve.link(v, last)
                dve.link(v, tt(HR[:, :, :], HR[:, :, :], rep(w("lns"), NT_TILES), ALU.mult))
                tt(HR[:, :, :], HR[:, :, :], rep(w("lnbi"), NT_TILES), ALU.add).then_inc(hr_ready, 1)
                expert_masks(c, v, SEL, SELF, MROWS)
                v.wait_ge(lg_made, 1)
                dve.link(v, tt(LG[:, :, :], PS[6][:, 0:NT_TILES * E8].rearrange("p (t e) -> p t e", e=E8),
                               rep(w("br2"), NT_TILES), ALU.add))
                softmax_top2(c, v, LG, T, (exp_wanted, exp_done))
                bc = lambda a: a[:, :].unsqueeze(2).to_broadcast([P, NT_TILES, E8])
                dve.link(v, tt(T.MX[:, :], T.M1[:, :], T.M2[:, :], ALU.add))
                dve.link(v, nc.vector.reciprocal(T.MX[:, :], T.MX[:, :]))
                tt(T.OH1[:, :, :], T.OH1[:, :, :], bc(T.M1), ALU.mult)
                dve.link(v, tt(T.OH2[:, :, :], T.OH2[:, :, :], bc(T.M2), ALU.mult))
                dve.link(v, tt(LG[:, :, :], T.OH1[:, :, :], T.OH2[:, :, :], ALU.add))
                dve.link(v, tt(LG[:, :, :], LG[:, :, :], bc(T.MX), ALU.mult))

        start_sums(c, "x", LG, ACC, c.W2S[:, D:2 * D], MT,
                   [sem(n_) for n_ in ("oh_turned", "oh_copied", "b_made", "b_copied")], True)
        x_made, ge_ready, g_ready, gh_ready, gl_ready, y_made, z_ready, mb_made, mb_ready, summed = (
            sem(n_) for n_ in ("x_made", "ge_ready", "g_ready", "gh_ready", "gl_ready", "y_made", "z_ready", "mb_made",
                               "mb_ready", "summed"))
        HL = ((0, 0), (0, 1), (1, 0))
        XB = (0, 2, 6)
        with nc.Block() as block:
            @block.sync
            def _(sp):
                for e in range(2, E8):
                    sp.wait_ge(w_low, 2 * (e - 1))
                    load(sp, e)

            @block.tensor
            def _(pe):
                for i in range(n + 1):
                    if i < n:
                        e, g = divmod(i, G)
                        if g == 0:
                            pe.wait_ge(w_low, 2 * (e + 1))
                        if i:
                            pe.wait_ge(mb_ready, i)
                        nc.tensor.matmul(PS[5][:, :], SEL[:, e, :], MT[:, GW * g:GW * g + GW],
                                         start=True, stop=True).then_inc(mb_made, 1)
                        for k in range(KC):
                            q = KC * i + k
                            if q >= 3:
                                pe.wait_ge(g_ready, q - 2)
                            for half in range(2):
                                for a, b in HL:
                                    last = nc.tensor.matmul(PS[XB[q % 3] + half][:, :],
                                                            WU[e % 2][:, a, F3 * half + P * k:F3 * half + P * k + P],
                                                            NS[:, b, GW * g:GW * g + GW],
                                                            start=((a, b) == HL[0]), stop=((a, b) == HL[-1]))
                            last.then_inc(x_made, 1)
                    if i:
                        e = (i - 1) // G
                        pe.wait_ge(gh_ready, KC * i)
                        pe.wait_ge(gl_ready, KC * i)
                        if i >= 2:
                            pe.wait_ge(z_ready, i - 1)
                        for k in range(KC):
                            for a, b in HL:
                                last = nc.tensor.matmul(PS[4][:, :], WD[e % 2][:, b, D * k:D * k + D],
                                                        GS[(i - 1) % 2][:, a, k, :],
                                                        start=(k == 0 and (a, b) == HL[0]),
                                                        stop=(k == KC - 1 and (a, b) == HL[-1]))
                        last.then_inc(y_made, 1)

            @block.scalar
            def _(act):
                for q in range(KC * n + 1):
                    if q < KC * n and q % KC == 0:
                        i = q // KC
                        act.wait_ge(mb_made, i + 1)
                        if i >= 2:
                            act.wait_ge(z_ready, i - 1)
                        nc.scalar.activation(MB[i % 2][:, :], PS[5][:, :], ACT.Copy).then_inc(mb_ready, 1)
                    if q < KC * n:
                        e, k = q // (KC * G), q % KC
                        act.wait_ge(x_made, q + 1)
                        if q >= 4:
                            act.wait_ge(g_ready, q - 3)
                        nc.scalar.activation(GE[q % 4][:, :], PS[XB[q % 3] + 1][:, :], ACT.Gelu_apprx_tanh,
                                             bias=w("b1g", 8 * e + KC + k, 1)).then_inc(ge_ready, 1)
                    if q:
                        p = q - 1
                        i, k = divmod(p, KC)
                        act.wait_ge(g_ready, q)
                        if i >= 2 and k == 0:
                            act.wait_ge(y_made, i - 1)
                        nc.scalar.activation(GS[i % 2][:, 0, k, :], GF[p % 4][:, :], ACT.Copy).then_inc(gh_ready, 1)
                    if q % (KC * G) == 2 * KC and 2 <= q // (KC * G) + 1 < E8:
                        e = q // (KC * G) + 1
                        act.wait_ge(y_made, G * (e - 1))
                        weights_high(act, e)

            @block.gpsimd
            def _(pool):
                def add(i):
                    gs = slice(GW * (i % G), GW * (i % G) + GW)
                    pool.wait_ge(z_ready, i + 1)
                    if i >= G:
                        pool.wait_ge(summed, i - G + 1)
                    nc.gpsimd.tensor_tensor(ACC[:, gs], ACC[:, gs], Z[i % 2][:, :], ALU.add).then_inc(summed, 1)

                for p in range(KC * n):
                    i, k = divmod(p, KC)
                    if i >= 2 and k == 2:
                        add(i - 2)
                    pool.wait_ge(gh_ready, p + 1)
                    nc.gpsimd.tensor_tensor(GS[i % 2][:, 1, k, :], GF[p % 4][:, :], GS[i % 2][:, 0, k, :].bitcast(F32),
                                            ALU.subtract).then_inc(gl_ready, 1)
                add(n - 2)
                add(n - 1)

            @block.vector
            def _(v):
                for i in range(n + 1):
                    if i < n:
                        e = i // G
                        for k in range(KC):
                            q = KC * i + k
                            v.wait_ge(ge_ready, q + 1)
                            if q >= 4:
                                v.wait_ge(gh_ready, q - 3)
                                v.wait_ge(gl_ready, q - 3)
                            nc.vector.scalar_tensor_tensor(GF[q % 4][:, :], PS[XB[q % 3]][:, :],
                                                           w("b1g", 8 * e + k, 1), GE[q % 4][:, :],
                                                           ALU.add, ALU.mult).then_inc(g_ready, 1)
                    if i:
                        v.wait_ge(y_made, i)
                        v.wait_ge(mb_ready, i)
                        if i >= 3:
                            v.wait_ge(summed, i - 2)
                        nc.vector.tensor_tensor(Z[(i - 1) % 2][:, :], PS[4][:, :], MB[(i - 1) % 2][:, :], ALU.mult)\
                            .then_inc(z_ready, 1)
                    if i % G == 2 and 2 <= i // G + 1 < E8:
                        weights_low(v, nc.vector.tensor_tensor, i // G + 1)

        nv0 = c.n_var
        acc_turned, acc_copied, x_final = sem("acc_turned"), sem("acc_copied"), sem("x_final")
        YF = W1[:, :, :].rearrange("p a (t d) -> p (a t) d", d=D)
        with nc.Block() as block:
            @block.sync
            def _(sp):
                for g in range(G):
                    sp.wait_ge(x_final, g + 1)
                    sp.dma_start(c.out[GT * g:GT * g + GT].rearrange("t p d -> p t d"),
                                 c.X[:, GT * g:GT * g + GT, :]).then_inc(c.out_stored, 16)
                sp.wait_ge(c.out_stored, 16 * G)

            @block.tensor
            def _(pe):
                for g in range(G):
                    for j in range(GT):
                        t = GT * g + j
                        last = nc.tensor.transpose(PS[g][:, P * j:P * j + P], ACC[:, P * t:P * t + P], w("ident"))
                    last.then_inc(acc_turned, 1)

            @block.scalar
            def _(act):
                for g in range(G):
                    act.wait_ge(acc_turned, g + 1)
                    nc.scalar.activation(YF[:, GT * g:GT * g + GT, :],
                                         PS[g][:, :].rearrange("p (t d) -> p t d", d=D), ACT.Copy)\
                        .then_inc(acc_copied, 1)

            @block.gpsimd
            def _(pool):
                rstds(c, pool, nv0, G)

            @block.vector
            def _(v):
                for g in range(G):
                    v.wait_ge(acc_copied, g + 1)
                    residual(c, v, g, YF[:, GT * g:GT * g + GT, :])
                    v.sem_inc(x_final, 1)


def kernel(**inputs):
    import numpy as np
    import concourse.bacc as bacc
    from concourse.bass_utils import run_bass_kernel_spmd as run

    nc = bacc.Bacc("TRN2", target_bir_lowering=False, num_devices=1)
    arrays = host_layout(inputs)
    args = {}
    for name, a in arrays.items():
        args[name] = nc.dram_tensor(f"in_{name}", a.shape, mybir.dt.from_np(a.dtype), kind="ExternalInput").ap()
    out = nc.dram_tensor("out", (NT_TILES, P, D), F32, kind="ExternalOutput").ap()
    program(nc, args["x"], args["pack"], args["b2s"], args["l1w1"], args["l1w2"], args["l3w1"], args["l3w2"],
            out)
    r = run(nc, [{f"in_{k}": a for k, a in arrays.items()}], core_ids=[0])
    return r.results[0]["out"].reshape(B, S, D)


def host_layout(i):
    f = np.float32
    i = {k: np.asarray(a) for k, a in i.items()}
    rows = lambda a: np.broadcast_to(a.reshape(1, -1), (P, a.size))
    ar = np.arange(P)
    angle = 2 * np.pi * (np.outer(ar, ar) % P) / P
    chan = lambda a: np.repeat(a, D // a.size).reshape(P, 1)
    win = i["L1_attn_W_in"]
    bc = win[:, 512:1024].reshape(D, 2, H1, 32, 2).transpose(0, 1, 2, 4, 3).reshape(D, 512)
    cols = {
        "ident": np.eye(P), "ones": np.ones((P, P)),
        "wq0": i["L0_attn_w_qkv"][0:128].T, "wk0": i["L0_attn_w_qkv"][128:256].T,
        "wv0": i["L0_attn_w_qkv"][256:384].T, "wfc": i["L0_attn_w_fc"].T,
        "bfc": rows(i["L0_attn_b_fc"]), "gam0": rows(i["L0_attn_gamma"]), "bet0": rows(i["L0_attn_beta"]),
        "wr": i["L0_ffn_w_freq_real"], "wi": i["L0_ffn_w_freq_imag"],
        "cos": np.cos(angle), "sin": np.sin(angle), "nsin": -np.sin(angle), "fbias": rows(i["L0_ffn_bias"]),
        "win": np.concatenate([win[:, 0:512], bc, win[:, 1024:]], 1),
        "nw": i["L1_attn_norm_weight"].reshape(2, P).T,
        "wout": i["L1_attn_W_out"].reshape(2, P, D).transpose(1, 0, 2).reshape(P, 2 * D),
        "dtb": rows(i["L1_attn_dt_bias"]), "alog": rows(i["L1_attn_A_log"]),
        "freq": rows((1.0 / 10000.0 ** (np.arange(32, dtype=f) / f(32))).astype(f)),
        "upper": (ar[:, None] <= ar[None, :]), "below": (ar[:, None] > ar[None, :]),
        "shift": (ar[:, None] == ar[None, :] + 1), "first": (ar[:, None] == 0) & (ar[None, :] == P - 1),
        "mask": np.where(ar[:, None] > ar[None, :], f(-30000.0), f(0.0)),
        "gw": i["L1_ffn_gate_W"], "gb": rows(i["L1_ffn_gate_b"]), "rank": rows(E8 - np.arange(E8, dtype=f)),
        "b1m": i["L1_ffn_b1"].reshape(E8, 2, P).transpose(2, 0, 1).reshape(P, 16),
        "lng": rows(i["L1_ffn_ln_gamma"]), "lnb": rows(i["L1_ffn_ln_beta"]),
        "mk": chan(i["L2_attn_mix_k"]), "mv": chan(i["L2_attn_mix_v"]), "mr": chan(i["L2_attn_mix_r"]),
        "wkey": i["L2_attn_W_key"].T, "wval": i["L2_attn_W_value"].T, "wrec": i["L2_attn_W_receptance"].T,
        "wo2": i["L2_attn_W_output"].T, "td": chan(i["L2_attn_time_decay"]), "tf": chan(i["L2_attn_time_first"]),
        "blocks": (ar[:, None] // 8 == ar[None, :] // 8), "time": rows(np.arange(S, dtype=f)),
        "w1f": i["L2_ffn_W1"], "b1f": i["L2_ffn_b1"].reshape(4, P).T,
        "w2f": i["L2_ffn_W2"].reshape(4, P, D).transpose(1, 0, 2).reshape(P, 4 * D), "b2f": rows(i["L2_ffn_b2"]),
        "wq3": i["L3_attn_Wq"].T, "wk3": i["L3_attn_Wk"].T, "wv3": i["L3_attn_Wv"].T, "wo3": i["L3_attn_Wo"].T,
        "bo3": rows(i["L3_attn_bo"]),
        "wr1": i["L3_ffn_Wr1"], "br1": rows(i["L3_ffn_br1"]), "lns": rows(i["L3_ffn_ln_scale"]),
        "lnbi": rows(i["L3_ffn_ln_bias"]),
        "wr2": np.concatenate([i["L3_ffn_Wr2"], i["L3_ffn_Wr2"]], 0), "br2": rows(i["L3_ffn_br2"]),
        "b1g": i["L3_ffn_b1"].reshape(E8, 8, P).transpose(2, 0, 1).reshape(P, 64),
    }
    pack = np.concatenate([np.asarray(cols[k]).astype(f).reshape(P, wd) for k, (_, wd) in PACK.items()], 1)
    return {
        "x": np.ascontiguousarray(i["L0_attn_x"].reshape(NT_TILES, P, D)),
        "pack": np.ascontiguousarray(pack),
        "b2s": np.ascontiguousarray(np.concatenate([i["L1_ffn_b2"], i["L3_ffn_b2"]], 1)),
        "l1w1": np.ascontiguousarray(i["L1_ffn_W1"]),
        "l1w2": np.ascontiguousarray(i["L1_ffn_W2"].reshape(E8, 2, P, D).transpose(0, 2, 1, 3)),
        "l3w1": np.ascontiguousarray(i["L3_ffn_W1"]),
        "l3w2": np.ascontiguousarray(i["L3_ffn_W2"].reshape(E8, 4, P, D).transpose(0, 2, 1, 3)),
    }
```

```python
import concourse.bass as bass
from concourse import mybir
from contextlib import ExitStack
import numpy as np

F32 = mybir.dt.float32
F32R = mybir.dt.float32r
BF16 = mybir.dt.bfloat16
U32 = mybir.dt.uint32
ALU = mybir.AluOpType
ACT = mybir.ActivationFunctionType
AX = mybir.AxisListType

B, S, D = 2, 1024, 128
P = 128
NT_TILES = B * S // P
TPB = S // P
GT = 4
G = NT_TILES // GT
GW = GT * P
TOK = B * S
STAGES = 8


def columns(widths):
    at, out = 0, {}
    for name, w in widths:
        out[name] = (at, w)
        at += w
    return out, at


H1, N1, P1 = 4, 64, 64
E8 = 8
HID1 = 256
HID2 = 512
F3 = 512
KR = 64
NH3, HD3 = 16, 8

PACK, PACK_W = columns([
    ("ident", 128), ("ones", 128),
    ("wq0", 128), ("wk0", 128), ("wv0", 128), ("wfc", 128), ("bfc", 128), ("gam0", 128), ("bet0", 128),
    ("wr", 128), ("wi", 128), ("cos", 128), ("sin", 128), ("nsin", 128), ("fbias", 128),
    ("win", 1028), ("nw", 2), ("wout", 256), ("dtb", H1), ("alog", H1), ("freq", 32),
    ("upper", 128), ("below", 128), ("shift", 128), ("first", 128), ("mask", 128),
    ("gw", E8), ("gb", E8), ("rank", E8), ("b1m", 16), ("lng", 128), ("lnb", 128),
    ("mk", 1), ("mv", 1), ("mr", 1), ("wkey", 128), ("wval", 128), ("wrec", 128), ("wo2", 128),
    ("td", 1), ("tf", 1), ("blocks", 128), ("time", 1024),
    ("w1f", HID2), ("b1f", 4), ("w2f", 4 * 128), ("b2f", 128),
    ("wq3", 128), ("wk3", 128), ("wv3", 128), ("wo3", 128), ("bo3", 128),
    ("wr1", KR), ("br1", KR), ("lns", KR), ("lnbi", KR), ("wr2", E8), ("br2", E8), ("b1g", 64),
])


def program(nc, x_in, pack, b2s, l1w1, l1w2, l3w1, l3w2, out):
    ctx = ExitStack()
    with ctx:
        sb = lambda n, s, d=F32: ctx.enter_context(nc.sbuf_tensor(n, s, d))
        sem = lambda n: ctx.enter_context(nc.semaphore(n))
        X = sb("X", [P, NT_TILES, D])
        XN = sb("XN", [P, NT_TILES, D])
        NT = [sb(f"NT{i}", [P, TOK]) for i in range(2)]
        W = sb("W", [P, PACK_W])
        W2S = sb("W2S", [E8, 2 * D])
        STAT = sb("STAT", [P, GT, 6])
        MV = sb("MV", [P, 6, GT, 2])
        VPE = sb("VPE", [P, 6, GT])
        RSTD = sb("RSTD", [P, 6, GT])
        NM, NMR = sb("NM", [P, 2, GT]), sb("NMR", [P, 2, GT])
        MHALF = sb("MHALF", [P, 64])
        PS = [ctx.enter_context(nc.psum_tensor(f"PS{i}", [P, 512], F32)) for i in range(8)]

        def w(name, a=0, n=None, rows=P):
            at, width = PACK[name]
            return W[0:rows, at + a:at + a + (width - a if n is None else n)]

        c = Common()
        c.nc, c.X, c.XN, c.NT, c.w, c.PS, c.W2S = nc, X, XN, NT, w, PS, W2S
        c.STAT, c.MV, c.VPE, c.RSTD, c.MHALF, c.NM, c.NMR = STAT, MV, VPE, RSTD, MHALF, NM, NMR
        c.nmr_ready = sem("nmr_ready")
        c.out = out
        c.var_ready, c.rstd_ready = sem("var_ready"), sem("rstd_ready")
        c.xs_ready, c.xs_transposed, c.nt_ready = sem("xs_ready"), sem("xs_transposed"), sem("nt_ready")
        c.out_stored = sem("out_stored")
        c.dve = Chain(sem("dve_steps"))
        c.n_var, c.n_front = 0, 0
        loads(c, x_in, pack, b2s)
        if STAGES >= 1:
            l0_attn(c)
        if STAGES >= 2:
            l0_ffn(c)
        if STAGES >= 3:
            l1_attn(c)
        if STAGES >= 4:
            l1_ffn(c, l1w1, l1w2)
        if STAGES >= 5:
            l2_attn(c)
        if STAGES >= 6:
            l2_ffn(c)
        if STAGES >= 7:
            l3_attn(c)
        if STAGES >= 8:
            l3_ffn(c, l3w1, l3w2)
        if STAGES < 8:
            with nc.Block() as block:
                @block.sync
                def _(sp):
                    sp.dma_start(out.rearrange("t p d -> p t d"), X[:, :, :]).then_inc(c.out_stored, 16)
                    sp.wait_ge(c.out_stored, 16)


class Common:
    pass


def cleared(nc, name, used):
    s = nc.alloc_semaphore(name)
    used.append(s)
    return s


class Chain:

    def __init__(self, sem):
        self.sem, self.n = sem, 0

    def link(self, eng, ins):
        self.n += 1
        ins.then_inc(self.sem, 1)
        eng.wait_ge(self.sem, self.n)


def schedule(phases):
    return [(step - p, p) for step in range(G + phases - 1) for p in range(phases) if 0 <= step - p < G]


def slot(phase, g):
    return 2 * phase + g % 2


def statistics(c, v, tiles, sl, negative_mean=None, eps=1e-5):
    nc = c.nc
    for j in range(GT):
        last = nc.vector.bn_stats(c.STAT[:, j, :], tiles[:, j, :])
    c.dve.link(v, last)
    for j in range(GT):
        last = nc.vector.bn_aggr(c.MV[:, sl, j, :], c.STAT[:, j, :])
    c.dve.link(v, last)
    if negative_mean is not None:
        c.dve.link(v, nc.vector.tensor_scalar(negative_mean, c.MV[:, sl, :, 0], -1.0, None, ALU.mult))
    nc.vector.tensor_scalar(c.VPE[:, sl, :], c.MV[:, sl, :, 1], eps, None, ALU.add).then_inc(c.var_ready, 1)


def normalise(c, eng, outs, tiles, sl):
    for j in range(GT):
        last = eng.tensor_scalar(outs[:, j, :], tiles[:, j, :], c.MV[:, sl, j, 0:1], c.RSTD[:, sl, j:j + 1], ALU.subtract, ALU.mult)
    return last


def tails(c, v, make, between=None, finish=None):
    phases = 3 if between else 2
    base, nv0 = c.n_front, c.n_var
    requests = [gp for gp in schedule(phases) if not (finish and gp[1] == phases - 1)]
    number = {gp: nv0 + k + 1 for k, gp in enumerate(requests)}
    made = {}
    for g, p in schedule(phases):
        if p:
            v.wait_ge(c.rstd_ready, number[g, p - 1])
        if p == 0:
            source = made[g] = make(g)
        elif p < phases - 1:
            c.dve.link(v, normalise(c, c.nc.vector, made[g], made[g], slot(p - 1, g)))
            source = made[g]
            between(source)
        else:
            source = c.X[:, GT * g:GT * g + GT, :]
            c.dve.link(v, normalise(c, c.nc.vector, made[g], made[g], slot(p - 1, g)))
            c.dve.link(v, c.nc.vector.tensor_tensor(source, source, made[g], ALU.add))
            if finish:
                finish(g)
                continue
            if g >= 2:
                v.wait_ge(c.xs_ready, base + g - 1)
        statistics(c, v, source, slot(p, g), c.NM[:, g % 2, :] if p == phases - 1 else None)
    c.n_var += len(requests)
    if not finish:
        c.n_front += G


def pool_tails(c, pool, phases, nv0, base, finish=False):
    n = nv0
    for g, p in schedule(phases):
        last = p == phases - 1
        if last and finish:
            continue
        n += 1
        sl = slot(p, g)
        pool.wait_ge(c.var_ready, n)
        c.nc.gpsimd.tensor_tensor(c.RSTD[:, sl, :], c.VPE[:, sl, :], c.MHALF[:, 0:GT], ALU.pow).then_inc(c.rstd_ready, 1)
        if last:
            pool.wait_ge(c.rstd_ready, n)
            if base + g >= 2:
                pool.wait_ge(c.xs_ready, base + g - 1)
            c.nc.gpsimd.tensor_tensor(c.NMR[:, g % 2, :], c.NM[:, g % 2, :], c.RSTD[:, sl, :], ALU.mult)\
                .then_inc(c.nmr_ready, 1)


def normalise_x(c, act, phases, base, g):
    act.wait_ge(c.nmr_ready, base + g + 1)
    sl = slot(phases - 1, g)
    for j in range(GT):
        last = c.nc.scalar.activation(c.XN[:, GT * g + j, :], c.X[:, GT * g + j, :], ACT.Identity,
                                      bias=c.NMR[:, g % 2, j:j + 1], scale=c.RSTD[:, sl, j:j + 1])
    last.then_inc(c.xs_ready, 1)


def transpose_xn(c, pe, base, g, bank):
    pe.wait_ge(c.xs_ready, base + g + 1)
    if base + g:
        pe.wait_ge(c.nt_ready, base + g)
    for j in range(GT):
        last = c.nc.tensor.transpose(bank[:, P * j:P * j + P], c.XN[:, GT * g + j, :], c.w("ident"))
    last.then_inc(c.xs_transposed, 1)


def act_tails(c, act, phases, base, nt, bank):
    for g in range(G + 1):
        if g < G:
            normalise_x(c, act, phases, base, g)
        if g:
            act.wait_ge(c.xs_transposed, base + g)
            c.nc.scalar.activation(nt[:, GW * (g - 1):GW * g], bank[:, :], ACT.Copy).then_inc(c.nt_ready, 1)


def loads(c, x_in, pack, b2s):
    nc = c.nc
    with ExitStack() as ctx:
        x_loaded = [ctx.enter_context(nc.semaphore(f"x_loaded{g}")) for g in range(G)]
        w_loaded = ctx.enter_context(nc.semaphore("w_loaded"))
        const_ready = ctx.enter_context(nc.semaphore("const_ready"))
        with nc.Block() as block:
            @block.sync
            def _(sp):
                for g in range(G):
                    sp.dma_start(c.X[:, GT * g:GT * g + GT, :],
                                 x_in[GT * g:GT * g + GT].rearrange("t p d -> p t d")).then_inc(x_loaded[g], 16)
                sp.dma_start(c.W2S[:, :], b2s).then_inc(w_loaded, 16)
                sp.wait_ge(w_loaded, 32)

            @block.scalar
            def _(act):
                act.dma_start(c.w("ident", 0, PACK_W), pack).then_inc(w_loaded, 16)
                act_tails(c, act, 1, 0, c.NT[0], c.PS[7])

            @block.tensor
            def _(pe):
                pe.wait_ge(w_loaded, 32)
                for g in range(G):
                    transpose_xn(c, pe, 0, g, c.PS[7])

            @block.gpsimd
            def _(pool):
                nc.gpsimd.memset(c.MHALF[:, :], -0.5).then_inc(const_ready, 1)
                pool.wait_ge(const_ready, 1)
                pool_tails(c, pool, 1, 0, 0)

            @block.vector
            def _(v):
                for g in range(G):
                    v.wait_ge(x_loaded[g], 16)
                    if g >= 2:
                        v.wait_ge(c.xs_ready, g - 1)
                    statistics(c, v, c.X[:, GT * g:GT * g + GT, :], slot(0, g), c.NM[:, g % 2, :])
                c.n_var, c.n_front = G, G


def l0_attn(c):
    nc, w, PS = c.nc, c.w, c.PS
    SCALE = D ** -0.5
    base = c.n_front
    nv0 = c.n_var
    with ExitStack() as ctx:
        sb = lambda n, s, d=F32: ctx.enter_context(nc.sbuf_tensor(n, s, d))
        sem = lambda n: ctx.enter_context(nc.semaphore(n))
        KT, QT = sb("a0_KT", [P, TOK]), sb("a0_QT", [P, TOK])
        MX, NB, L, AS = sb("a0_MX", [P, 16, 2]), sb("a0_NB", [P, 16]), sb("a0_L", [P, 16]), sb("a0_AS", [P, 16])
        MXC, LH = sb("a0_MXC", [P, 16]), sb("a0_LH", [P, 16, 2])
        NSUM, VS, VB, FB = sb("a0_NS", [P, B]), sb("a0_VS", [P, B]), sb("a0_VB", [P, B, D]), sb("a0_FB", [P, B, D])
        Y = sb("a0_Y", [P, 3, GT, D])
        EJ = sb("a0_E", [P, S])
        qk_done, qk_copied = sem("qk_done"), sem("qk_copied")
        l_half = sem("l_half")
        scores_ready, bias_ready, exp_done = sem("scores_ready"), sem("bias_ready"), sem("exp_done")
        nsum_ready, v_ready, vb_ready, f_ready, fb_ready = (
            sem("nsum_ready"), sem("v_ready"), sem("vb_ready"), sem("f_ready"), sem("fb_ready"))
        dve = c.dve
        with nc.Block() as block:
            @block.tensor
            def _(pe):
                for g in range(G):
                    if g:
                        pe.wait_ge(qk_copied, 2 * g)
                    for j, name in enumerate(("wq0", "wk0")):
                        nc.tensor.matmul(PS[j][:, :], w(name), c.NT[0][:, GW * g:GW * g + GW],
                                         start=True, stop=True).then_inc(qk_done, 1)
                pe.wait_ge(nsum_ready, 1)
                nc.tensor.matmul(PS[2][:, 0:B], w("wv0"), NSUM[:, :], start=True, stop=True).then_inc(v_ready, 1)
                pe.wait_ge(vb_ready, 1)
                for b in range(B):
                    last = nc.tensor.matmul(PS[3][:, b * D:b * D + D], VB[:, b, :], w("wfc"), start=True, stop=True)
                last.then_inc(f_ready, 1)
                pe.wait_ge(qk_copied, 2 * G)
                for t in range(NT_TILES):
                    b, s = t // TPB, t % 2
                    if t >= 2:
                        pe.wait_ge(exp_done, t - 1)
                    for half in range(2):
                        last = nc.tensor.matmul(PS[(0, 4)[s] + half][:, :], QT[:, P * t:P * t + P],
                                                KT[:, S * b + 512 * half:S * b + 512 * half + 512],
                                                start=True, stop=True)
                    last.then_inc(scores_ready, 1)
                for g in range(G):
                    transpose_xn(c, pe, base, g, PS[7])

            @block.scalar
            def _(act):
                for g in range(G):
                    for j, dst in enumerate((QT, KT)):
                        act.wait_ge(qk_done, 2 * g + j + 1)
                        nc.scalar.activation(dst[:, GW * g:GW * g + GW], PS[j][:, :], ACT.Copy).then_inc(qk_copied, 1)
                for t in range(NT_TILES):
                    act.wait_ge(bias_ready, t + 1)
                    if t >= 1:
                        act.wait_ge(exp_done, t)
                    for half in range(2):
                        k = (0, 4)[t % 2] + half
                        if half:
                            act.wait_ge(l_half, t + 1)
                        ins = nc.scalar.activation(EJ[:, 512 * half:512 * half + 512], PS[k][:, :], ACT.Exp,
                                                   bias=NB[:, t:t + 1], scale=SCALE,
                                                   accum_out=LH[:, t, half:half + 1])
                        ins.then_inc(exp_done if half else l_half, 1)
                act_tails(c, act, 3, base, c.NT[1], PS[7])

            @block.gpsimd
            def _(pool):
                pool_tails(c, pool, 3, nv0, base)

            @block.vector
            def _(v):
                for b in range(B):
                    last = nc.vector.reduce_sum(NSUM[:, b:b + 1], c.NT[0][:, S * b:S * b + S], axis=AX.X)
                last.then_inc(nsum_ready, 1)
                v.wait_ge(v_ready, 1)
                dve.link(v, nc.vector.tensor_copy(VS[:, :], PS[2][:, 0:B]))
                nc.vector.tensor_copy(VB[:, :, :], VS[:, :].unsqueeze(2).to_broadcast([P, B, D])).then_inc(vb_ready, 1)
                v.wait_ge(f_ready, 1)
                dve.link(v, nc.vector.tensor_copy(FB[:, :, :], PS[3][:, 0:B * D].rearrange("p (b d) -> p b d", b=B)))
                for t in range(NT_TILES):
                    v.wait_ge(scores_ready, t + 1)
                    for half in range(2):
                        last = nc.vector.reduce_max(MX[:, t, half:half + 1], PS[(0, 4)[t % 2] + half][:, :], axis=AX.X)
                    dve.link(v, last)
                    dve.link(v, nc.vector.reduce_max(MXC[:, t:t + 1], MX[:, t, :], axis=AX.X))
                    nc.vector.tensor_scalar(NB[:, t:t + 1], MXC[:, t:t + 1], -SCALE, None, ALU.mult).then_inc(bias_ready, 1)
                v.wait_ge(exp_done, NT_TILES)
                dve.link(v, nc.vector.reduce_sum(L[:, :], LH[:, :, :], axis=AX.X))
                dve.link(v, nc.vector.reciprocal(AS[:, :], L[:, :]))
                dve.link(v, nc.vector.tensor_tensor(AS[:, :], AS[:, :], L[:, :], ALU.mult))

                def make(g):
                    b = g // 2
                    YG = Y[:, g % 3, :, :]
                    dve.link(v, nc.vector.tensor_tensor(YG, c.XN[:, GT * g:GT * g + GT, :], rep(w("bfc"), GT), ALU.add))
                    for j in range(GT):
                        t = GT * g + j
                        last = nc.vector.scalar_tensor_tensor(YG[:, j, :], FB[:, b, :], AS[:, t:t + 1], YG[:, j, :],
                                                              ALU.mult, ALU.add)
                    dve.link(v, last)
                    return YG

                def own(YG):
                    dve.link(v, nc.vector.tensor_tensor(YG, YG, rep(w("gam0"), GT), ALU.mult))
                    dve.link(v, nc.vector.tensor_tensor(YG, YG, rep(w("bet0"), GT), ALU.add))
                tails(c, v, make, own)


def rep(ap, n):
    return ap.unsqueeze(1).to_broadcast([ap.shape[0], n, ap.shape[1]])


def project_tail(c, name, products, bias, nt_out, scale=None):
    nc, w, PS = c.nc, c.w, c.PS
    base, nv0 = c.n_front, c.n_var
    with ExitStack() as ctx:
        Y = ctx.enter_context(nc.sbuf_tensor(name + "_Y", [P, 2, GT, D], F32))
        y_made = ctx.enter_context(nc.semaphore(name + "_y_made"))
        y_read = ctx.enter_context(nc.semaphore(name + "_y_read"))
        with nc.Block() as block:
            @block.tensor
            def _(pe):
                for g in range(G + 2):
                    if g < G:
                        products(pe, g, PS[g]).then_inc(y_made, 1)
                    if g >= 2:
                        transpose_xn(c, pe, base, g - 2, PS[7])

            @block.scalar
            def _(act):
                act_tails(c, act, 2, base, nt_out, PS[7])

            @block.gpsimd
            def _(pool):
                pool_tails(c, pool, 2, nv0, base)

            @block.vector
            def _(v):
                def make(g):
                    v.wait_ge(y_made, g + 1)
                    made, YG = PS[g][:, :].rearrange("p (t d) -> p t d", t=GT), Y[:, g % 2, :, :]
                    if bias:
                        ins = nc.vector.tensor_tensor(YG, made, rep(w(bias), GT), ALU.add)
                    elif scale is not None:
                        ins = nc.vector.tensor_tensor(YG, made, scale[:, GT * g:GT * g + GT].unsqueeze(2)
                                                      .to_broadcast([P, GT, D]), ALU.mult)
                    else:
                        ins = nc.vector.tensor_copy(YG, made)
                    ins.then_inc(y_read, 1)
                    v.wait_ge(y_read, g + 1)
                    return YG
                tails(c, v, make)


def l0_ffn(c):
    nc, w, PS = c.nc, c.w, c.PS
    with ExitStack() as ctx:
        sb = lambda n, s, d=F32: ctx.enter_context(nc.sbuf_tensor(n, s, d))
        sem = lambda n: ctx.enter_context(nc.semaphore(n))
        AB, M = sb("f0_AB", [P, 2, D]), sb("f0_M", [P, D])
        ab_made, ab_copied, m_made, m_copied = sem("ab_made"), sem("ab_copied"), sem("m_made"), sem("m_copied")
        with nc.Block() as block:
            @block.tensor
            def _(pe):
                mm = nc.tensor.matmul
                mm(PS[0][:, 0:D], w("wr"), w("cos"), start=True, stop=False)
                mm(PS[0][:, 0:D], w("wi"), w("sin"), start=False, stop=True)
                mm(PS[1][:, 0:D], w("wi"), w("cos"), start=True, stop=False)
                mm(PS[1][:, 0:D], w("wr"), w("nsin"), start=False, stop=True).then_inc(ab_made, 1)
                pe.wait_ge(ab_copied, 2)
                mm(PS[2][:, 0:D], AB[:, 0, :], w("cos"), start=True, stop=False)
                mm(PS[2][:, 0:D], AB[:, 1, :], w("nsin"), start=False, stop=True).then_inc(m_made, 1)

            @block.scalar
            def _(act):
                act.wait_ge(ab_made, 1)
                for k in range(2):
                    nc.scalar.activation(AB[:, k, :], PS[k][:, 0:D], ACT.Copy).then_inc(ab_copied, 1)
                act.wait_ge(m_made, 1)
                nc.scalar.activation(M[:, :], PS[2][:, 0:D], ACT.Copy, scale=1.0 / D).then_inc(m_copied, 1)
                act.wait_ge(m_copied, 1)

        def products(pe, g, bank):
            for j in range(GT):
                t = GT * g + j
                last = nc.tensor.matmul(bank[:, P * j:P * j + P], c.NT[1][:, P * t:P * t + P], M[:, :],
                                        start=True, stop=True)
            return last
        project_tail(c, "f0", products, "fbias", c.NT[0])


def l1_attn(c):
    nc, w, PS = c.nc, c.w, c.PS
    dve = c.dve
    NTI = c.NT[0]
    TH = NT_TILES * H1
    used = []
    with ExitStack() as ctx:
        sb = lambda n, s, d=F32: ctx.enter_context(nc.sbuf_tensor(n, s, d))
        sem = lambda n: ctx.enter_context(nc.semaphore(n))
        SIN, COS = sb("s_SIN", [P, NT_TILES, H1 * 32]), sb("s_COS", [P, NT_TILES, H1 * 32])
        DT, DTA = sb("s_DT", [P, TH]), sb("s_DTA", [P, TH])
        EC, ETP = sb("s_EC", [P, TH]), sb("s_ETP", [P, NT_TILES, 2])
        WS, WED, CD = sb("s_WS", [P, TH]), sb("s_WED", [P, TH]), sb("s_CD", [P, TH])
        YT = sb("s_YT", [P, 2, TOK])
        SS, RR = sb("s_SS", [P, NT_TILES]), sb("s_RR", [P, NT_TILES])
        with ExitStack() as ctx1:
            sb1 = lambda n, s, d=F32: ctx1.enter_context(nc.sbuf_tensor(n, s, d))
            sem1 = lambda n: cleared(nc, n, used)
            RAW, AB, EX, LN = (sb1(n, [P, TH]) for n in ("s_RAW", "s_AB", "s_EX", "s_LN"))
            NEGA, CAR, TOTA, ET = sb1("s_NEGA", [P, H1]), sb1("s_CAR", [P, TH]), sb1("s_TOTA", [P, TH]), sb1("s_ET", [P, TH])
            TOT, CUM = sb1("s_TOT", [P, TH]), sb1("s_CUM", [P, TH])
            ANG, TURN = sb1("s_ANG", [P, TH, 32]), sb1("s_TURN", [P, TH, 32])
            dt_made, ab_ready, soft_ready, a_ready, dt_ready, sums_made = (sem1(n) for n in (
                "dt_made", "ab_ready", "soft_ready", "a_ready", "dt_ready", "sums_made"))
            decay_ready, decays, ang_ready, sin_ready, ex_ready = (sem1(n) for n in (
                "decay_ready", "decays", "ang_ready", "sin_ready", "ex_ready"))
            with nc.Block() as block:
                @block.tensor
                def _(pe):
                    mm = nc.tensor.matmul
                    for t in range(NT_TILES):
                        last = mm(PS[0][:, H1 * t:H1 * t + H1], NTI[:, P * t:P * t + P], w("win", 1024, H1),
                                  start=True, stop=True)
                    last.then_inc(dt_made, 1)
                    pe.wait_ge(dt_ready, 1)
                    for k, (lhs, rhs) in enumerate((("upper", DT), ("ones", DT), ("upper", DTA), ("ones", DTA))):
                        mm(PS[1 + k][:, 0:TH], w(lhs), rhs[:, :], start=True, stop=True)
                    mm(PS[5][:, 0:TH], w("shift"), DT[:, :], start=True, stop=False)
                    mm(PS[5][:, 0:TH - H1], w("first"), DT[:, H1:TH], start=False, stop=True).then_inc(sums_made, 1)

                @block.scalar
                def _(act):
                    nc.scalar.activation(NEGA[:, :], w("alog"), ACT.Exp).then_inc(a_ready, 1)
                    act.wait_ge(ab_ready, 1)
                    nc.scalar.activation(EX[:, :], AB[:, :], ACT.Exp, scale=-1.0).then_inc(ex_ready, 1)
                    act.wait_ge(ex_ready, 1)
                    nc.scalar.activation(LN[:, :], EX[:, :], ACT.Ln, bias=1.0).then_inc(soft_ready, 1)
                    act.wait_ge(decay_ready, 1)
                    nc.scalar.activation(EC[:, :], PS[3][:, 0:TH], ACT.Exp).then_inc(decays, 1)
                    nc.scalar.activation(ET[:, :], TOTA[:, :], ACT.Exp).then_inc(decays, 1)
                    nc.scalar.activation(WED[:, :], AB[:, :], ACT.Exp).then_inc(decays, 1)
                    act.wait_ge(ang_ready, 1)
                    nc.scalar.activation(SIN[:, :, :], ANG[:, :, :].rearrange("p (t h) f -> p t (h f)", h=H1), ACT.Sin)\
                        .then_inc(sin_ready, 1)
                    nc.scalar.activation(COS[:, :, :], ANG[:, :, :].rearrange("p (t h) f -> p t (h f)", h=H1), ACT.Sin,
                                         scale=0.5).then_inc(sin_ready, 1)

                @block.vector
                def _(v):
                    tt, ts, stt = nc.vector.tensor_tensor, nc.vector.tensor_scalar, nc.vector.scalar_tensor_tensor
                    v.wait_ge(dt_made, 1)
                    th = lambda a: a[:, :].rearrange("p (t h) -> p t h", h=H1)
                    dve.link(v, tt(th(RAW), PS[0][:, 0:TH].rearrange("p (t h) -> p t h", h=H1),
                                   rep(w("dtb"), NT_TILES), ALU.add))
                    stt(AB[:, :], RAW[:, :], -1.0, RAW[:, :], ALU.mult, ALU.max).then_inc(ab_ready, 1)
                    v.wait_ge(soft_ready, 1)
                    dve.link(v, stt(DT[:, :], RAW[:, :], 0.0, LN[:, :], ALU.max, ALU.add))
                    v.wait_ge(a_ready, 1)
                    dve.link(v, ts(NEGA[:, :], NEGA[:, :], -1.0, None, ALU.mult))
                    tt(th(DTA), th(DT), rep(NEGA[:, :], NT_TILES), ALU.mult).then_inc(dt_ready, 1)
                    v.wait_ge(sums_made, 1)
                    dve.link(v, nc.vector.tensor_copy(TOTA[:, :], PS[4][:, 0:TH]))
                    dve.link(v, tt(AB[:, :], TOTA[:, :], PS[3][:, 0:TH], ALU.subtract))
                    nc.vector.tensor_copy(TOT[:, :], PS[2][:, 0:TH]).then_inc(decay_ready, 1)
                    v.wait_ge(decay_ready, 1)
                    bc = lambda a, k: a[:, :].rearrange("p (b c h) -> p b c h", b=B, h=H1)[:, :, k, :]
                    dve.link(v, nc.vector.memset(bc(CAR, 0), 0.0))
                    for k in range(1, TPB):
                        dve.link(v, tt(bc(CAR, k), bc(CAR, k - 1), bc(TOT, k - 1), ALU.add))
                    dve.link(v, tt(CUM[:, :], CAR[:, :], PS[1][:, 0:TH], ALU.add))
                    ts_magic = 12582912.0
                    dve.link(v, tt(ANG[:, :, :], CUM[:, :].unsqueeze(2).to_broadcast([P, TH, 32]),
                                   rep(w("freq"), TH), ALU.mult))
                    dve.link(v, ts(TURN[:, :, :], ANG[:, :, :], 1.0 / (2 * np.pi), ts_magic, ALU.mult, ALU.add))
                    dve.link(v, ts(TURN[:, :, :], TURN[:, :, :], ts_magic, None, ALU.subtract))
                    for part in turn_parts():
                        dve.link(v, stt(ANG[:, :, :], TURN[:, :, :], -part, ANG[:, :, :], ALU.mult, ALU.add))
                    lim = float(np.nextafter(np.float32(np.pi), np.float32(0)))
                    ts(ANG[:, :, :], ANG[:, :, :], lim, -lim, ALU.min, ALU.max).then_inc(ang_ready, 1)
                    dve.link(v, ts(CD[:, :], PS[5][:, 0:TH], 0.5, None, ALU.mult))
                    dve.link(v, stt(WS[:, :], DT[:, :], 0.5, CD[:, :], ALU.mult, ALU.add))
                    v.wait_ge(decays, 3)
                    dve.link(v, tt(WED[:, :], WED[:, :], WS[:, :], ALU.mult))
                    for r in range(2):
                        last = nc.vector.tensor_copy(ETP[64 * r:64 * r + 64, :, :],
                                                     th(ET)[64 * r:64 * r + 64, :, r::2])
                    dve.link(v, last)
                    v.wait_ge(sin_ready, 2)
                    dve.link(v, tt(COS[:, :, :], COS[:, :, :], COS[:, :, :], ALU.mult))
                    dve.link(v, ts(COS[:, :, :], COS[:, :, :], -2.0, 1.0, ALU.mult, ALU.add))

        with ExitStack() as ctx1:
            sb1 = lambda n, s, d=F32: ctx1.enter_context(nc.sbuf_tensor(n, s, d))
            sem1 = lambda n: cleared(nc, n, used)
            two = lambda n, s: [sb1(f"{n}{i}", s) for i in range(2)]
            ZX, EZ = two("s_ZX", [P, 512]), two("s_EZ", [P, 256])
            PR = sb1("s_PR", [P, 4, 256])
            R = two("s_R", [P, 2, H1, 2, 32])
            CS = sb1("s_CS", [P, H1, 64])
            SL = sb1("s_SL", [P, H1, P])
            TB, TC = two("s_TB", [P, 512]), two("s_TC", [P, 256])
            ED = two("s_ED", [P, 512])
            XW, XD = two("s_XW", [P, H1, 64]), two("s_XD", [P, H1, 64])
            CB, CC = sb1("s_CB", [P, H1, 64]), two("s_CC", [P, H1])
            GE, H = sb1("s_GE", [P, 512]), sb1("s_H", [P, 2, P])
            YG, SG, XC = two("s_YG", [P, 256]), sb1("s_SG", [P, 256]), sb1("s_XC", [P, 256])
            SQ = sb1("s_SQ", [P, 256])
            (proj_made, zx_copied, ez_ready, prods_ready, rot_ready, cs_ready, sl_ready, decay_made, decay_read,
             turned, turned_copied, g_made, ge_ready, xw_ready, y_made, y_read, h_ready, yg_ready, ss_ready,
             rr_ready, yt_made, yt_copied, cc_ready, h_zero, sg_ready, rr_in, g_half) = (
                sem1("ssd_" + n) for n in (
                    "proj_made", "zx_copied", "ez_ready", "prods_ready", "rot_ready", "cs_ready", "sl_ready",
                    "decay_made", "decay_read", "turned", "turned_copied", "g_made", "ge_ready", "xw_ready",
                    "y_made", "y_read", "h_ready", "yg_ready", "ss_ready", "rr_ready", "yt_made",
                    "yt_copied", "cc_ready", "h_zero", "sg_ready", "rr_in", "g_half"))
            zb, bb, db, tb, tcb, gb, yb, ob = PS[0], PS[1], PS[2], PS[3], PS[4], PS[5], PS[6], PS[7]
            BCV = bb[:, :].rearrange("p (c h e f) -> p (c h) e f", c=2, h=H1, e=2)
            rsel = lambda r, k: r[:, k, :, :, :].rearrange("p h e f -> p h (e f)")
            steps = range(NT_TILES + 2)
            with nc.Block() as block:
                @block.tensor
                def _(pe):
                    mm, tr = nc.tensor.matmul, nc.tensor.transpose
                    for i in steps:
                        if i < NT_TILES:
                            t = i
                            if t:
                                pe.wait_ge(zx_copied, t)
                                pe.wait_ge(ez_ready, t)
                                pe.wait_ge(prods_ready, t)
                            for k, bank in enumerate((bb, zb)):
                                last = mm(bank[:, :], NTI[:, P * t:P * t + P], w("win", 512 * (1 - k), 512),
                                          start=True, stop=True)
                            last.then_inc(proj_made, 1)
                        if 1 <= i <= NT_TILES:
                            t = i - 1
                            pe.wait_ge(turned_copied, 2 * t + 2)
                            if t:
                                pe.wait_ge(ge_ready, t)
                            for h in (0, 2, 1, 3):
                                r, q = 64 * (h % 2), P * (h // 2)
                                if h == 1:
                                    last.then_inc(g_half, 1)
                                    pe.wait_ge(g_half, t + 1)
                                last = mm(gb[:, P * h:P * h + P], TB[t % 2][r:r + 64, q:q + P],
                                          TB[t % 2][r:r + 64, 256 + q:256 + q + P], start=True, stop=True)
                            last.then_inc(g_made, 1)
                        if i < NT_TILES:
                            t = i
                            pe.wait_ge(sl_ready, t + 1)
                            if t:
                                pe.wait_ge(decay_read, t)
                            for h in range(H1):
                                last = mm(db[:, P * h:P * h + P], SL[:, h, :], w("upper"), start=True, stop=False)
                                last = mm(db[:, P * h:P * h + P], w("ident"), w("mask"), start=False, stop=True)
                            last.then_inc(decay_made, 1)
                        if 1 <= i <= NT_TILES:
                            t = i - 1
                            pe.wait_ge(ge_ready, t + 1)
                            pe.wait_ge(xw_ready, t + 1)
                            if t:
                                pe.wait_ge(y_read, t)
                                pe.wait_ge(h_ready, t)
                            first = True
                            if t % TPB:
                                for pair in range(2):
                                    mm(yb[:, P * pair:P * pair + P], TC[t % 2][:, P * pair:P * pair + P], H[:, pair, :],
                                       start=first, stop=False, skip_group_check=True)
                                    first = False
                            for h in range(H1):
                                mm(yb[:, 64 * h:64 * h + 64], GE[:, P * h:P * h + P], XW[t % 2][:, h, :],
                                   start=first, stop=True, skip_group_check=True)
                                first = False
                            for pair in range(2):
                                last = mm(yb[:, 256 + P * pair:256 + P * pair + P],
                                          rsel(R[t % 2], 0)[:, 2 * pair:2 * pair + 2, :].rearrange("p h n -> p (h n)"),
                                          XD[t % 2][:, 2 * pair:2 * pair + 2, :].rearrange("p h n -> p (h n)"),
                                          start=False, stop=True, skip_group_check=True)
                            last.then_inc(y_made, 1)
                        if i >= 2:
                            t = i - 2
                            pe.wait_ge(yg_ready, t + 1)
                            if t:
                                pe.wait_ge(yt_copied, t)
                            for pair in range(2):
                                last = tr(ob[:, P * pair:P * pair + P], YG[t % 2][:, P * pair:P * pair + P], w("ident"))
                            last.then_inc(yt_made, 1)
                        if i < NT_TILES:
                            t = i
                            pe.wait_ge(rot_ready, t + 1)
                            pe.wait_ge(cs_ready, t + 1)
                            if t:
                                pe.wait_ge(turned_copied, 2 * t)
                            for k in range(2):
                                for pair in range(2):
                                    tr(tb[:, 256 * k + P * pair:256 * k + P * pair + P],
                                       rsel(R[t % 2], k)[:, 2 * pair:2 * pair + 2, :].rearrange("p h n -> p (h n)"),
                                       w("ident"))
                            for pair in range(2):
                                last = tr(tcb[:, P * pair:P * pair + P],
                                          CS[:, 2 * pair:2 * pair + 2, :].rearrange("p h n -> p (h n)"), w("ident"))
                            last.then_inc(turned, 1)

                @block.scalar
                def _(act):
                    av = nc.scalar.activation
                    for i in steps:
                        if i < NT_TILES:
                            t = i
                            act.wait_ge(proj_made, t + 1)
                            if t >= 2:
                                act.wait_ge(yg_ready, t - 1)
                                act.wait_ge(xw_ready, t - 1)
                                act.wait_ge(sg_ready, t - 1)
                            av(ZX[t % 2][:, :], zb[:, :], ACT.Copy).then_inc(zx_copied, 1)
                            av(EZ[t % 2][:, :], zb[:, 0:256], ACT.Exp, scale=-1.0).then_inc(ez_ready, 1)
                            act.wait_ge(decay_made, t + 1)
                            if t >= 2:
                                act.wait_ge(ge_ready, t - 1)
                            av(ED[t % 2][:, :], db[:, :], ACT.Exp).then_inc(decay_read, 1)
                            act.wait_ge(turned, t + 1)
                            if t >= 2:
                                act.wait_ge(y_made, t - 1)
                            av(TB[t % 2][:, :], tb[:, :], ACT.Copy).then_inc(turned_copied, 1)
                            av(TC[t % 2][:, :], tcb[:, 0:256], ACT.Copy).then_inc(turned_copied, 1)
                        if 1 <= i <= NT_TILES:
                            t = i - 1
                            act.wait_ge(yg_ready, t + 1)
                            if t:
                                act.wait_ge(ss_ready, t)
                            av(SQ[:, :], YG[t % 2][:, :], ACT.Square, accum_out=SS[:, t:t + 1]).then_inc(ss_ready, 1)
                        if i >= 2:
                            t = i - 2
                            act.wait_ge(yt_made, t + 1)
                            for pair in range(2):
                                last = av(YT[:, pair, P * t:P * t + P], ob[:, P * pair:P * pair + P], ACT.Copy,
                                          scale=w("nw", pair, 1))
                            last.then_inc(yt_copied, 1)

                @block.gpsimd
                def _(pool):
                    gt = nc.gpsimd.tensor_tensor
                    for i in steps:
                        if i < NT_TILES:
                            t, hs = i, slice(H1 * i, H1 * i + H1)
                            if t:
                                pool.wait_ge(decay_made, t)
                            gt(SL[:, :, :], rep(w("below"), H1), DTA[:, hs].unsqueeze(2).to_broadcast([P, H1, P]),
                               ALU.mult).then_inc(sl_ready, 1)
                            pool.wait_ge(prods_ready, t + 1)
                            if t >= 2:
                                pool.wait_ge(y_made, t - 1)
                                pool.wait_ge(cc_ready, t - 1)
                            pr = lambda k: PR[:, k, :].rearrange("p (c f) -> p c f", f=32)
                            ro = lambda e: R[t % 2][:, :, :, e, :].rearrange("p c h f -> p (c h) f")
                            gt(ro(0), pr(0), pr(1), ALU.subtract)
                            gt(ro(1), pr(2), pr(3), ALU.add).then_inc(rot_ready, 1)
                            pool.wait_ge(rot_ready, t + 1)
                            if t:
                                pool.wait_ge(turned, t)
                            gt(CS[:, :, :], rsel(R[t % 2], 1), EC[:, hs].unsqueeze(2).to_broadcast([P, H1, 64]),
                               ALU.mult).then_inc(cs_ready, 1)
                            pool.wait_ge(zx_copied, t + 1)
                            if t >= 2:
                                pool.wait_ge(y_made, t - 1)
                            xh = ZX[t % 2][:, 256:512].rearrange("p (h n) -> p h n", h=H1)
                            gt(XW[t % 2][:, :, :], xh, WS[:, hs].unsqueeze(2).to_broadcast([P, H1, 64]), ALU.mult)
                            gt(XD[t % 2][:, :, :], xh, WED[:, hs].unsqueeze(2).to_broadcast([P, H1, 64]), ALU.mult)\
                                .then_inc(xw_ready, 1)
                    pool.wait_ge(rr_in, 1)
                    gt(RR[:, :], SS[:, :], c.MHALF[:, 0:NT_TILES], ALU.pow).then_inc(rr_ready, 1)

                @block.vector
                def _(v):
                    tt, ts, stt = nc.vector.tensor_tensor, nc.vector.tensor_scalar, nc.vector.scalar_tensor_tensor
                    nc.vector.memset(H[:, :, :], 0.0).then_inc(h_zero, 1)
                    v.wait_ge(h_zero, 1)
                    for i in steps:
                        if i < NT_TILES:
                            t, hs = i, slice(H1 * i, H1 * i + H1)
                            v.wait_ge(proj_made, t + 1)
                            if t:
                                v.wait_ge(rot_ready, t)
                            cs, sn = (a[:, t, :].rearrange("p (h f) -> p h f", h=H1) for a in (COS, SIN))
                            for k, (e, tr) in enumerate(((0, cs), (1, sn), (0, sn), (1, cs))):
                                for cc in range(2):
                                    last = tt(PR[:, k, P * cc:P * cc + P].rearrange("p (h f) -> p h f", h=H1),
                                              BCV[:, H1 * cc:H1 * cc + H1, e, :], tr, ALU.mult)
                            last.then_inc(prods_ready, 1)
                        if 1 <= i <= NT_TILES:
                            t = i - 1
                            v.wait_ge(g_made, t + 1)
                            v.wait_ge(decay_read, t + 1)
                            if t:
                                v.wait_ge(y_made, t)
                            tt(GE[:, :], gb[:, :], ED[t % 2][:, :], ALU.mult).then_inc(ge_ready, 1)
                            xh = ZX[t % 2][:, 256:512].rearrange("p (h n) -> p h n", h=H1)
                            v.wait_ge(zx_copied, t + 1)
                            dve.link(v, tt(XC[:, :].rearrange("p (h n) -> p h n", h=H1), xh,
                                           CC[t % 2][:, :].unsqueeze(2).to_broadcast([P, H1, 64]), ALU.mult))
                        if i < NT_TILES:
                            t, hs = i, slice(H1 * i, H1 * i + H1)
                            v.wait_ge(rot_ready, t + 1)
                            dve.link(v, tt(CB[:, :, :], rsel(R[t % 2], 0), rsel(R[t % 2], 1), ALU.mult))
                            dve.link(v, nc.vector.reduce_sum(CC[t % 2][:, :], CB[:, :, :], axis=AX.X))
                            tt(CC[t % 2][:, :], CC[t % 2][:, :], CD[:, hs], ALU.mult).then_inc(cc_ready, 1)
                            v.wait_ge(cc_ready, t + 1)
                        if 1 <= i <= NT_TILES:
                            t = i - 1
                            v.wait_ge(ez_ready, t + 1)
                            dve.link(v, ts(SG[:, :], EZ[t % 2][:, :], 1.0, None, ALU.add))
                            dve.link(v, nc.vector.reciprocal(SG[:, :], SG[:, :]))
                            tt(SG[:, :], SG[:, :], ZX[t % 2][:, 0:256], ALU.mult).then_inc(sg_ready, 1)
                            v.wait_ge(y_made, t + 1)
                            if t >= 2:
                                v.wait_ge(yt_made, t - 1)
                                v.wait_ge(ss_ready, t - 1)
                            tt(YG[t % 2][:, :], yb[:, 0:256], XC[:, :], ALU.subtract).then_inc(y_read, 1)
                            for pair in range(2):
                                for r in range(2):
                                    rows, cols = slice(64 * r, 64 * r + 64), slice(64 * r, 64 * r + 64)
                                    src = yb[rows, 256 + P * pair + 64 * r:256 + P * pair + 64 * r + 64]
                                    if t % TPB == 0:
                                        last = nc.vector.tensor_copy(H[rows, pair, cols], src)
                                    else:
                                        last = stt(H[rows, pair, cols], H[rows, pair, cols],
                                                   ETP[rows, t, pair:pair + 1], src, ALU.mult, ALU.add)
                            last.then_inc(h_ready, 1)
                            v.wait_ge(y_read, t + 1)
                            v.wait_ge(sg_ready, t + 1)
                            tt(YG[t % 2][:, :], YG[t % 2][:, :], SG[:, :], ALU.mult).then_inc(yg_ready, 1)
                    v.wait_ge(ss_ready, NT_TILES)
                    ts(SS[:, :], SS[:, :], 1.0 / 256, 1e-6, ALU.mult, ALU.add).then_inc(rr_in, 1)

        def products(pe, g, bank):
            for j in range(GT):
                t = GT * g + j
                for k in range(2):
                    last = nc.tensor.matmul(bank[:, P * j:P * j + P], YT[:, k, P * t:P * t + P], w("wout", D * k, D),
                                            start=(k == 0), stop=(k == 1))
            return last
        nc.clear_and_free_semaphores(used)
        nc.all_engine_barrier()
        project_tail(c, "s1", products, None, c.NT[1], scale=RR)


def turn_parts():
    a = 6.28125
    b = float(np.float32(np.round((2 * np.pi - a) * 2 ** 20) / 2 ** 20))
    return a, b, 2 * np.pi - a - b


def softmax_top2(c, v, LG, T, probs_exp):
    nc, w, link = c.nc, c.w, c.dve.link
    tt, ts, stt = nc.vector.tensor_tensor, nc.vector.tensor_scalar, nc.vector.scalar_tensor_tensor
    n = NT_TILES
    bc = lambda a: a[:, :].unsqueeze(2).to_broadcast([P, n, E8])
    rmax = lambda o, a: link(v, nc.vector.reduce_max(o[:, :], a[:, :, :], axis=AX.X))
    exp_wanted, exp_done = probs_exp
    rmax(T.MX, LG)
    tt(T.A[:, :, :], LG[:, :, :], bc(T.MX), ALU.subtract).then_inc(exp_wanted, 1)
    v.wait_ge(exp_done, 1)
    link(v, nc.vector.reduce_sum(T.MX[:, :], T.PB[:, :, :], axis=AX.X))
    link(v, nc.vector.reciprocal(T.MX[:, :], T.MX[:, :]))
    link(v, tt(T.PB[:, :, :], T.PB[:, :, :], bc(T.MX), ALU.mult))
    for oh, m in ((T.OH1, T.M1), (T.OH2, T.M2)):
        rmax(m, T.PB)
        link(v, tt(T.A[:, :, :], T.PB[:, :, :], bc(m), ALU.is_equal))
        link(v, tt(T.A[:, :, :], T.A[:, :, :], rep(w("rank"), n), ALU.mult))
        rmax(T.MX, T.A)
        link(v, tt(oh[:, :, :], T.A[:, :, :], bc(T.MX), ALU.is_equal))
        if oh is T.OH1:
            link(v, stt(T.PB[:, :, :], oh[:, :, :], -2.0, T.PB[:, :, :], ALU.mult, ALU.add))


def choice_tiles(sb, tag):
    T = Common()
    T.A, T.PB, T.OH1, T.OH2 = (sb(f"{tag}_{n}", [P, NT_TILES, E8]) for n in ("A", "PB", "OH1", "OH2"))
    T.MX, T.M1, T.M2 = (sb(f"{tag}_{n}", [P, NT_TILES]) for n in ("MX", "M1", "M2"))
    return T


def start_sums(c, tag, OH, ACC, b2, MT, sums, split):
    nc, w, PS = c.nc, c.w, c.PS
    with ExitStack() as ctx:
        OHT = c.NT[0][0:E8, :]
        REST = ctx.enter_context(nc.sbuf_tensor(tag + "_REST", [E8, TOK], F32)) if split else None
        MID = ctx.enter_context(nc.sbuf_tensor(tag + "_MID", [E8, TOK], BF16)) if split else None
        oh_turned, oh_copied, b_made, b_copied = sums
        with nc.Block() as block:
            @block.tensor
            def _(pe):
                for g in range(G):
                    for j in range(GT):
                        last = nc.tensor.transpose(PS[g][0:E8, P * j:P * j + P], OH[:, GT * g + j, :], w("ident"))
                    last.then_inc(oh_turned, 1)
                for g in range(G):
                    pe.wait_ge(oh_copied, g + 1)
                    nc.tensor.matmul(PS[4 + g][:, :], b2, OHT[:, GW * g:GW * g + GW], start=True, stop=True)\
                        .then_inc(b_made, 1)

            @block.scalar
            def _(act):
                for g in range(G):
                    act.wait_ge(oh_turned, g + 1)
                    nc.scalar.activation(OHT[:, GW * g:GW * g + GW], PS[g][0:E8, :], ACT.Copy).then_inc(oh_copied, 1)
                for g in range(G):
                    act.wait_ge(b_made, g + 1)
                    nc.scalar.activation(ACC[:, GW * g:GW * g + GW], PS[4 + g][:, :], ACT.Copy).then_inc(b_copied, 1)

            @block.vector
            def _(v):
                cp, tt, link = nc.vector.tensor_copy, nc.vector.tensor_tensor, c.dve.link
                v.wait_ge(oh_copied, G)
                if not split:
                    cp(MT[:, :], OHT[:, :])
                else:
                    link(v, nc.vector.memset(MT[:, :].bitcast(U32), 0))
                    link(v, cp(MT[0:E8, :], OHT[:, :]))
                    link(v, tt(REST[:, :], OHT[:, :], MT[0:E8, :], ALU.subtract))
                    link(v, cp(MID[:, :], REST[:, :]))
                    cp(MT[32:32 + E8, :], MID[:, :])
                    link(v, tt(REST[:, :], REST[:, :], MID[:, :], ALU.subtract))
                    cp(MT[64:64 + E8, :], REST[:, :])


def expert_masks(c, v, SEL, SELF, rows):
    nc, w, link = c.nc, c.w, c.dve.link
    link(v, nc.vector.tensor_copy(SELF[0:rows, :], w("ident", 0, E8)[0:rows, :]))
    for part in range(32, rows, 32):
        link(v, nc.vector.tensor_tensor(SELF[0:rows, :], SELF[0:rows, :], w("ident", part, E8)[0:rows, :], ALU.add))
    link(v, nc.vector.tensor_copy(SEL[:, :, :], SELF[0:rows, :].unsqueeze(2).to_broadcast([rows, E8, P])))


HL = ((0, 0), (0, 1), (1, 0))


def l1_ffn(c, w1_dram, w2_dram):
    nc, w, PS = c.nc, c.w, c.PS
    dve = c.dve
    NTI = c.NT[1]
    with ExitStack() as ctx:
        sb = lambda n, s, d=F32: ctx.enter_context(nc.sbuf_tensor("m_" + n, s, d))
        sem = lambda n: ctx.enter_context(nc.semaphore("m_" + n))
        W1, W2 = sb("W1", [P, E8, HID1]), sb("W2", [P, E8, 2 * D])
        WU, WD = sb("WU", [P, 2, E8, HID1], F32R), sb("WD", [P, 2, E8, 2 * D], F32R)
        NS = sb("NS", [P, 2, TOK], F32R)
        T, LG = choice_tiles(sb, "m"), sb("LG", [P, NT_TILES, E8])
        ACC = [sb(f"ACC{i}", [P, TOK]) for i in range(2)]
        BT = sb("BT", [P, TOK])
        MT, SEL, SELF = sb("MT", [E8, TOK], BF16), sb("SEL", [E8, E8, P], BF16), sb("SELF", [E8, E8])
        loaded = sem("loaded")
        (lg_made, exp_wanted, exp_done, w_high, w_low, n_high, n_low, b_ready) = (sem(n) for n in (
            "lg_made", "exp_wanted", "exp_done", "w_high", "w_low", "n_high", "n_low", "b_ready"))

        def tokens_high(act, src):
            for g in range(G):
                gs = slice(GW * g, GW * g + GW)
                nc.scalar.activation(NS[:, 0, gs], src[:, gs], ACT.Copy).then_inc(n_high, 1)

        def tokens_low(pool, src, first):
            for g in range(G):
                gs = slice(GW * g, GW * g + GW)
                pool.wait_ge(n_high, first + g + 1)
                nc.gpsimd.tensor_tensor(NS[:, 1, gs], src[:, gs], NS[:, 0, gs].bitcast(F32), ALU.subtract)\
                    .then_inc(n_low, 1)

        with nc.Block() as block:
            @block.sync
            def _(sp):
                for dst, src in ((W1, w1_dram), (W2, w2_dram.rearrange("e p k d -> e p (k d)"))):
                    sp.dma_start(dst[:, :, :], src.rearrange("e p n -> p e n")).then_inc(loaded, 16)

            @block.tensor
            def _(pe):
                for t in range(NT_TILES):
                    last = nc.tensor.matmul(PS[0][:, E8 * t:E8 * t + E8], NTI[:, P * t:P * t + P], w("gw"),
                                            start=True, stop=True)
                last.then_inc(lg_made, 1)

            @block.scalar
            def _(act):
                tokens_high(act, NTI)
                act.wait_ge(exp_wanted, 1)
                nc.scalar.activation(T.PB[:, :, :], T.A[:, :, :], ACT.Exp).then_inc(exp_done, 1)
                act.wait_ge(loaded, 32)
                for raw, part in ((W1, WU), (W2, WD)):
                    nc.scalar.activation(part[:, 0, :, :], raw[:, :, :], ACT.Copy).then_inc(w_high, 1)

            @block.gpsimd
            def _(pool):
                tokens_low(pool, NTI, 0)
                for k, (raw, part) in enumerate(((W1, WU), (W2, WD))):
                    pool.wait_ge(w_high, k + 1)
                    nc.gpsimd.tensor_tensor(part[:, 1, :, :], raw[:, :, :], part[:, 0, :, :].bitcast(F32),
                                            ALU.subtract).then_inc(w_low, 1)

            @block.vector
            def _(v):
                expert_masks(c, v, SEL, SELF, E8)
                v.wait_ge(lg_made, 1)
                dve.link(v, nc.vector.tensor_tensor(LG[:, :, :],
                                                    PS[0][:, 0:NT_TILES * E8].rearrange("p (t e) -> p t e", e=E8),
                                                    rep(w("gb"), NT_TILES), ALU.add))
                softmax_top2(c, v, LG, T, (exp_wanted, exp_done))

        sums = [[sem(f"{n}{r}") for n in ("oh_turned", "oh_copied", "b_made", "b_copied")] for r in range(2)]
        start_sums(c, "m0", T.OH1, ACC[0], c.W2S[:, 0:D], MT, sums[0], False)
        expert_round(c, "m0", NS, WU, WD, MT, SEL, ACC[0])
        with nc.Block() as block:
            @block.vector
            def _(v):
                for g in range(G):
                    gs = slice(GW * g, GW * g + GW)
                    nc.vector.scalar_tensor_tensor(BT[:, gs], ACC[0][:, gs], 0.5, NTI[:, gs], ALU.mult, ALU.add)\
                        .then_inc(b_ready, 1)

            @block.scalar
            def _(act):
                act.wait_ge(b_ready, G)
                tokens_high(act, BT)

            @block.gpsimd
            def _(pool):
                tokens_low(pool, BT, G)
        start_sums(c, "m1", T.OH2, ACC[1], c.W2S[:, 0:D], MT, sums[1], False)
        expert_round(c, "m1", NS, WU, WD, MT, SEL, ACC[1])

        base, nv0 = c.n_front, c.n_var
        Y = BT[:, :].rearrange("p (t d) -> p t d", d=D)
        turned, y_ready = sem("turned"), sem("y_ready")
        with nc.Block() as block:
            @block.tensor
            def _(pe):
                for g in range(G):
                    for r in range(2):
                        i = 2 * g + r
                        if i >= 6:
                            pe.wait_ge(y_ready, i - 5)
                        for j in range(GT):
                            t = GT * g + j
                            last = nc.tensor.transpose(PS[i % 6][:, P * j:P * j + P], ACC[r][:, P * t:P * t + P],
                                                       w("ident"))
                        last.then_inc(turned, 1)
                for g in range(G):
                    transpose_xn(c, pe, base, g, PS[7])

            @block.scalar
            def _(act):
                act_tails(c, act, 3, base, c.NT[0], PS[7])

            @block.gpsimd
            def _(pool):
                pool_tails(c, pool, 3, nv0, base)

            @block.vector
            def _(v):

                def make(g):
                    for r, (m, src) in enumerate(((T.M1, c.XN), (T.M2, Y))):
                        v.wait_ge(turned, 2 * g + r + 1)
                        for j in range(GT):
                            t = GT * g + j
                            last = nc.vector.scalar_tensor_tensor(Y[:, t, :], PS[(2 * g + r) % 6][:, P * j:P * j + P],
                                                                  m[:, t:t + 1], src[:, t, :], ALU.mult, ALU.add)
                        last.then_inc(y_ready, 1)
                        v.wait_ge(y_ready, 2 * g + r + 1)
                    return Y[:, GT * g:GT * g + GT, :]

                def own(YG):
                    dve.link(v, nc.vector.tensor_tensor(YG, YG, rep(w("lng"), GT), ALU.mult))
                    dve.link(v, nc.vector.tensor_tensor(YG, YG, rep(w("lnb"), GT), ALU.add))
                tails(c, v, make, own)


def expert_round(c, tag, NS, WU, WD, MT, SEL, ACC):
    nc, w, PS = c.nc, c.w, c.PS
    n = E8 * G
    with ExitStack() as ctx:
        sb = lambda s, shape, d=F32: ctx.enter_context(nc.sbuf_tensor(tag + s, shape, d))
        sem = lambda s: ctx.enter_context(nc.semaphore(tag + s))
        HS = [sb(f"_HS{i}", [P, 2, 2, GW], F32R) for i in range(2)]
        HF = [sb(f"_HF{i}", [P, 2, GW]) for i in range(2)]
        MB = [sb(f"_MB{i}", [P, GW]) for i in range(2)]
        Z = sb("_Z", [P, GW])
        (h_made, high_ready, full0, full1, low_ready, mb_made, mb_ready, y_made, z_ready, summed) = (sem(s) for s in (
            "_h_made", "_high_ready", "_full0", "_full1", "_low_ready", "_mb_made", "_mb_ready", "_y_made", "_z_ready",
            "_summed"))
        with nc.Block() as block:
            @block.tensor
            def _(pe):
                for i in range(n + 1):
                    if i < n:
                        e, g = divmod(i, G)
                        gs = slice(GW * g, GW * g + GW)
                        if i >= 2:
                            pe.wait_ge(mb_ready, i - 1)
                        nc.tensor.matmul(PS[6 + i % 2][:, :], SEL[:, e, :], MT[:, gs], start=True, stop=True)\
                            .then_inc(mb_made, 1)
                        for k in range(2):
                            if i >= 2:
                                pe.wait_ge(high_ready, 2 * (i - 2) + k + 1)
                                pe.wait_ge((full0, full1)[k], i - 1)
                            for a, b in HL:
                                last = nc.tensor.matmul(PS[2 * (i % 2) + k][:, :], WU[:, a, e, P * k:P * k + P],
                                                        NS[:, b, gs], start=((a, b) == HL[0]), stop=((a, b) == HL[-1]))
                            last.then_inc(h_made, 1)
                    if i:
                        q = i - 1
                        e = q // G
                        pe.wait_ge(high_ready, 2 * q + 2)
                        pe.wait_ge(low_ready, 2 * q + 2)
                        if q >= 2:
                            pe.wait_ge(z_ready, q - 1)
                        for k in range(2):
                            for a, b in HL:
                                last = nc.tensor.matmul(PS[4 + q % 2][:, :], WD[:, b, e, D * k:D * k + D],
                                                        HS[q % 2][:, a, k, :], start=(k == 0 and (a, b) == HL[0]),
                                                        stop=(k == 1 and (a, b) == HL[-1]))
                        last.then_inc(y_made, 1)

            @block.scalar
            def _(act):
                for i in range(n):
                    e = i // G
                    act.wait_ge(mb_made, i + 1)
                    if i >= 2:
                        act.wait_ge(z_ready, i - 1)
                    nc.scalar.activation(MB[i % 2][:, :], PS[6 + i % 2][:, :], ACT.Copy).then_inc(mb_ready, 1)
                    if i >= 2:
                        act.wait_ge(y_made, i - 1)
                        act.wait_ge(low_ready, 2 * (i - 2) + 2)
                    for k in range(2):
                        act.wait_ge(h_made, 2 * i + k + 1)
                        bias = w("b1m", 2 * e + k, 1)
                        nc.scalar.activation(HS[i % 2][:, 0, k, :], PS[2 * (i % 2) + k][:, :], ACT.Relu, bias=bias)\
                            .then_inc(high_ready, 1)
                    nc.scalar.activation(HF[i % 2][:, 1, :], PS[2 * (i % 2) + 1][:, :], ACT.Relu, bias=bias)\
                        .then_inc(full1, 1)

            @block.gpsimd
            def _(pool):
                for i in range(n):
                    for k in range(2):
                        pool.wait_ge(high_ready, 2 * i + k + 1)
                        pool.wait_ge((full0, full1)[k], i + 1)
                        nc.gpsimd.tensor_tensor(HS[i % 2][:, 1, k, :], HF[i % 2][:, k, :],
                                                HS[i % 2][:, 0, k, :].bitcast(F32), ALU.subtract).then_inc(low_ready, 1)

            @block.vector
            def _(v):
                for i in range(n + 1):
                    if i < n:
                        e = i // G
                        v.wait_ge(high_ready, 2 * i + 1)
                        if i >= 2:
                            v.wait_ge(low_ready, 2 * (i - 2) + 1)
                        nc.vector.tensor_scalar(HF[i % 2][:, 0, :], PS[2 * (i % 2)][:, :], w("b1m", 2 * e, 1), 0.0,
                                                ALU.add, ALU.max).then_inc(full0, 1)
                    if i:
                        q = i - 1
                        gs = slice(GW * (q % G), GW * (q % G) + GW)
                        v.wait_ge(y_made, q + 1)
                        v.wait_ge(mb_ready, q + 1)
                        if q:
                            v.wait_ge(summed, q)
                        nc.vector.tensor_tensor(Z[:, :], PS[4 + q % 2][:, :], MB[q % 2][:, :], ALU.mult)\
                            .then_inc(z_ready, 1)
                        v.wait_ge(z_ready, q + 1)
                        nc.vector.tensor_tensor(ACC[:, gs], ACC[:, gs], Z[:, :], ALU.add).then_inc(summed, 1)


def l2_attn(c):
    nc, w, PS = c.nc, c.w, c.PS
    dve = c.dve
    NTI = c.NT[0]
    FMAX = float(np.finfo(np.float32).max)
    with ExitStack() as ctx:
        sb = lambda n, s, d=F32: ctx.enter_context(nc.sbuf_tensor(n, s, d))
        sem = lambda n: ctx.enter_context(nc.semaphore(n))
        OT = sb("r_OT", [P, TOK])
        with ExitStack() as ctx1:
            sb1 = lambda n, s, d=F32: ctx1.enter_context(nc.sbuf_tensor(n, s, d))
            sem1 = lambda n: ctx1.enter_context(nc.semaphore("r_" + n))
            NP = sb1("r_NP", [P, B, S + 1])
            WM = sb1("r_WM", [P, 3, 2, D])
            OM = sb1("r_OM", [P, 3])
            LA, EU, EW = sb1("r_LA", [P, 1]), sb1("r_EU", [P, 1]), sb1("r_EW", [P, 1])
            AP, RN = sb1("r_AP", [P, S]), sb1("r_RN", [P, S])
            ONE = sb1("r_ONE", [P, S])
            EK, EKV, SK, RR = (sb1("r_" + n, [P, TOK]) for n in ("EK", "EKV", "SK", "RR"))
            F_, CSUM = sb1("r_F", [P, S]), sb1("r_CS", [P, S + 1])
            ST, STN, MK, DEN = sb1("r_ST", [P, S]), sb1("r_STN", [P, S]), sb1("r_MK", [P, S], U32), sb1("r_DEN", [P, S])
            (np_ready, wm_ready, kvr_made, ek_ready, ekv_ready, er_ready, sk_made, sk_ready, td_ready, la_ready, ap_ready,
             const_ready) = (sem1(n) for n in (
                 "np_ready", "wm_ready", "kvr_made", "ek_ready", "ekv_ready", "er_ready", "sk_made", "sk_ready",
                 "td_ready", "la_ready", "ap_ready", "const_ready"))
            with nc.Block() as block:
                @block.tensor
                def _(pe):
                    mm = nc.tensor.matmul
                    pe.wait_ge(np_ready, 1)
                    pe.wait_ge(wm_ready, 1)
                    for g in range(G + 1):
                        if g < G:
                            b, at = g // 2, GW * (g % 2)
                            if g:
                                pe.wait_ge(ek_ready, g)
                                pe.wait_ge(ekv_ready, g)
                                pe.wait_ge(er_ready, g)
                            for k in range(3):
                                mm(PS[k][:, :], WM[:, k, 0, :], NP[:, b, 1 + at:1 + at + GW], start=True, stop=False)
                                mm(PS[k][:, :], WM[:, k, 1, :], NP[:, b, at:at + GW], start=False, stop=True)\
                                    .then_inc(kvr_made, 1)
                        if g:
                            q = g - 1
                            pe.wait_ge(ek_ready, q + 1)
                            if q >= 2:
                                pe.wait_ge(sk_ready, q - 1)
                            mm(PS[3 + q % 2][:, :], w("blocks"), EK[:, GW * q:GW * q + GW], start=True, stop=True)\
                                .then_inc(sk_made, 1)

                @block.scalar
                def _(act):
                    av = nc.scalar.activation
                    av(LA[:, :], w("td"), ACT.Exp)
                    av(EU[:, :], w("tf"), ACT.Exp).then_inc(td_ready, 1)
                    act.wait_ge(la_ready, 1)
                    av(EW[:, :], LA[:, :], ACT.Exp)
                    av(AP[:, :], w("time"), ACT.Exp, scale=LA[:, 0:1]).then_inc(ap_ready, 1)
                    for g in range(G):
                        gs = slice(GW * g, GW * g + GW)
                        act.wait_ge(kvr_made, 3 * g + 1)
                        av(EK[:, gs], PS[0][:, :], ACT.Exp).then_inc(ek_ready, 1)
                        act.wait_ge(kvr_made, 3 * g + 3)
                        av(RR[:, gs], PS[2][:, :], ACT.Exp, scale=-1.0).then_inc(er_ready, 1)
                        act.wait_ge(sk_made, g + 1)
                        av(SK[:, gs], PS[3 + g % 2][:, :], ACT.Copy).then_inc(sk_ready, 1)

                @block.gpsimd
                def _(pool):
                    nc.gpsimd.memset(ONE[:, :], 1.0)
                    nc.gpsimd.memset(CSUM[:, 0:1], 0.0).then_inc(const_ready, 1)
                    nc.gpsimd.memset(NP[:, :, 0:1], 0.0)
                    for b in range(B):
                        last = nc.gpsimd.tensor_copy(NP[:, b, 1:1 + S], NTI[:, S * b:S * b + S])
                    last.then_inc(np_ready, 1)

                @block.vector
                def _(v):
                    tt, ts, stt = nc.vector.tensor_tensor, nc.vector.tensor_scalar, nc.vector.scalar_tensor_tensor
                    dve.link(v, ts(OM[:, :], w("mk", 0, 3), -1.0, 1.0, ALU.mult, ALU.add))
                    for k, (m, wn) in enumerate((("mk", "wkey"), ("mv", "wval"), ("mr", "wrec"))):
                        ts(WM[:, k, 0, :], w(wn), w(m), None, ALU.mult)
                        last = ts(WM[:, k, 1, :], w(wn), OM[:, k:k + 1], None, ALU.mult)
                    last.then_inc(wm_ready, 1)
                    v.wait_ge(td_ready, 1)
                    ts(LA[:, :], LA[:, :], -1.0, None, ALU.mult).then_inc(la_ready, 1)
                    v.wait_ge(ap_ready, 1)
                    dve.link(v, ts(RN[:, :], AP[:, :], EW[:, 0:1], None, ALU.mult))
                    dve.link(v, nc.vector.reciprocal(RN[:, :], RN[:, :]))
                    for g in range(G):
                        gs = slice(GW * g, GW * g + GW)
                        v.wait_ge(kvr_made, 3 * g + 2)
                        v.wait_ge(ek_ready, g + 1)
                        tt(EKV[:, gs], PS[1][:, :], EK[:, gs], ALU.mult).then_inc(ekv_ready, 1)
                    v.wait_ge(ekv_ready, G)
                    v.wait_ge(er_ready, G)
                    v.wait_ge(sk_ready, G)
                    v.wait_ge(const_ready, 1)
                    for b in range(B):
                        bs = slice(S * b, S * b + S)
                        for src, state in ((EKV, "a"), (SK, "b")):
                            dve.link(v, tt(F_[:, :], src[:, bs], RN[:, :], ALU.mult))
                            dve.link(v, nc.vector.tensor_tensor_scan(CSUM[:, 1:1 + S], ONE[:, :], F_[:, :], 0.0,
                                                                     ALU.mult, ALU.add))
                            dve.link(v, tt(ST[:, :], AP[:, :], CSUM[:, 0:S], ALU.mult))
                            ts(MK[:, :], ST[:, :], FMAX, None, ALU.is_le)
                            ts(F_[:, :], ST[:, :], -FMAX, None, ALU.max)
                            dve.link(v, nc.vector.memset(STN[:, :], 0.0))
                            dve.link(v, nc.vector.copy_predicated(STN[:, :], MK[:, :], F_[:, :]))
                            if state == "a":
                                dve.link(v, stt(EKV[:, bs], EKV[:, bs], EU[:, 0:1], STN[:, :], ALU.mult, ALU.add))
                            else:
                                dve.link(v, stt(DEN[:, :], SK[:, bs], EU[:, 0:1], STN[:, :], ALU.mult, ALU.add))
                        dve.link(v, ts(DEN[:, :], DEN[:, :], 1e-6, None, ALU.max))
                        dve.link(v, ts(RR[:, bs], RR[:, bs], 1.0, None, ALU.add))
                        dve.link(v, nc.vector.reciprocal(DEN[:, :], DEN[:, :]))
                        dve.link(v, nc.vector.reciprocal(RR[:, bs], RR[:, bs]))
                        dve.link(v, tt(EKV[:, bs], EKV[:, bs], DEN[:, :], ALU.mult))
                        dve.link(v, tt(OT[:, bs], EKV[:, bs], RR[:, bs], ALU.mult))

        def products(pe, g, bank):
            for j in range(GT):
                t = GT * g + j
                last = nc.tensor.matmul(bank[:, P * j:P * j + P], OT[:, P * t:P * t + P], w("wo2"),
                                        start=True, stop=True)
            return last
        project_tail(c, "r1", products, None, c.NT[1])


def l2_ffn(c):
    nc, w, PS = c.nc, c.w, c.PS
    NTI = c.NT[1]
    KC = HID2 // P
    with ExitStack() as ctx:
        HT = ctx.enter_context(nc.sbuf_tensor("g_HT", [P, KC, TOK], F32))
        h_made, h_ready = ctx.enter_context(nc.semaphore("g_h_made")), ctx.enter_context(nc.semaphore("g_h_ready"))
        with nc.Block() as block:
            @block.tensor
            def _(pe):
                for i in range(G * KC):
                    g, k = divmod(i, KC)
                    if i >= 4:
                        pe.wait_ge(h_ready, i - 3)
                    nc.tensor.matmul(PS[i % 4][:, :], w("w1f", P * k, P), NTI[:, GW * g:GW * g + GW],
                                     start=True, stop=True).then_inc(h_made, 1)

            @block.scalar
            def _(act):
                for i in range(G * KC):
                    g, k = divmod(i, KC)
                    act.wait_ge(h_made, i + 1)
                    nc.scalar.activation(HT[:, k, GW * g:GW * g + GW], PS[i % 4][:, :], ACT.Relu,
                                         bias=w("b1f", k, 1)).then_inc(h_ready, 1)

        def products(pe, g, bank):
            for j in range(GT):
                t = GT * g + j
                for k in range(KC):
                    last = nc.tensor.matmul(bank[:, P * j:P * j + P], HT[:, k, P * t:P * t + P], w("w2f", D * k, D),
                                            start=(k == 0), stop=(k == KC - 1))
            return last
        project_tail(c, "g1", products, "b2f", c.NT[0])


def l3_attn(c):
    nc, w, PS = c.nc, c.w, c.PS
    dve = c.dve
    NH, HD = NH3, HD3
    M = D // HD
    R = S // M
    NTM = c.NT[0][:, :].rearrange("c (b r m) -> c m b r", b=B, m=M)
    OT = c.NT[0]
    with ExitStack() as ctx:
        sb = lambda n_, s, d=F32: ctx.enter_context(nc.sbuf_tensor("h_" + n_, s, d))
        sem = lambda n_: ctx.enter_context(nc.semaphore("h_" + n_))
        two = lambda n_, s: [sb(f"{n_}{i}", s) for i in range(2)]
        OUT = sb("OUT", [P, NH, M, HD])
        QKV, PR = two("QKV", [P, 3, NH, HD]), two("PR", [P, NH, NH, HD])
        SCR, E, PV = two("SCR", [P, NH, NH]), two("E", [P, NH, NH]), sb("PV", [P, NH, HD, NH])
        MX, SM = sb("MX", [P, NH]), sb("SM", [P, NH])
        (made, copied, prod_ready, prod_read, scr_ready, e_ready, e_read, done, turned, ot_copied) = (
            sem(n_) for n_ in ("made", "copied", "prod_ready", "prod_read", "scr_ready", "e_ready", "e_read", "done",
                               "turned", "ot_copied"))
        over = lambda a: a.unsqueeze(2).to_broadcast([P, NH, NH])
        with nc.Block() as block:
            @block.tensor
            def _(pe):
                for m in range(M):
                    if m >= 2:
                        pe.wait_ge(copied, m - 1)
                    nc.tensor.matmul(PS[m % 2][:, 0:3 * D], NTM[:, m, :, :], w("wq3", 0, 3 * D),
                                     start=True, stop=True).then_inc(made, 1)
                pe.wait_ge(done, M)
                for h in range(NH):
                    if h >= 4:
                        pe.wait_ge(ot_copied, h - 3)
                    nc.tensor.transpose(PS[2 + h % 4][:, 0:P], OUT[:, h, :, :].rearrange("p m d -> p (m d)"), w("ident"))\
                        .then_inc(turned, 1)

            @block.scalar
            def _(act):
                for m in range(M + 1):
                    if m < M:
                        act.wait_ge(made, m + 1)
                        if m >= 2:
                            act.wait_ge(prod_ready, m - 1)
                            act.wait_ge(done, m - 1)
                        nc.scalar.activation(QKV[m % 2][:, :, :, :].rearrange("p k h d -> p (k h d)"),
                                             PS[m % 2][:, 0:3 * D], ACT.Copy).then_inc(copied, 1)
                    if m:
                        q = m - 1
                        act.wait_ge(scr_ready, q + 1)
                        if q >= 2:
                            act.wait_ge(e_read, q - 1)
                        nc.scalar.activation(E[q % 2][:, :, :], SCR[q % 2][:, :, :], ACT.Exp, scale=HD ** -0.5)\
                            .then_inc(e_ready, 1)
                for h in range(NH):
                    act.wait_ge(turned, h + 1)
                    nc.scalar.activation(OT[:, :].rearrange("c (b x) -> c b x", b=B)[:, :, R * h:R * h + R],
                                         PS[2 + h % 4][:, 0:P].rearrange("c (b r) -> c b r", b=B), ACT.Copy)\
                        .then_inc(ot_copied, 1)

            @block.gpsimd
            def _(pool):
                for m in range(M):
                    s = m % 2
                    pool.wait_ge(copied, m + 1)
                    if m >= 2:
                        pool.wait_ge(prod_read, m - 1)
                    nc.gpsimd.tensor_tensor(PR[s][:, :, :, :],
                                            QKV[s][:, 0, :, :].unsqueeze(2).to_broadcast([P, NH, NH, HD]),
                                            QKV[s][:, 1, :, :].unsqueeze(1).to_broadcast([P, NH, NH, HD]), ALU.mult)\
                        .then_inc(prod_ready, 1)

            @block.vector
            def _(v):
                tt = nc.vector.tensor_tensor
                for m in range(M + 1):
                    if m < M:
                        s = m % 2
                        v.wait_ge(prod_ready, m + 1)
                        if m >= 2:
                            v.wait_ge(e_ready, m - 1)
                        nc.vector.reduce_sum(SCR[s][:, :, :], PR[s][:, :, :, :], axis=AX.X).then_inc(prod_read, 1)
                        v.wait_ge(prod_read, m + 1)
                        dve.link(v, nc.vector.reduce_max(MX[:, :], SCR[s][:, :, :], axis=AX.X))
                        tt(SCR[s][:, :, :], SCR[s][:, :, :], over(MX[:, :]), ALU.subtract).then_inc(scr_ready, 1)
                    if m:
                        q, s = m - 1, (m - 1) % 2
                        v.wait_ge(e_ready, q + 1)
                        if q:
                            v.wait_ge(done, q)
                        dve.link(v, nc.vector.reduce_sum(SM[:, :], E[s][:, :, :], axis=AX.X))
                        dve.link(v, tt(PV[:, :, :, :], E[s][:, :, :].unsqueeze(2).to_broadcast([P, NH, HD, NH]),
                                       QKV[s][:, 2, :, :].rearrange("p k d -> p d k").unsqueeze(1)
                                       .to_broadcast([P, NH, HD, NH]), ALU.mult))
                        nc.vector.reduce_sum(OUT[:, :, q, :], PV[:, :, :, :], axis=AX.X).then_inc(e_read, 1)
                        dve.link(v, nc.vector.reciprocal(SM[:, :], SM[:, :]))
                        v.wait_ge(e_read, q + 1)
                        tt(OUT[:, :, q, :], OUT[:, :, q, :], SM[:, :].unsqueeze(2).to_broadcast([P, NH, HD]),
                           ALU.mult).then_inc(done, 1)

        def products(pe, g, bank):
            for j in range(GT):
                t = GT * g + j
                last = nc.tensor.matmul(bank[:, P * j:P * j + P], OT[:, P * t:P * t + P], w("wo3"),
                                        start=True, stop=True)
            return last
        project_tail(c, "h1", products, "bo3", c.NT[1])


def l3_ffn(c, w1_dram, w2_dram):
    nc, w, PS = c.nc, c.w, c.PS
    dve = c.dve
    NTI = c.NT[1]
    KC = F3 // P
    n = E8 * G
    with ExitStack() as ctx:
        sb = lambda n_, s, d=F32: ctx.enter_context(nc.sbuf_tensor(n_, s, d))
        sem = lambda n_: ctx.enter_context(nc.semaphore("x_" + n_))
        W1, W2 = sb("x_W1", [P, 2, 2 * F3]), sb("x_W2", [P, 2, KC * D])
        WU = [sb(f"x_WU{i}", [P, 2, 2 * F3], F32R) for i in range(2)]
        WD = [sb(f"x_WD{i}", [P, 2, KC * D], F32R) for i in range(2)]
        NS = sb("x_NS", [P, 2, TOK], F32R)
        T, LG = choice_tiles(sb, "x"), sb("x_LG", [P, NT_TILES, E8])
        HR, HRT = sb("x_HR", [P, NT_TILES, KR]), c.NT[0][0:KR, :]
        ACC = c.XN[:, :, :].rearrange("p t d -> p (t d)")
        MROWS = 64 + E8
        MT, SEL, SELF = sb("x_MT", [MROWS, TOK], BF16), sb("x_SEL", [MROWS, E8, P], BF16), sb("x_SELF", [MROWS, E8])
        MB = [sb(f"x_MB{i}", [P, GW]) for i in range(2)]
        Z = [sb(f"x_Z{i}", [P, GW]) for i in range(2)]
        RST, RMV, RV, RRS = (sb("x_RST", [P, NT_TILES, 6]), sb("x_RMV", [P, NT_TILES, 2]),
                             sb("x_RV", [P, NT_TILES]), sb("x_RRS", [P, NT_TILES]))
        GE = [sb(f"x_GE{i}", [P, GW]) for i in range(4)]
        GF = [sb(f"x_GF{i}", [P, GW]) for i in range(4)]
        GS = [sb(f"x_GS{i}", [P, 2, KC, GW], F32R) for i in range(2)]
        loaded = [sem(f"loaded{e}") for e in range(E8)]
        w_high, w_low, n_high, n_low = sem("w_high"), sem("w_low"), sem("n_high"), sem("n_low")

        def load(sp, e):
            sp.dma_start(W1[:, e % 2, :], w1_dram[e]).then_inc(loaded[e], 16)
            sp.dma_start(W2[:, e % 2, :], w2_dram[e].rearrange("p k d -> p (k d)")).then_inc(loaded[e], 16)

        def weights_high(act, e):
            act.wait_ge(loaded[e], 32)
            for raw, part in ((W1, WU), (W2, WD)):
                nc.scalar.activation(part[e % 2][:, 0, :], raw[:, e % 2, :], ACT.Copy).then_inc(w_high, 1)

        def weights_low(eng, tensor_tensor, e):
            for k, (raw, part) in enumerate(((W1, WU), (W2, WD))):
                eng.wait_ge(w_high, 2 * e + k + 1)
                tensor_tensor(part[e % 2][:, 1, :], raw[:, e % 2, :], part[e % 2][:, 0, :].bitcast(F32),
                                        ALU.subtract).then_inc(w_low, 1)
        (r_made, rv_ready, rr_ready, hr_ready, gelu_ready, r_turned, r_copied, lg_made, exp_wanted, exp_done) = (
            sem(n_) for n_ in ("r_made", "rv_ready", "rr_ready", "hr_ready", "gelu_ready", "r_turned", "r_copied",
                               "lg_made", "exp_wanted", "exp_done"))
        with nc.Block() as block:
            @block.sync
            def _(sp):
                for e in range(2):
                    load(sp, e)

            @block.tensor
            def _(pe):
                for t in range(NT_TILES):
                    last = nc.tensor.matmul(PS[t // 8][:, KR * (t % 8):KR * (t % 8) + KR], NTI[:, P * t:P * t + P],
                                            w("wr1"), start=True, stop=True)
                last.then_inc(r_made, 1)
                pe.wait_ge(gelu_ready, 1)
                for g in range(G):
                    for j in range(GT):
                        last = nc.tensor.transpose(PS[2 + g][0:KR, P * j:P * j + P], HR[:, GT * g + j, :], w("ident"))
                    last.then_inc(r_turned, 1)
                pe.wait_ge(r_copied, G)
                for t in range(NT_TILES):
                    last = nc.tensor.matmul(PS[6][:, E8 * t:E8 * t + E8], HRT[:, P * t:P * t + P], w("wr2", rows=KR),
                                            start=True, stop=True)
                last.then_inc(lg_made, 1)

            @block.scalar
            def _(act):
                for g in range(G):
                    nc.scalar.activation(NS[:, 0, GW * g:GW * g + GW], NTI[:, GW * g:GW * g + GW], ACT.Copy)\
                        .then_inc(n_high, 1)
                act.wait_ge(hr_ready, 1)
                nc.scalar.activation(HR[:, :, :], HR[:, :, :], ACT.Gelu_apprx_tanh).then_inc(gelu_ready, 1)
                for g in range(G):
                    act.wait_ge(r_turned, g + 1)
                    nc.scalar.activation(HRT[:, GW * g:GW * g + GW], PS[2 + g][0:KR, :], ACT.Copy).then_inc(r_copied, 1)
                for e in range(2):
                    weights_high(act, e)
                act.wait_ge(exp_wanted, 1)
                nc.scalar.activation(T.PB[:, :, :], T.A[:, :, :], ACT.Exp).then_inc(exp_done, 1)

            @block.gpsimd
            def _(pool):
                pool.wait_ge(rv_ready, 1)
                nc.gpsimd.tensor_tensor(RRS[:, :], RV[:, :], c.MHALF[:, 0:NT_TILES], ALU.pow).then_inc(rr_ready, 1)
                for g in range(G):
                    gs = slice(GW * g, GW * g + GW)
                    pool.wait_ge(n_high, g + 1)
                    nc.gpsimd.tensor_tensor(NS[:, 1, gs], NTI[:, gs], NS[:, 0, gs].bitcast(F32), ALU.subtract)\
                        .then_inc(n_low, 1)
                for e in range(2):
                    weights_low(pool, nc.gpsimd.tensor_tensor, e)

            @block.vector
            def _(v):
                tt, ts = nc.vector.tensor_tensor, nc.vector.tensor_scalar
                v.wait_ge(r_made, 1)
                for k in range(2):
                    last = tt(HR[:, 8 * k:8 * k + 8, :], PS[k][:, :].rearrange("p (t r) -> p t r", r=KR),
                              rep(w("br1"), 8), ALU.add)
                dve.link(v, last)
                for t in range(NT_TILES):
                    last = nc.vector.bn_stats(RST[:, t, :], HR[:, t, :])
                dve.link(v, last)
                for t in range(NT_TILES):
                    last = nc.vector.bn_aggr(RMV[:, t, :], RST[:, t, :])
                dve.link(v, last)
                ts(RV[:, :], RMV[:, :, 1], 1e-6, None, ALU.add).then_inc(rv_ready, 1)
                v.wait_ge(rr_ready, 1)
                for t in range(NT_TILES):
                    last = ts(HR[:, t, :], HR[:, t, :], RMV[:, t, 0:1], RRS[:, t:t + 1], ALU.subtract, ALU.mult)
                dve.link(v, last)
                dve.link(v, tt(HR[:, :, :], HR[:, :, :], rep(w("lns"), NT_TILES), ALU.mult))
                tt(HR[:, :, :], HR[:, :, :], rep(w("lnbi"), NT_TILES), ALU.add).then_inc(hr_ready, 1)
                expert_masks(c, v, SEL, SELF, MROWS)
                v.wait_ge(lg_made, 1)
                dve.link(v, tt(LG[:, :, :], PS[6][:, 0:NT_TILES * E8].rearrange("p (t e) -> p t e", e=E8),
                               rep(w("br2"), NT_TILES), ALU.add))
                softmax_top2(c, v, LG, T, (exp_wanted, exp_done))
                bc = lambda a: a[:, :].unsqueeze(2).to_broadcast([P, NT_TILES, E8])
                dve.link(v, tt(T.MX[:, :], T.M1[:, :], T.M2[:, :], ALU.add))
                dve.link(v, nc.vector.reciprocal(T.MX[:, :], T.MX[:, :]))
                tt(T.OH1[:, :, :], T.OH1[:, :, :], bc(T.M1), ALU.mult)
                dve.link(v, tt(T.OH2[:, :, :], T.OH2[:, :, :], bc(T.M2), ALU.mult))
                dve.link(v, tt(LG[:, :, :], T.OH1[:, :, :], T.OH2[:, :, :], ALU.add))
                dve.link(v, tt(LG[:, :, :], LG[:, :, :], bc(T.MX), ALU.mult))

        start_sums(c, "x", LG, ACC, c.W2S[:, D:2 * D], MT,
                   [sem(n_) for n_ in ("oh_turned", "oh_copied", "b_made", "b_copied")], True)
        x_made, ge_ready, g_ready, gh_ready, gl_ready, y_made, z_ready, mb_made, mb_ready, summed = (
            sem(n_) for n_ in ("x_made", "ge_ready", "g_ready", "gh_ready", "gl_ready", "y_made", "z_ready", "mb_made",
                               "mb_ready", "summed"))
        XB = (0, 2, 6)
        with nc.Block() as block:
            @block.sync
            def _(sp):
                for e in range(2, E8):
                    sp.wait_ge(w_low, 2 * (e - 1))
                    load(sp, e)

            @block.tensor
            def _(pe):
                for i in range(n + 1):
                    if i < n:
                        e, g = divmod(i, G)
                        if g == 0:
                            pe.wait_ge(w_low, 2 * (e + 1))
                        if i:
                            pe.wait_ge(mb_ready, i)
                        nc.tensor.matmul(PS[5][:, :], SEL[:, e, :], MT[:, GW * g:GW * g + GW],
                                         start=True, stop=True).then_inc(mb_made, 1)
                        for k in range(KC):
                            q = KC * i + k
                            if q >= 3:
                                pe.wait_ge(g_ready, q - 2)
                            for half in range(2):
                                for a, b in HL:
                                    last = nc.tensor.matmul(PS[XB[q % 3] + half][:, :],
                                                            WU[e % 2][:, a, F3 * half + P * k:F3 * half + P * k + P],
                                                            NS[:, b, GW * g:GW * g + GW],
                                                            start=((a, b) == HL[0]), stop=((a, b) == HL[-1]))
                            last.then_inc(x_made, 1)
                    if i:
                        e = (i - 1) // G
                        pe.wait_ge(gh_ready, KC * i)
                        pe.wait_ge(gl_ready, KC * i)
                        if i >= 2:
                            pe.wait_ge(z_ready, i - 1)
                        for k in range(KC):
                            for a, b in HL:
                                last = nc.tensor.matmul(PS[4][:, :], WD[e % 2][:, b, D * k:D * k + D],
                                                        GS[(i - 1) % 2][:, a, k, :],
                                                        start=(k == 0 and (a, b) == HL[0]),
                                                        stop=(k == KC - 1 and (a, b) == HL[-1]))
                        last.then_inc(y_made, 1)

            @block.scalar
            def _(act):
                for q in range(KC * n + 1):
                    if q < KC * n and q % KC == 0:
                        i = q // KC
                        act.wait_ge(mb_made, i + 1)
                        if i >= 2:
                            act.wait_ge(z_ready, i - 1)
                        nc.scalar.activation(MB[i % 2][:, :], PS[5][:, :], ACT.Copy).then_inc(mb_ready, 1)
                    if q < KC * n:
                        e, k = q // (KC * G), q % KC
                        act.wait_ge(x_made, q + 1)
                        if q >= 4:
                            act.wait_ge(g_ready, q - 3)
                        nc.scalar.activation(GE[q % 4][:, :], PS[XB[q % 3] + 1][:, :], ACT.Gelu_apprx_tanh,
                                             bias=w("b1g", 8 * e + KC + k, 1)).then_inc(ge_ready, 1)
                    if q:
                        p = q - 1
                        i, k = divmod(p, KC)
                        act.wait_ge(g_ready, q)
                        if i >= 2 and k == 0:
                            act.wait_ge(y_made, i - 1)
                        nc.scalar.activation(GS[i % 2][:, 0, k, :], GF[p % 4][:, :], ACT.Copy).then_inc(gh_ready, 1)
                    if q % (KC * G) == 2 * KC and 2 <= q // (KC * G) + 1 < E8:
                        e = q // (KC * G) + 1
                        act.wait_ge(y_made, G * (e - 1))
                        weights_high(act, e)

            @block.gpsimd
            def _(pool):
                def add(i):
                    gs = slice(GW * (i % G), GW * (i % G) + GW)
                    pool.wait_ge(z_ready, i + 1)
                    if i >= G:
                        pool.wait_ge(summed, i - G + 1)
                    nc.gpsimd.tensor_tensor(ACC[:, gs], ACC[:, gs], Z[i % 2][:, :], ALU.add).then_inc(summed, 1)

                for p in range(KC * n):
                    i, k = divmod(p, KC)
                    if i >= 2 and k == 2:
                        add(i - 2)
                    pool.wait_ge(gh_ready, p + 1)
                    nc.gpsimd.tensor_tensor(GS[i % 2][:, 1, k, :], GF[p % 4][:, :], GS[i % 2][:, 0, k, :].bitcast(F32),
                                            ALU.subtract).then_inc(gl_ready, 1)
                add(n - 2)
                add(n - 1)

            @block.vector
            def _(v):
                for i in range(n + 1):
                    if i < n:
                        e = i // G
                        for k in range(KC):
                            q = KC * i + k
                            v.wait_ge(ge_ready, q + 1)
                            if q >= 4:
                                v.wait_ge(gh_ready, q - 3)
                                v.wait_ge(gl_ready, q - 3)
                            nc.vector.scalar_tensor_tensor(GF[q % 4][:, :], PS[XB[q % 3]][:, :],
                                                           w("b1g", 8 * e + k, 1), GE[q % 4][:, :],
                                                           ALU.add, ALU.mult).then_inc(g_ready, 1)
                    if i:
                        v.wait_ge(y_made, i)
                        v.wait_ge(mb_ready, i)
                        if i >= 3:
                            v.wait_ge(summed, i - 2)
                        nc.vector.tensor_tensor(Z[(i - 1) % 2][:, :], PS[4][:, :], MB[(i - 1) % 2][:, :], ALU.mult)\
                            .then_inc(z_ready, 1)
                    if i % G == 2 and 2 <= i // G + 1 < E8:
                        weights_low(v, nc.vector.tensor_tensor, i // G + 1)

        nv0 = c.n_var
        acc_turned, acc_copied, x_final = sem("acc_turned"), sem("acc_copied"), sem("x_final")
        YF = W1[:, :, :].rearrange("p a (t d) -> p (a t) d", d=D)
        with nc.Block() as block:
            @block.sync
            def _(sp):
                for g in range(G):
                    sp.wait_ge(x_final, g + 1)
                    sp.dma_start(c.out[GT * g:GT * g + GT].rearrange("t p d -> p t d"),
                                 c.X[:, GT * g:GT * g + GT, :]).then_inc(c.out_stored, 16)
                sp.wait_ge(c.out_stored, 16 * G)

            @block.tensor
            def _(pe):
                for g in range(G):
                    for j in range(GT):
                        t = GT * g + j
                        last = nc.tensor.transpose(PS[g][:, P * j:P * j + P], ACC[:, P * t:P * t + P], w("ident"))
                    last.then_inc(acc_turned, 1)

            @block.scalar
            def _(act):
                for g in range(G):
                    act.wait_ge(acc_turned, g + 1)
                    nc.scalar.activation(YF[:, GT * g:GT * g + GT, :],
                                         PS[g][:, :].rearrange("p (t d) -> p t d", d=D), ACT.Copy)\
                        .then_inc(acc_copied, 1)

            @block.gpsimd
            def _(pool):
                pool_tails(c, pool, 2, nv0, c.n_front, finish=True)

            @block.vector
            def _(v):
                def make(g):
                    v.wait_ge(acc_copied, g + 1)
                    return YF[:, GT * g:GT * g + GT, :]
                tails(c, v, make, finish=lambda g: v.sem_inc(x_final, 1))


def kernel(**inputs):
    import numpy as np
    import concourse.bacc as bacc
    from concourse.bass_utils import run_bass_kernel_spmd as run

    nc = bacc.Bacc("TRN2", target_bir_lowering=False, num_devices=1)
    arrays = host_layout(inputs)
    args = {}
    for name, a in arrays.items():
        args[name] = nc.dram_tensor(f"in_{name}", a.shape, mybir.dt.from_np(a.dtype), kind="ExternalInput").ap()
    out = nc.dram_tensor("out", (NT_TILES, P, D), F32, kind="ExternalOutput").ap()
    program(nc, args["x"], args["pack"], args["b2s"], args["l1w1"], args["l1w2"], args["l3w1"], args["l3w2"],
            out)
    r = run(nc, [{f"in_{k}": a for k, a in arrays.items()}], core_ids=[0])
    return r.results[0]["out"].reshape(B, S, D)


def host_layout(i):
    f = np.float32
    i = {k: np.asarray(a) for k, a in i.items()}
    rows = lambda a: np.broadcast_to(a.reshape(1, -1), (P, a.size))
    ar = np.arange(P)
    angle = 2 * np.pi * (np.outer(ar, ar) % P) / P
    chan = lambda a: np.repeat(a, D // a.size).reshape(P, 1)
    win = i["L1_attn_W_in"]
    bc = win[:, 512:1024].reshape(D, 2, H1, 32, 2).transpose(0, 1, 2, 4, 3).reshape(D, 512)
    cols = {
        "ident": np.eye(P), "ones": np.ones((P, P)),
        "wq0": i["L0_attn_w_qkv"][0:128].T, "wk0": i["L0_attn_w_qkv"][128:256].T,
        "wv0": i["L0_attn_w_qkv"][256:384].T, "wfc": i["L0_attn_w_fc"].T,
        "bfc": rows(i["L0_attn_b_fc"]), "gam0": rows(i["L0_attn_gamma"]), "bet0": rows(i["L0_attn_beta"]),
        "wr": i["L0_ffn_w_freq_real"], "wi": i["L0_ffn_w_freq_imag"],
        "cos": np.cos(angle), "sin": np.sin(angle), "nsin": -np.sin(angle), "fbias": rows(i["L0_ffn_bias"]),
        "win": np.concatenate([win[:, 0:512], bc, win[:, 1024:]], 1),
        "nw": i["L1_attn_norm_weight"].reshape(2, P).T,
        "wout": i["L1_attn_W_out"].reshape(2, P, D).transpose(1, 0, 2).reshape(P, 2 * D),
        "dtb": rows(i["L1_attn_dt_bias"]), "alog": rows(i["L1_attn_A_log"]),
        "freq": rows((1.0 / 10000.0 ** (np.arange(32, dtype=f) / f(32))).astype(f)),
        "upper": (ar[:, None] <= ar[None, :]), "below": (ar[:, None] > ar[None, :]),
        "shift": (ar[:, None] == ar[None, :] + 1), "first": (ar[:, None] == 0) & (ar[None, :] == P - 1),
        "mask": np.where(ar[:, None] > ar[None, :], f(-30000.0), f(0.0)),
        "gw": i["L1_ffn_gate_W"], "gb": rows(i["L1_ffn_gate_b"]), "rank": rows(E8 - np.arange(E8, dtype=f)),
        "b1m": i["L1_ffn_b1"].reshape(E8, 2, P).transpose(2, 0, 1).reshape(P, 16),
        "lng": rows(i["L1_ffn_ln_gamma"]), "lnb": rows(i["L1_ffn_ln_beta"]),
        "mk": chan(i["L2_attn_mix_k"]), "mv": chan(i["L2_attn_mix_v"]), "mr": chan(i["L2_attn_mix_r"]),
        "wkey": i["L2_attn_W_key"].T, "wval": i["L2_attn_W_value"].T, "wrec": i["L2_attn_W_receptance"].T,
        "wo2": i["L2_attn_W_output"].T, "td": chan(i["L2_attn_time_decay"]), "tf": chan(i["L2_attn_time_first"]),
        "blocks": (ar[:, None] // 8 == ar[None, :] // 8), "time": rows(np.arange(S, dtype=f)),
        "w1f": i["L2_ffn_W1"], "b1f": i["L2_ffn_b1"].reshape(4, P).T,
        "w2f": i["L2_ffn_W2"].reshape(4, P, D).transpose(1, 0, 2).reshape(P, 4 * D), "b2f": rows(i["L2_ffn_b2"]),
        "wq3": i["L3_attn_Wq"].T, "wk3": i["L3_attn_Wk"].T, "wv3": i["L3_attn_Wv"].T, "wo3": i["L3_attn_Wo"].T,
        "bo3": rows(i["L3_attn_bo"]),
        "wr1": i["L3_ffn_Wr1"], "br1": rows(i["L3_ffn_br1"]), "lns": rows(i["L3_ffn_ln_scale"]),
        "lnbi": rows(i["L3_ffn_ln_bias"]),
        "wr2": np.concatenate([i["L3_ffn_Wr2"], i["L3_ffn_Wr2"]], 0), "br2": rows(i["L3_ffn_br2"]),
        "b1g": i["L3_ffn_b1"].reshape(E8, 8, P).transpose(2, 0, 1).reshape(P, 64),
    }
    pack = np.concatenate([np.asarray(cols[k]).astype(f).reshape(P, wd) for k, (_, wd) in PACK.items()], 1)
    return {
        "x": np.ascontiguousarray(i["L0_attn_x"].reshape(NT_TILES, P, D)),
        "pack": np.ascontiguousarray(pack),
        "b2s": np.ascontiguousarray(np.concatenate([i["L1_ffn_b2"], i["L3_ffn_b2"]], 1)),
        "l1w1": np.ascontiguousarray(i["L1_ffn_W1"]),
        "l1w2": np.ascontiguousarray(i["L1_ffn_W2"].reshape(E8, 2, P, D).transpose(0, 2, 1, 3)),
        "l3w1": np.ascontiguousarray(i["L3_ffn_W1"]),
        "l3w2": np.ascontiguousarray(i["L3_ffn_W2"].reshape(E8, 4, P, D).transpose(0, 2, 1, 3)),
    }
```

```python
import concourse.bass as bass
from concourse import mybir
from contextlib import ExitStack
import numpy as np

F32 = mybir.dt.float32
F32R = mybir.dt.float32r
BF16 = mybir.dt.bfloat16
U32 = mybir.dt.uint32
ALU = mybir.AluOpType
ACT = mybir.ActivationFunctionType
AX = mybir.AxisListType

B, S, D = 2, 1024, 128
P = 128
NT_TILES = B * S // P
TPB = S // P
GT = 4
G = NT_TILES // GT
GW = GT * P
TOK = B * S


def columns(widths):
    at, out = 0, {}
    for name, w in widths:
        out[name] = (at, w)
        at += w
    return out, at


H1, N1, P1 = 4, 64, 64
E8 = 8
HID1 = 256
HID2 = 512
F3 = 512
KR = 64
NH3, HD3 = 16, 8

PACK, PACK_W = columns([
    ("ident", 128), ("ones", 128),
    ("wq0", 128), ("wk0", 128), ("wv0", 128), ("wfc", 128), ("bfc", 128), ("gam0", 128), ("bet0", 128),
    ("wr", 128), ("wi", 128), ("cos", 128), ("sin", 128), ("nsin", 128), ("fbias", 128),
    ("win", 1028), ("nw", 2), ("wout", 256), ("dtb", H1), ("alog", H1), ("freq", 32),
    ("upper", 128), ("below", 128), ("shift", 128), ("first", 128), ("mask", 128),
    ("gw", E8), ("gb", E8), ("rank", E8), ("b1m", 16), ("lng", 128), ("lnb", 128),
    ("mk", 1), ("mv", 1), ("mr", 1), ("wkey", 128), ("wval", 128), ("wrec", 128), ("wo2", 128),
    ("td", 1), ("tf", 1), ("blocks", 128), ("time", 1024),
    ("w1f", HID2), ("b1f", 4), ("w2f", 4 * 128), ("b2f", 128),
    ("wq3", 128), ("wk3", 128), ("wv3", 128), ("wo3", 128), ("bo3", 128),
    ("wr1", KR), ("br1", KR), ("lns", KR), ("lnbi", KR), ("wr2", E8), ("br2", E8), ("b1g", 64),
])
FIRST_W = PACK["wr"][0]


def program(nc, x_in, pack, b2s, l1w1, l1w2, l3w1, l3w2, out):
    ctx = ExitStack()
    with ctx:
        sb = lambda n, s, d=F32: ctx.enter_context(nc.sbuf_tensor(n, s, d))
        sem = lambda n: ctx.enter_context(nc.semaphore(n))
        X = sb("X", [P, NT_TILES, D])
        XN = sb("XN", [P, NT_TILES, D])
        NT = [sb(f"NT{i}", [P, TOK]) for i in range(2)]
        W = sb("W", [P, PACK_W])
        W2S = sb("W2S", [E8, 2 * D])
        STAT = sb("STAT", [P, GT, 6])
        MV = sb("MV", [P, 6, GT, 2])
        VPE = sb("VPE", [P, 6, GT])
        RSTD = sb("RSTD", [P, 6, GT])
        NM, NMR = sb("NM", [P, 6, GT]), sb("NMR", [P, 6, GT])
        MHALF = sb("MHALF", [P, 64])
        PS = [ctx.enter_context(nc.psum_tensor(f"PS{i}", [P, 512], F32)) for i in range(8)]

        def w(name, a=0, n=None, rows=P):
            at, width = PACK[name]
            return W[0:rows, at + a:at + a + (width - a if n is None else n)]

        c = Common()
        c.nc, c.X, c.XN, c.NT, c.w, c.PS, c.W2S = nc, X, XN, NT, w, PS, W2S
        c.STAT, c.MV, c.VPE, c.RSTD, c.MHALF, c.NM, c.NMR = STAT, MV, VPE, RSTD, MHALF, NM, NMR
        c.nmr_ready, c.y_normed = sem("nmr_ready"), sem("y_normed")
        c.n_normed = 0
        c.out = out
        c.var_ready, c.rstd_ready = sem("var_ready"), sem("rstd_ready")
        c.xs_ready, c.xs_transposed, c.nt_ready = sem("xs_ready"), sem("xs_transposed"), sem("nt_ready")
        c.out_stored = sem("out_stored")
        c.rest_loaded = sem("rest_loaded")
        c.dve = Chain(sem("dve_steps"))
        c.n_var, c.n_front = 0, 0
        loads(c, x_in, pack, b2s)
        l0_attn(c)
        l0_ffn(c)
        l1_attn(c)
        l1_ffn(c, l1w1, l1w2)
        l2_attn(c)
        l2_ffn(c)
        l3_attn(c)
        l3_ffn(c, l3w1, l3w2)


class Common:
    pass


def cleared(nc, name, used):
    s = nc.alloc_semaphore(name)
    used.append(s)
    return s


class Chain:

    def __init__(self, sem):
        self.sem, self.n = sem, 0

    def link(self, eng, ins):
        self.n += 1
        ins.then_inc(self.sem, 1)
        eng.wait_ge(self.sem, self.n)


def schedule(phases):
    return [(step - p, p) for step in range(G + phases - 1) for p in range(phases) if 0 <= step - p < G]


def slot(phase, g):
    return 2 * phase + g % 2


def statistics(c, v, tiles, sl, eps=1e-5):
    nc = c.nc
    for j in range(GT):
        last = nc.vector.bn_stats(c.STAT[:, j, :], tiles[:, j, :])
    c.dve.link(v, last)
    for j in range(GT):
        last = nc.vector.bn_aggr(c.MV[:, sl, j, :], c.STAT[:, j, :])
    c.dve.link(v, last)
    c.dve.link(v, nc.vector.tensor_scalar(c.NM[:, sl, :], c.MV[:, sl, :, 0], -1.0, None, ALU.mult))
    nc.vector.tensor_scalar(c.VPE[:, sl, :], c.MV[:, sl, :, 1], eps, None, ALU.add).then_inc(c.var_ready, 1)


def tails(c, v, make, between=None, finish=None):
    phases = 3 if between else 2
    base = c.n_front
    requests = [gp for gp in schedule(phases) if not (finish and gp[1] == phases - 1)]
    inner = [gp for gp in requests if gp[1] < phases - 1]
    number = {gp: c.n_normed + k + 1 for k, gp in enumerate(inner)}
    made = {}
    for g, p in schedule(phases):
        if p:
            v.wait_ge(c.y_normed, number[g, p - 1])
        if p == 0:
            source = made[g] = make(g)
        elif p < phases - 1:
            source = made[g]
            between(source)
        else:
            source = c.X[:, GT * g:GT * g + GT, :]
            c.dve.link(v, c.nc.vector.tensor_tensor(source, source, made[g], ALU.add))
            if finish:
                finish(g)
                continue
            if g >= 2:
                v.wait_ge(c.xs_ready, base + g - 1)
        statistics(c, v, source, slot(p, g))
    c.n_var += len(requests)
    c.n_normed += len(inner)
    if not finish:
        c.n_front += G


def pool_tails(c, pool, phases, nv0, base, finish=False):
    n = nv0
    for g, p in schedule(phases):
        if p == phases - 1 and finish:
            continue
        n += 1
        sl = slot(p, g)
        pool.wait_ge(c.var_ready, n)
        c.nc.gpsimd.tensor_tensor(c.RSTD[:, sl, :], c.VPE[:, sl, :], c.MHALF[:, 0:GT], ALU.pow).then_inc(c.rstd_ready, 1)
        pool.wait_ge(c.rstd_ready, n)
        c.nc.gpsimd.tensor_tensor(c.NMR[:, sl, :], c.NM[:, sl, :], c.RSTD[:, sl, :], ALU.mult).then_inc(c.nmr_ready, 1)


def act_tails(c, act, phases, nv0, base, made=None, nt=None, bank=None):
    def copy_nt(g):
        act.wait_ge(c.xs_transposed, base + g + 1)
        c.nc.scalar.activation(nt[:, GW * g:GW * g + GW], bank[:, :], ACT.Copy).then_inc(c.nt_ready, 1)

    n = nv0
    for g, p in schedule(phases):
        last, gs, sl = p == phases - 1, slice(GT * g, GT * g + GT), slot(p, g)
        if last and nt is None:
            continue
        n += 1
        src, dst, done = (c.X[:, gs, :], c.XN[:, gs, :], c.xs_ready) if last else (made(g), made(g), c.y_normed)
        act.wait_ge(c.nmr_ready, n)
        for j in range(GT):
            ins = c.nc.scalar.activation(dst[:, j, :], src[:, j, :], ACT.Identity, bias=c.NMR[:, sl, j:j + 1],
                                         scale=c.RSTD[:, sl, j:j + 1])
        ins.then_inc(done, 1)
        if last and g:
            copy_nt(g - 1)
    if nt is not None:
        copy_nt(G - 1)


def transpose_xn(c, pe, base, g, bank):
    pe.wait_ge(c.xs_ready, base + g + 1)
    if base + g:
        pe.wait_ge(c.nt_ready, base + g)
    for j in range(GT):
        last = c.nc.tensor.transpose(bank[:, P * j:P * j + P], c.XN[:, GT * g + j, :], c.w("ident"))
    last.then_inc(c.xs_transposed, 1)


def loads(c, x_in, pack, b2s):
    nc = c.nc
    with ExitStack() as ctx:
        x_loaded = [ctx.enter_context(nc.semaphore(f"x_loaded{g}")) for g in range(G)]
        w_loaded = ctx.enter_context(nc.semaphore("w_loaded"))
        const_ready = ctx.enter_context(nc.semaphore("const_ready"))
        with nc.Block() as block:
            @block.sync
            def _(sp):
                for g in range(G):
                    sp.dma_start(c.X[:, GT * g:GT * g + GT, :],
                                 x_in[GT * g:GT * g + GT].rearrange("t p d -> p t d")).then_inc(x_loaded[g], 16)
                sp.dma_start(c.W2S[:, :], b2s).then_inc(c.rest_loaded, 16)

            @block.scalar
            def _(act):
                act.dma_start(c.w("ident", 0, FIRST_W), pack[:, 0:FIRST_W]).then_inc(w_loaded, 16)
                act.dma_start(c.w("wr", 0, PACK_W - FIRST_W), pack[:, FIRST_W:PACK_W]).then_inc(c.rest_loaded, 16)
                act_tails(c, act, 1, 0, 0, None, c.NT[0], c.PS[7])

            @block.tensor
            def _(pe):
                pe.wait_ge(w_loaded, 16)
                for g in range(G):
                    transpose_xn(c, pe, 0, g, c.PS[7])

            @block.gpsimd
            def _(pool):
                nc.gpsimd.memset(c.MHALF[:, :], -0.5).then_inc(const_ready, 1)
                pool.wait_ge(const_ready, 1)
                pool_tails(c, pool, 1, 0, 0)

            @block.vector
            def _(v):
                for g in range(G):
                    v.wait_ge(x_loaded[g], 16)
                    if g >= 2:
                        v.wait_ge(c.xs_ready, g - 1)
                    statistics(c, v, c.X[:, GT * g:GT * g + GT, :], slot(0, g))
                c.n_var, c.n_front = G, G


def l0_attn(c):
    nc, w, PS = c.nc, c.w, c.PS
    SCALE = D ** -0.5
    base = c.n_front
    nv0 = c.n_var
    with ExitStack() as ctx:
        sb = lambda n, s, d=F32: ctx.enter_context(nc.sbuf_tensor(n, s, d))
        sem = lambda n: ctx.enter_context(nc.semaphore(n))
        KT, QT = sb("a0_KT", [P, TOK]), sb("a0_QT", [P, TOK])
        MX, NB, L, AS = sb("a0_MX", [P, 16, 2]), sb("a0_NB", [P, 16]), sb("a0_L", [P, 16]), sb("a0_AS", [P, 16])
        MXC, LH = sb("a0_MXC", [P, 16]), sb("a0_LH", [P, 16, 2])
        NSUM, VS, VB, FB = sb("a0_NS", [P, B]), sb("a0_VS", [P, B]), sb("a0_VB", [P, B, D]), sb("a0_FB", [P, B, D])
        Y = sb("a0_Y", [P, 3, GT, D])
        EJ = sb("a0_E", [P, S])
        SB = (0, 4, 2)
        qk_done, qk_copied = sem("qk_done"), sem("qk_copied")
        l_half = sem("l_half")
        scores_ready, bias_ready, exp_done = sem("scores_ready"), sem("bias_ready"), sem("exp_done")
        nsum_ready, v_ready, vb_ready, f_ready = (
            sem("nsum_ready"), sem("v_ready"), sem("vb_ready"), sem("f_ready"))
        dve = c.dve
        with nc.Block() as block:
            @block.sync
            def _(sp):
                sp.wait_ge(c.rest_loaded, 32)

            @block.tensor
            def _(pe):
                for g in range(G):
                    if g >= 2:
                        pe.wait_ge(qk_copied, 2 * (g - 1))
                    for j, name in enumerate(("wq0", "wk0")):
                        nc.tensor.matmul(PS[4 * (g % 2) + j][:, :], w(name), c.NT[0][:, GW * g:GW * g + GW],
                                         start=True, stop=True).then_inc(qk_done, 1)
                pe.wait_ge(nsum_ready, 1)
                nc.tensor.matmul(PS[2][:, 0:B], w("wv0"), NSUM[:, :], start=True, stop=True).then_inc(v_ready, 1)
                pe.wait_ge(vb_ready, 1)
                for b in range(B):
                    last = nc.tensor.matmul(PS[3][:, b * D:b * D + D], VB[:, b, :], w("wfc"), start=True, stop=True)
                last.then_inc(f_ready, 1)
                pe.wait_ge(qk_copied, 2 * G)
                for t in range(NT_TILES):
                    b = t // TPB
                    if t >= 3:
                        pe.wait_ge(exp_done, t - 2)
                    elif t == 2:
                        pe.wait_ge(bias_ready, 1)
                    for half in range(2):
                        last = nc.tensor.matmul(PS[SB[t % 3] + half][:, :], QT[:, P * t:P * t + P],
                                                KT[:, S * b + 512 * half:S * b + 512 * half + 512],
                                                start=True, stop=True)
                    last.then_inc(scores_ready, 1)
                for g in range(G):
                    transpose_xn(c, pe, base, g, PS[7])

            @block.scalar
            def _(act):
                for g in range(G):
                    for j, dst in enumerate((QT, KT)):
                        act.wait_ge(qk_done, 2 * g + j + 1)
                        nc.scalar.activation(dst[:, GW * g:GW * g + GW], PS[4 * (g % 2) + j][:, :], ACT.Copy)\
                            .then_inc(qk_copied, 1)
                for t in range(NT_TILES):
                    act.wait_ge(bias_ready, t + 1)
                    if t >= 1:
                        act.wait_ge(exp_done, t)
                    for half in range(2):
                        k = SB[t % 3] + half
                        if half:
                            act.wait_ge(l_half, t + 1)
                        ins = nc.scalar.activation(EJ[:, 512 * half:512 * half + 512], PS[k][:, :], ACT.Exp,
                                                   bias=NB[:, t:t + 1], scale=SCALE,
                                                   accum_out=LH[:, t, half:half + 1])
                        ins.then_inc(exp_done if half else l_half, 1)
                act_tails(c, act, 3, nv0, base, lambda g: Y[:, g % 3, :, :], c.NT[1], PS[7])

            @block.gpsimd
            def _(pool):
                pool_tails(c, pool, 3, nv0, base)

            @block.vector
            def _(v):
                for b in range(B):
                    last = nc.vector.reduce_sum(NSUM[:, b:b + 1], c.NT[0][:, S * b:S * b + S], axis=AX.X)
                last.then_inc(nsum_ready, 1)
                v.wait_ge(v_ready, 1)
                dve.link(v, nc.vector.tensor_copy(VS[:, :], PS[2][:, 0:B]))
                nc.vector.tensor_copy(VB[:, :, :], VS[:, :].unsqueeze(2).to_broadcast([P, B, D])).then_inc(vb_ready, 1)
                v.wait_ge(f_ready, 1)
                dve.link(v, nc.vector.tensor_copy(FB[:, :, :], PS[3][:, 0:B * D].rearrange("p (b d) -> p b d", b=B)))
                for t in range(NT_TILES):
                    v.wait_ge(scores_ready, t + 1)
                    for half in range(2):
                        last = nc.vector.reduce_max(MX[:, t, half:half + 1], PS[SB[t % 3] + half][:, :], axis=AX.X)
                    dve.link(v, last)
                    dve.link(v, nc.vector.reduce_max(MXC[:, t:t + 1], MX[:, t, :], axis=AX.X))
                    nc.vector.tensor_scalar(NB[:, t:t + 1], MXC[:, t:t + 1], -SCALE, None, ALU.mult).then_inc(bias_ready, 1)
                v.wait_ge(exp_done, NT_TILES)
                dve.link(v, nc.vector.reduce_sum(L[:, :], LH[:, :, :], axis=AX.X))
                dve.link(v, nc.vector.reciprocal(AS[:, :], L[:, :]))
                dve.link(v, nc.vector.tensor_tensor(AS[:, :], AS[:, :], L[:, :], ALU.mult))

                def make(g):
                    b = g // 2
                    YG = Y[:, g % 3, :, :]
                    dve.link(v, nc.vector.tensor_tensor(YG, c.XN[:, GT * g:GT * g + GT, :], rep(w("bfc"), GT), ALU.add))
                    for j in range(GT):
                        t = GT * g + j
                        last = nc.vector.scalar_tensor_tensor(YG[:, j, :], FB[:, b, :], AS[:, t:t + 1], YG[:, j, :],
                                                              ALU.mult, ALU.add)
                    dve.link(v, last)
                    return YG

                def own(YG):
                    dve.link(v, nc.vector.tensor_tensor(YG, YG, rep(w("gam0"), GT), ALU.mult))
                    dve.link(v, nc.vector.tensor_tensor(YG, YG, rep(w("bet0"), GT), ALU.add))
                tails(c, v, make, own)


def rep(ap, n):
    return ap.unsqueeze(1).to_broadcast([ap.shape[0], n, ap.shape[1]])


def project_tail(c, name, products, bias, nt_out, scale=None):
    nc, w, PS = c.nc, c.w, c.PS
    base, nv0 = c.n_front, c.n_var
    with ExitStack() as ctx:
        Y = ctx.enter_context(nc.sbuf_tensor(name + "_Y", [P, 2, GT, D], F32))
        y_made = ctx.enter_context(nc.semaphore(name + "_y_made"))
        y_read = ctx.enter_context(nc.semaphore(name + "_y_read"))
        in_bank = lambda g: PS[g][:, :].rearrange("p (t d) -> p t d", t=GT)
        made = in_bank if not bias and scale is None else lambda g: Y[:, g % 2, :, :]
        with nc.Block() as block:
            @block.tensor
            def _(pe):
                for g in range(G + 2):
                    if g < G:
                        products(pe, g, PS[g]).then_inc(y_made, 1)
                    if g >= 2:
                        transpose_xn(c, pe, base, g - 2, PS[7])

            @block.scalar
            def _(act):
                act_tails(c, act, 2, nv0, base, made, nt_out, PS[7])

            @block.gpsimd
            def _(pool):
                pool_tails(c, pool, 2, nv0, base)

            @block.vector
            def _(v):
                def make(g):
                    v.wait_ge(y_made, g + 1)
                    if not bias and scale is None:
                        return made(g)
                    out, YG = in_bank(g), made(g)
                    if bias:
                        ins = nc.vector.tensor_tensor(YG, out, rep(w(bias), GT), ALU.add)
                    else:
                        ins = nc.vector.tensor_tensor(YG, out, scale[:, GT * g:GT * g + GT].unsqueeze(2)
                                                      .to_broadcast([P, GT, D]), ALU.mult)
                    ins.then_inc(y_read, 1)
                    v.wait_ge(y_read, g + 1)
                    return YG
                tails(c, v, make)


def l0_ffn(c):
    nc, w, PS = c.nc, c.w, c.PS
    with ExitStack() as ctx:
        sb = lambda n, s, d=F32: ctx.enter_context(nc.sbuf_tensor(n, s, d))
        sem = lambda n: ctx.enter_context(nc.semaphore(n))
        AB, M = sb("f0_AB", [P, 2, D]), sb("f0_M", [P, D])
        ab_made, ab_copied, m_made, m_copied = sem("ab_made"), sem("ab_copied"), sem("m_made"), sem("m_copied")
        with nc.Block() as block:
            @block.tensor
            def _(pe):
                mm = nc.tensor.matmul
                mm(PS[0][:, 0:D], w("wr"), w("cos"), start=True, stop=False)
                mm(PS[0][:, 0:D], w("wi"), w("sin"), start=False, stop=True)
                mm(PS[1][:, 0:D], w("wi"), w("cos"), start=True, stop=False)
                mm(PS[1][:, 0:D], w("wr"), w("nsin"), start=False, stop=True).then_inc(ab_made, 1)
                pe.wait_ge(ab_copied, 2)
                mm(PS[2][:, 0:D], AB[:, 0, :], w("cos"), start=True, stop=False)
                mm(PS[2][:, 0:D], AB[:, 1, :], w("nsin"), start=False, stop=True).then_inc(m_made, 1)

            @block.scalar
            def _(act):
                act.wait_ge(ab_made, 1)
                for k in range(2):
                    nc.scalar.activation(AB[:, k, :], PS[k][:, 0:D], ACT.Copy).then_inc(ab_copied, 1)
                act.wait_ge(m_made, 1)
                nc.scalar.activation(M[:, :], PS[2][:, 0:D], ACT.Copy, scale=1.0 / D).then_inc(m_copied, 1)
                act.wait_ge(m_copied, 1)

        def products(pe, g, bank):
            for j in range(GT):
                t = GT * g + j
                last = nc.tensor.matmul(bank[:, P * j:P * j + P], c.NT[1][:, P * t:P * t + P], M[:, :],
                                        start=True, stop=True)
            return last
        project_tail(c, "f0", products, "fbias", c.NT[0])


def l1_attn(c):
    nc, w, PS = c.nc, c.w, c.PS
    dve = c.dve
    NTI = c.NT[0]
    TH = NT_TILES * H1
    used = []
    with ExitStack() as ctx:
        sb = lambda n, s, d=F32: ctx.enter_context(nc.sbuf_tensor(n, s, d))
        sem = lambda n: ctx.enter_context(nc.semaphore(n))
        SIN, COS = sb("s_SIN", [P, NT_TILES, H1 * 32]), sb("s_COS", [P, NT_TILES, H1 * 32])
        DT, DTA = sb("s_DT", [P, TH]), sb("s_DTA", [P, TH])
        EC, ETP = sb("s_EC", [P, TH]), sb("s_ETP", [P, NT_TILES, 2])
        WS, WED, CD = sb("s_WS", [P, TH]), sb("s_WED", [P, TH]), sb("s_CD", [P, TH])
        YT = sb("s_YT", [P, 2, TOK])
        NS, WI = sb("s_NS", [P, 2, TOK], F32R), sb("s_WI", [P, 2, 1024], F32R)
        IDB, MKB = sb("s_IDB", [P, P], BF16), sb("s_MKB", [P, H1, P], BF16)
        SS, RR = sb("s_SS", [P, NT_TILES]), sb("s_RR", [P, NT_TILES])
        with ExitStack() as ctx1:
            sb1 = lambda n, s, d=F32: ctx1.enter_context(nc.sbuf_tensor(n, s, d))
            sem1 = lambda n: cleared(nc, n, used)
            RAW, AB, EX, LN = (sb1(n, [P, TH]) for n in ("s_RAW", "s_AB", "s_EX", "s_LN"))
            NEGA, CAR, TOTA, ET = sb1("s_NEGA", [P, H1]), sb1("s_CAR", [P, TH]), sb1("s_TOTA", [P, TH]), sb1("s_ET", [P, TH])
            TOT, CUM = sb1("s_TOT", [P, TH]), sb1("s_CUM", [P, TH])
            ANG, TURN = sb1("s_ANG", [P, TH, 32]), sb1("s_TURN", [P, TH, 32])
            dt_made, ab_ready, soft_ready, a_ready, dt_ready, sums_made = (sem1(n) for n in (
                "dt_made", "ab_ready", "soft_ready", "a_ready", "dt_ready", "sums_made"))
            decay_ready, decays, ang_ready, sin_ready, ex_ready, wi_high, ns_high, split_low = (sem1(n) for n in (
                "decay_ready", "decays", "ang_ready", "sin_ready", "ex_ready", "wi_high", "ns_high", "split_low"))
            with nc.Block() as block:
                @block.tensor
                def _(pe):
                    mm = nc.tensor.matmul
                    for t in range(NT_TILES):
                        last = mm(PS[0][:, H1 * t:H1 * t + H1], NTI[:, P * t:P * t + P], w("win", 1024, H1),
                                  start=True, stop=True)
                    last.then_inc(dt_made, 1)
                    pe.wait_ge(dt_ready, 1)
                    for k, (lhs, rhs) in enumerate((("upper", DT), ("ones", DT), ("upper", DTA), ("ones", DTA))):
                        mm(PS[1 + k][:, 0:TH], w(lhs), rhs[:, :], start=True, stop=True)
                    mm(PS[5][:, 0:TH], w("shift"), DT[:, :], start=True, stop=False)
                    mm(PS[5][:, 0:TH - H1], w("first"), DT[:, H1:TH], start=False, stop=True).then_inc(sums_made, 1)

                @block.scalar
                def _(act):
                    nc.scalar.activation(NEGA[:, :], w("alog"), ACT.Exp).then_inc(a_ready, 1)
                    nc.scalar.activation(WI[:, 0, :], w("win", 0, 1024), ACT.Copy).then_inc(wi_high, 1)
                    act.wait_ge(ab_ready, 1)
                    nc.scalar.activation(EX[:, :], AB[:, :], ACT.Exp, scale=-1.0).then_inc(ex_ready, 1)
                    act.wait_ge(ex_ready, 1)
                    nc.scalar.activation(LN[:, :], EX[:, :], ACT.Ln, bias=1.0).then_inc(soft_ready, 1)
                    for g in range(G):
                        gs = slice(GW * g, GW * g + GW)
                        nc.scalar.activation(NS[:, 0, gs], NTI[:, gs], ACT.Copy).then_inc(ns_high, 1)
                    act.wait_ge(decay_ready, 1)
                    nc.scalar.activation(EC[:, :], PS[3][:, 0:TH], ACT.Exp).then_inc(decays, 1)
                    nc.scalar.activation(ET[:, :], TOTA[:, :], ACT.Exp).then_inc(decays, 1)
                    nc.scalar.activation(WED[:, :], AB[:, :], ACT.Exp).then_inc(decays, 1)
                    act.wait_ge(ang_ready, 1)
                    nc.scalar.activation(SIN[:, :, :], ANG[:, :, :].rearrange("p (t h) f -> p t (h f)", h=H1), ACT.Sin)\
                        .then_inc(sin_ready, 1)
                    nc.scalar.activation(COS[:, :, :], ANG[:, :, :].rearrange("p (t h) f -> p t (h f)", h=H1), ACT.Sin,
                                         scale=0.5).then_inc(sin_ready, 1)

                @block.gpsimd
                def _(pool):
                    pool.wait_ge(wi_high, 1)
                    nc.gpsimd.tensor_tensor(WI[:, 1, :], w("win", 0, 1024), WI[:, 0, :].bitcast(F32), ALU.subtract)\
                        .then_inc(split_low, 1)
                    for g in range(G):
                        gs = slice(GW * g, GW * g + GW)
                        pool.wait_ge(ns_high, g + 1)
                        nc.gpsimd.tensor_tensor(NS[:, 1, gs], NTI[:, gs], NS[:, 0, gs].bitcast(F32), ALU.subtract)\
                            .then_inc(split_low, 1)

                @block.vector
                def _(v):
                    tt, ts, stt = nc.vector.tensor_tensor, nc.vector.tensor_scalar, nc.vector.scalar_tensor_tensor
                    dve.link(v, nc.vector.tensor_copy(IDB[:, :], w("ident")))
                    dve.link(v, nc.vector.tensor_copy(MKB[:, :, :], rep(w("mask"), H1)))
                    v.wait_ge(dt_made, 1)
                    th = lambda a: a[:, :].rearrange("p (t h) -> p t h", h=H1)
                    dve.link(v, tt(th(RAW), PS[0][:, 0:TH].rearrange("p (t h) -> p t h", h=H1),
                                   rep(w("dtb"), NT_TILES), ALU.add))
                    stt(AB[:, :], RAW[:, :], -1.0, RAW[:, :], ALU.mult, ALU.max).then_inc(ab_ready, 1)
                    v.wait_ge(soft_ready, 1)
                    dve.link(v, stt(DT[:, :], RAW[:, :], 0.0, LN[:, :], ALU.max, ALU.add))
                    v.wait_ge(a_ready, 1)
                    dve.link(v, ts(NEGA[:, :], NEGA[:, :], -1.0, None, ALU.mult))
                    tt(th(DTA), th(DT), rep(NEGA[:, :], NT_TILES), ALU.mult).then_inc(dt_ready, 1)
                    v.wait_ge(sums_made, 1)
                    dve.link(v, nc.vector.tensor_copy(TOTA[:, :], PS[4][:, 0:TH]))
                    dve.link(v, tt(AB[:, :], TOTA[:, :], PS[3][:, 0:TH], ALU.subtract))
                    nc.vector.tensor_copy(TOT[:, :], PS[2][:, 0:TH]).then_inc(decay_ready, 1)
                    v.wait_ge(decay_ready, 1)
                    bc = lambda a, k: a[:, :].rearrange("p (b c h) -> p b c h", b=B, h=H1)[:, :, k, :]
                    dve.link(v, nc.vector.memset(bc(CAR, 0), 0.0))
                    for k in range(1, TPB):
                        dve.link(v, tt(bc(CAR, k), bc(CAR, k - 1), bc(TOT, k - 1), ALU.add))
                    dve.link(v, tt(CUM[:, :], CAR[:, :], PS[1][:, 0:TH], ALU.add))
                    ts_magic = 12582912.0
                    dve.link(v, tt(ANG[:, :, :], CUM[:, :].unsqueeze(2).to_broadcast([P, TH, 32]),
                                   rep(w("freq"), TH), ALU.mult))
                    dve.link(v, ts(TURN[:, :, :], ANG[:, :, :], 1.0 / (2 * np.pi), ts_magic, ALU.mult, ALU.add))
                    dve.link(v, ts(TURN[:, :, :], TURN[:, :, :], ts_magic, None, ALU.subtract))
                    for part in turn_parts():
                        dve.link(v, stt(ANG[:, :, :], TURN[:, :, :], -part, ANG[:, :, :], ALU.mult, ALU.add))
                    lim = float(np.nextafter(np.float32(np.pi), np.float32(0)))
                    ts(ANG[:, :, :], ANG[:, :, :], lim, -lim, ALU.min, ALU.max).then_inc(ang_ready, 1)
                    dve.link(v, ts(CD[:, :], PS[5][:, 0:TH], 0.5, None, ALU.mult))
                    dve.link(v, stt(WS[:, :], DT[:, :], 0.5, CD[:, :], ALU.mult, ALU.add))
                    v.wait_ge(decays, 3)
                    dve.link(v, tt(WED[:, :], WED[:, :], WS[:, :], ALU.mult))
                    for r in range(2):
                        last = nc.vector.tensor_copy(ETP[64 * r:64 * r + 64, :, :],
                                                     th(ET)[64 * r:64 * r + 64, :, r::2])
                    dve.link(v, last)
                    v.wait_ge(sin_ready, 2)
                    dve.link(v, tt(COS[:, :, :], COS[:, :, :], COS[:, :, :], ALU.mult))
                    dve.link(v, ts(COS[:, :, :], COS[:, :, :], -2.0, 1.0, ALU.mult, ALU.add))

        with ExitStack() as ctx1:
            sb1 = lambda n, s, d=F32: ctx1.enter_context(nc.sbuf_tensor(n, s, d))
            sem1 = lambda n: cleared(nc, n, used)
            two = lambda n, s: [sb1(f"{n}{i}", s) for i in range(2)]
            ZX, TZ = two("s_ZX", [P, 512]), two("s_TZ", [P, 256])
            PR = sb1("s_PR", [P, 4, 256])
            R = two("s_R", [P, 2, H1, 2, 32])
            CS = sb1("s_CS", [P, H1, 64])
            SL = sb1("s_SL", [P, H1, P])
            TB, TC = two("s_TB", [P, 512]), two("s_TC", [P, 256])
            ED = two("s_ED", [P, 512])
            XW, XD = two("s_XW", [P, H1, 64]), two("s_XD", [P, H1, 64])
            CB, CC = sb1("s_CB", [P, H1, 64]), two("s_CC", [P, H1])
            GE, H = sb1("s_GE", [P, 512]), sb1("s_H", [P, 2, P])
            YG, SG, XC = two("s_YG", [P, 256]), sb1("s_SG", [P, 256]), sb1("s_XC", [P, 256])
            SQ = sb1("s_SQ", [P, 256])
            (proj_made, zx_copied, tz_ready, prods_ready, rot_ready, cs_ready, sl_ready, decay_made, decay_read,
             turned, turned_copied, g_made, ge_ready, xw_ready, y_made, y_read, h_ready, yg_ready, ss_ready,
             rr_ready, yt_made, yt_copied, cc_ready, h_zero, sg_ready, rr_in, g_half) = (
                sem1("ssd_" + n) for n in (
                    "proj_made", "zx_copied", "tz_ready", "prods_ready", "rot_ready", "cs_ready", "sl_ready",
                    "decay_made", "decay_read", "turned", "turned_copied", "g_made", "ge_ready", "xw_ready",
                    "y_made", "y_read", "h_ready", "yg_ready", "ss_ready", "rr_ready", "yt_made",
                    "yt_copied", "cc_ready", "h_zero", "sg_ready", "rr_in", "g_half"))
            zb, bb, db, tb, tcb, gb, yb, ob = PS[0], PS[1], PS[2], PS[3], PS[4], PS[5], PS[6], PS[7]
            BCV = bb[:, :].rearrange("p (c h e f) -> p (c h) e f", c=2, h=H1, e=2)
            rsel = lambda r, k: r[:, k, :, :, :].rearrange("p h e f -> p h (e f)")
            steps = range(NT_TILES + 2)
            with nc.Block() as block:
                @block.tensor
                def _(pe):
                    mm, tr = nc.tensor.matmul, nc.tensor.transpose
                    for i in steps:
                        if i < NT_TILES:
                            t = i
                            if t:
                                pe.wait_ge(zx_copied, t)
                                pe.wait_ge(tz_ready, t)
                                pe.wait_ge(prods_ready, t)
                            for k, bank in enumerate((bb, zb)):
                                for a, b in HL:
                                    last = mm(bank[:, :], NS[:, a, P * t:P * t + P], WI[:, b, 512 * (1 - k):512 * (2 - k)],
                                              start=((a, b) == HL[0]), stop=((a, b) == HL[-1]))
                            last.then_inc(proj_made, 1)
                        if 1 <= i <= NT_TILES:
                            t = i - 1
                            pe.wait_ge(turned_copied, 2 * t + 2)
                            if t:
                                pe.wait_ge(ge_ready, t)
                            for h in (0, 2, 1, 3):
                                r, q = 64 * (h % 2), P * (h // 2)
                                if h == 1:
                                    last.then_inc(g_half, 1)
                                    pe.wait_ge(g_half, t + 1)
                                last = mm(gb[:, P * h:P * h + P], TB[t % 2][r:r + 64, q:q + P],
                                          TB[t % 2][r:r + 64, 256 + q:256 + q + P], start=True, stop=True)
                            last.then_inc(g_made, 1)
                        if i < NT_TILES:
                            t = i
                            pe.wait_ge(sl_ready, t + 1)
                            if t:
                                pe.wait_ge(decay_read, t)
                            mm(db[:, :], IDB[:, :], MKB[:, :, :], start=True, stop=False)
                            for h in range(H1):
                                last = mm(db[:, P * h:P * h + P], SL[:, h, :], w("upper"), start=False, stop=h == H1 - 1)
                            last.then_inc(decay_made, 1)
                        if 1 <= i <= NT_TILES:
                            t = i - 1
                            pe.wait_ge(ge_ready, t + 1)
                            pe.wait_ge(xw_ready, t + 1)
                            if t:
                                pe.wait_ge(y_read, t)
                                pe.wait_ge(h_ready, t)
                            first = True
                            if t % TPB:
                                for pair in range(2):
                                    mm(yb[:, P * pair:P * pair + P], TC[t % 2][:, P * pair:P * pair + P], H[:, pair, :],
                                       start=first, stop=False, skip_group_check=True)
                                    first = False
                            for h in range(H1):
                                mm(yb[:, 64 * h:64 * h + 64], GE[:, P * h:P * h + P], XW[t % 2][:, h, :],
                                   start=first, stop=True, skip_group_check=True)
                                first = False
                            for pair in range(2):
                                last = mm(yb[:, 256 + P * pair:256 + P * pair + P],
                                          rsel(R[t % 2], 0)[:, 2 * pair:2 * pair + 2, :].rearrange("p h n -> p (h n)"),
                                          XD[t % 2][:, 2 * pair:2 * pair + 2, :].rearrange("p h n -> p (h n)"),
                                          start=False, stop=True, skip_group_check=True)
                            last.then_inc(y_made, 1)
                        if i >= 2:
                            t = i - 2
                            pe.wait_ge(yg_ready, t + 1)
                            if t:
                                pe.wait_ge(yt_copied, t)
                            for pair in range(2):
                                last = tr(ob[:, P * pair:P * pair + P], YG[t % 2][:, P * pair:P * pair + P], w("ident"))
                            last.then_inc(yt_made, 1)
                        if i < NT_TILES:
                            t = i
                            pe.wait_ge(rot_ready, t + 1)
                            pe.wait_ge(cs_ready, t + 1)
                            if t:
                                pe.wait_ge(turned_copied, 2 * t)
                            for k in range(2):
                                for pair in range(2):
                                    tr(tb[:, 256 * k + P * pair:256 * k + P * pair + P],
                                       rsel(R[t % 2], k)[:, 2 * pair:2 * pair + 2, :].rearrange("p h n -> p (h n)"),
                                       w("ident"))
                            for pair in range(2):
                                last = tr(tcb[:, P * pair:P * pair + P],
                                          CS[:, 2 * pair:2 * pair + 2, :].rearrange("p h n -> p (h n)"), w("ident"))
                            last.then_inc(turned, 1)

                @block.scalar
                def _(act):
                    av = nc.scalar.activation
                    for i in steps:
                        if i < NT_TILES:
                            t = i
                            act.wait_ge(proj_made, t + 1)
                            if t >= 2:
                                act.wait_ge(yg_ready, t - 1)
                                act.wait_ge(xw_ready, t - 1)
                                act.wait_ge(sg_ready, t - 1)
                            av(ZX[t % 2][:, :], zb[:, :], ACT.Copy).then_inc(zx_copied, 1)
                            av(TZ[t % 2][:, :], zb[:, 0:256], ACT.Tanh, scale=0.5).then_inc(tz_ready, 1)
                            act.wait_ge(decay_made, t + 1)
                            if t >= 2:
                                act.wait_ge(ge_ready, t - 1)
                            av(ED[t % 2][:, :], db[:, :], ACT.Exp).then_inc(decay_read, 1)
                            act.wait_ge(turned, t + 1)
                            if t >= 2:
                                act.wait_ge(y_made, t - 1)
                            av(TB[t % 2][:, :], tb[:, :], ACT.Copy).then_inc(turned_copied, 1)
                            av(TC[t % 2][:, :], tcb[:, 0:256], ACT.Copy).then_inc(turned_copied, 1)
                        if 1 <= i <= NT_TILES:
                            t = i - 1
                            act.wait_ge(yg_ready, t + 1)
                            if t:
                                act.wait_ge(ss_ready, t)
                            av(SQ[:, :], YG[t % 2][:, :], ACT.Square, accum_out=SS[:, t:t + 1]).then_inc(ss_ready, 1)
                        if i >= 2:
                            t = i - 2
                            act.wait_ge(yt_made, t + 1)
                            for pair in range(2):
                                last = av(YT[:, pair, P * t:P * t + P], ob[:, P * pair:P * pair + P], ACT.Copy,
                                          scale=w("nw", pair, 1))
                            last.then_inc(yt_copied, 1)

                @block.gpsimd
                def _(pool):
                    gt = nc.gpsimd.tensor_tensor
                    for i in steps:
                        if i < NT_TILES:
                            t, hs = i, slice(H1 * i, H1 * i + H1)
                            if t:
                                pool.wait_ge(decay_made, t)
                            gt(SL[:, :, :], rep(w("below"), H1), DTA[:, hs].unsqueeze(2).to_broadcast([P, H1, P]),
                               ALU.mult).then_inc(sl_ready, 1)
                            pool.wait_ge(prods_ready, t + 1)
                            if t >= 2:
                                pool.wait_ge(y_made, t - 1)
                                pool.wait_ge(cc_ready, t - 1)
                            pr = lambda k: PR[:, k, :].rearrange("p (c f) -> p c f", f=32)
                            ro = lambda e: R[t % 2][:, :, :, e, :].rearrange("p c h f -> p (c h) f")
                            gt(ro(0), pr(0), pr(1), ALU.subtract)
                            gt(ro(1), pr(2), pr(3), ALU.add).then_inc(rot_ready, 1)
                            pool.wait_ge(rot_ready, t + 1)
                            if t:
                                pool.wait_ge(turned, t)
                            gt(CS[:, :, :], rsel(R[t % 2], 1), EC[:, hs].unsqueeze(2).to_broadcast([P, H1, 64]),
                               ALU.mult).then_inc(cs_ready, 1)
                            pool.wait_ge(zx_copied, t + 1)
                            if t >= 2:
                                pool.wait_ge(y_made, t - 1)
                            xh = ZX[t % 2][:, 256:512].rearrange("p (h n) -> p h n", h=H1)
                            gt(XW[t % 2][:, :, :], xh, WS[:, hs].unsqueeze(2).to_broadcast([P, H1, 64]), ALU.mult)
                            gt(XD[t % 2][:, :, :], xh, WED[:, hs].unsqueeze(2).to_broadcast([P, H1, 64]), ALU.mult)\
                                .then_inc(xw_ready, 1)
                    pool.wait_ge(rr_in, 1)
                    gt(RR[:, :], SS[:, :], c.MHALF[:, 0:NT_TILES], ALU.pow).then_inc(rr_ready, 1)

                @block.vector
                def _(v):
                    tt, ts, stt = nc.vector.tensor_tensor, nc.vector.tensor_scalar, nc.vector.scalar_tensor_tensor
                    nc.vector.memset(H[:, :, :], 0.0).then_inc(h_zero, 1)
                    v.wait_ge(h_zero, 1)
                    for i in steps:
                        if i < NT_TILES:
                            t, hs = i, slice(H1 * i, H1 * i + H1)
                            v.wait_ge(proj_made, t + 1)
                            if t:
                                v.wait_ge(rot_ready, t)
                            cs, sn = (a[:, t, :].rearrange("p (h f) -> p h f", h=H1) for a in (COS, SIN))
                            for k, (e, tr) in enumerate(((0, cs), (1, sn), (0, sn), (1, cs))):
                                last = tt(PR[:, k, :].rearrange("p (c h f) -> p c h f", c=2, h=H1),
                                          BCV[:, :, e, :].rearrange("p (c h) f -> p c h f", c=2),
                                          tr.unsqueeze(1).to_broadcast([P, 2, H1, 32]), ALU.mult)
                            last.then_inc(prods_ready, 1)
                        if 1 <= i <= NT_TILES:
                            t = i - 1
                            v.wait_ge(g_made, t + 1)
                            v.wait_ge(decay_read, t + 1)
                            if t:
                                v.wait_ge(y_made, t)
                            tt(GE[:, :], gb[:, :], ED[t % 2][:, :], ALU.mult).then_inc(ge_ready, 1)
                            xh = ZX[t % 2][:, 256:512].rearrange("p (h n) -> p h n", h=H1)
                            v.wait_ge(zx_copied, t + 1)
                            dve.link(v, tt(XC[:, :].rearrange("p (h n) -> p h n", h=H1), xh,
                                           CC[t % 2][:, :].unsqueeze(2).to_broadcast([P, H1, 64]), ALU.mult))
                        if i < NT_TILES:
                            t, hs = i, slice(H1 * i, H1 * i + H1)
                            v.wait_ge(rot_ready, t + 1)
                            dve.link(v, tt(CB[:, :, :], rsel(R[t % 2], 0), rsel(R[t % 2], 1), ALU.mult))
                            dve.link(v, nc.vector.reduce_sum(CC[t % 2][:, :], CB[:, :, :], axis=AX.X))
                            tt(CC[t % 2][:, :], CC[t % 2][:, :], CD[:, hs], ALU.mult).then_inc(cc_ready, 1)
                            v.wait_ge(cc_ready, t + 1)
                        if 1 <= i <= NT_TILES:
                            t = i - 1
                            v.wait_ge(tz_ready, t + 1)
                            stt(SG[:, :], TZ[t % 2][:, :], 1.0, ZX[t % 2][:, 0:256], ALU.add, ALU.mult)\
                                .then_inc(sg_ready, 1)
                            v.wait_ge(y_made, t + 1)
                            if t >= 2:
                                v.wait_ge(yt_made, t - 1)
                                v.wait_ge(ss_ready, t - 1)
                            tt(YG[t % 2][:, :], yb[:, 0:256], XC[:, :], ALU.subtract).then_inc(y_read, 1)
                            for pair in range(2):
                                for r in range(2):
                                    rows, cols = slice(64 * r, 64 * r + 64), slice(64 * r, 64 * r + 64)
                                    src = yb[rows, 256 + P * pair + 64 * r:256 + P * pair + 64 * r + 64]
                                    if t % TPB == 0:
                                        last = nc.vector.tensor_copy(H[rows, pair, cols], src)
                                    else:
                                        last = stt(H[rows, pair, cols], H[rows, pair, cols],
                                                   ETP[rows, t, pair:pair + 1], src, ALU.mult, ALU.add)
                            last.then_inc(h_ready, 1)
                            v.wait_ge(y_read, t + 1)
                            v.wait_ge(sg_ready, t + 1)
                            tt(YG[t % 2][:, :], YG[t % 2][:, :], SG[:, :], ALU.mult).then_inc(yg_ready, 1)
                    v.wait_ge(ss_ready, NT_TILES)
                    ts(SS[:, :], SS[:, :], 1.0 / 256, 4e-6, ALU.mult, ALU.add).then_inc(rr_in, 1)

        def products(pe, g, bank):
            for j in range(GT):
                t = GT * g + j
                for k in range(2):
                    last = nc.tensor.matmul(bank[:, P * j:P * j + P], YT[:, k, P * t:P * t + P], w("wout", D * k, D),
                                            start=(k == 0), stop=(k == 1))
            return last
        nc.clear_and_free_semaphores(used)
        nc.all_engine_barrier()
        project_tail(c, "s1", products, None, c.NT[1], scale=RR)


def turn_parts():
    a = 6.28125
    b = float(np.float32(np.round((2 * np.pi - a) * 2 ** 20) / 2 ** 20))
    return a, b, 2 * np.pi - a - b


def softmax_top2(c, v, LG, T, probs_exp):
    nc, w, link = c.nc, c.w, c.dve.link
    tt, ts, stt = nc.vector.tensor_tensor, nc.vector.tensor_scalar, nc.vector.scalar_tensor_tensor
    n = NT_TILES
    bc = lambda a: a[:, :].unsqueeze(2).to_broadcast([P, n, E8])
    rmax = lambda o, a: link(v, nc.vector.reduce_max(o[:, :], a[:, :, :], axis=AX.X))
    exp_wanted, exp_done = probs_exp
    rmax(T.MX, LG)
    tt(T.A[:, :, :], LG[:, :, :], bc(T.MX), ALU.subtract).then_inc(exp_wanted, 1)
    v.wait_ge(exp_done, 1)
    link(v, nc.vector.reduce_sum(T.MX[:, :], T.PB[:, :, :], axis=AX.X))
    link(v, nc.vector.reciprocal(T.MX[:, :], T.MX[:, :]))
    link(v, tt(T.PB[:, :, :], T.PB[:, :, :], bc(T.MX), ALU.mult))
    for oh, m in ((T.OH1, T.M1), (T.OH2, T.M2)):
        rmax(m, T.PB)
        link(v, tt(T.A[:, :, :], T.PB[:, :, :], bc(m), ALU.is_equal))
        link(v, tt(T.A[:, :, :], T.A[:, :, :], rep(w("rank"), n), ALU.mult))
        rmax(T.MX, T.A)
        link(v, tt(oh[:, :, :], T.A[:, :, :], bc(T.MX), ALU.is_equal))
        if oh is T.OH1:
            link(v, stt(T.PB[:, :, :], oh[:, :, :], -2.0, T.PB[:, :, :], ALU.mult, ALU.add))


def choice_tiles(sb, tag):
    T = Common()
    T.A, T.PB, T.OH1, T.OH2 = (sb(f"{tag}_{n}", [P, NT_TILES, E8]) for n in ("A", "PB", "OH1", "OH2"))
    T.MX, T.M1, T.M2 = (sb(f"{tag}_{n}", [P, NT_TILES]) for n in ("MX", "M1", "M2"))
    return T


def start_sums(c, tag, OH, ACC, b2, MT, sums, split, first=True, beside=None):
    nc, w, PS = c.nc, c.w, c.PS
    with ExitStack() as ctx:
        OHT = c.NT[0][0:E8, :]
        REST = ctx.enter_context(nc.sbuf_tensor(tag + "_REST", [E8, TOK], F32)) if split else None
        MID = ctx.enter_context(nc.sbuf_tensor(tag + "_MID", [E8, TOK], BF16)) if split else None
        oh_turned, oh_copied, b_made, b_copied = sums
        with nc.Block() as block:
            @block.tensor
            def _(pe):
                for g in range(G):
                    for j in range(GT):
                        last = nc.tensor.transpose(PS[g][0:E8, P * j:P * j + P], OH[:, GT * g + j, :], w("ident"))
                    last.then_inc(oh_turned, 1)
                for g in range(G):
                    pe.wait_ge(oh_copied, g + 1)
                    nc.tensor.matmul(PS[4 + g][:, :], b2, OHT[:, GW * g:GW * g + GW], start=True, stop=True)\
                        .then_inc(b_made, 1)

            @block.scalar
            def _(act):
                for g in range(G):
                    act.wait_ge(oh_turned, g + 1)
                    nc.scalar.activation(OHT[:, GW * g:GW * g + GW], PS[g][0:E8, :], ACT.Copy).then_inc(oh_copied, 1)
                if beside:
                    beside[1](act)
                for g in range(G):
                    act.wait_ge(b_made, g + 1)
                    nc.scalar.activation(ACC[:, GW * g:GW * g + GW], PS[4 + g][:, :], ACT.Copy).then_inc(b_copied, 1)

            if beside:
                @block.gpsimd
                def _(pool):
                    beside[2](pool)

            @block.vector
            def _(v):
                cp, tt, link = nc.vector.tensor_copy, nc.vector.tensor_tensor, c.dve.link
                if beside:
                    beside[0](v)
                if first:
                    link(v, nc.vector.memset(MT[:, :].bitcast(U32), 0))
                v.wait_ge(oh_copied, G)
                link(v, cp(MT[0:E8, :], OHT[:, :]))
                if split:
                    link(v, tt(REST[:, :], OHT[:, :], MT[0:E8, :], ALU.subtract))
                    link(v, cp(MID[:, :], REST[:, :]))
                    cp(MT[32:32 + E8, :], MID[:, :])
                    link(v, tt(REST[:, :], REST[:, :], MID[:, :], ALU.subtract))
                    cp(MT[64:64 + E8, :], REST[:, :])


def expert_masks(c, v, SEL, SELF, rows):
    nc, w, link = c.nc, c.w, c.dve.link
    link(v, nc.vector.tensor_copy(SELF[0:rows, :], w("ident", 0, E8)[0:rows, :]))
    for part in range(32, rows, 32):
        link(v, nc.vector.tensor_tensor(SELF[0:rows, :], SELF[0:rows, :], w("ident", part, E8)[0:rows, :], ALU.add))
    link(v, nc.vector.tensor_copy(SEL[:, :, :], SELF[0:rows, :].unsqueeze(2).to_broadcast([rows, E8, P])))


HL = ((0, 0), (0, 1), (1, 0))


def l1_ffn(c, w1_dram, w2_dram):
    nc, w, PS = c.nc, c.w, c.PS
    dve = c.dve
    NTI = c.NT[1]
    with ExitStack() as ctx:
        sb = lambda n, s, d=F32: ctx.enter_context(nc.sbuf_tensor("m_" + n, s, d))
        sem = lambda n: ctx.enter_context(nc.semaphore("m_" + n))
        W1, W2 = sb("W1", [P, E8, HID1]), sb("W2", [P, E8, 2 * D])
        WU, WD = sb("WU", [P, 2, E8, HID1], F32R), sb("WD", [P, 2, E8, 2 * D], F32R)
        NS = sb("NS", [P, 2, TOK], F32R)
        T, LG = choice_tiles(sb, "m"), sb("LG", [P, NT_TILES, E8])
        ACC = [sb(f"ACC{i}", [P, TOK]) for i in range(2)]
        BT = sb("BT", [P, TOK])
        MT, SEL, SELF = sb("MT", [P, TOK], BF16), sb("SEL", [P, E8, P], BF16), sb("SELF", [P, E8])
        loaded = sem("loaded")
        (lg_made, exp_wanted, exp_done, w_high, w_low, n_high, n_low, b_ready) = (sem(n) for n in (
            "lg_made", "exp_wanted", "exp_done", "w_high", "w_low", "n_high", "n_low", "b_ready"))

        def tokens_high(act, src, src_ready=None):
            for g in range(G):
                gs = slice(GW * g, GW * g + GW)
                if src_ready is not None:
                    act.wait_ge(src_ready, g + 1)
                nc.scalar.activation(NS[:, 0, gs], src[:, gs], ACT.Copy).then_inc(n_high, 1)

        def tokens_low(pool, src, first):
            for g in range(G):
                gs = slice(GW * g, GW * g + GW)
                pool.wait_ge(n_high, first + g + 1)
                nc.gpsimd.tensor_tensor(NS[:, 1, gs], src[:, gs], NS[:, 0, gs].bitcast(F32), ALU.subtract)\
                    .then_inc(n_low, 1)

        def weights_low(eng, tensor_tensor, k):
            raw, part = ((W1, WU), (W2, WD))[k]
            eng.wait_ge(w_high, k + 1)
            tensor_tensor(part[:, 1, :, :], raw[:, :, :], part[:, 0, :, :].bitcast(F32), ALU.subtract)\
                .then_inc(w_low, 1)

        with nc.Block() as block:
            @block.sync
            def _(sp):
                for dst, src in ((W1, w1_dram), (W2, w2_dram.rearrange("e p k d -> e p (k d)"))):
                    sp.dma_start(dst[:, :, :], src.rearrange("e p n -> p e n")).then_inc(loaded, 16)

            @block.tensor
            def _(pe):
                for t in range(NT_TILES):
                    last = nc.tensor.matmul(PS[0][:, E8 * t:E8 * t + E8], NTI[:, P * t:P * t + P], w("gw"),
                                            start=True, stop=True)
                last.then_inc(lg_made, 1)

            @block.scalar
            def _(act):
                tokens_high(act, NTI)
                act.wait_ge(loaded, 32)
                nc.scalar.activation(WU[:, 0, :, :], W1[:, :, :], ACT.Copy).then_inc(w_high, 1)
                act.wait_ge(exp_wanted, 1)
                nc.scalar.activation(T.PB[:, :, :], T.A[:, :, :], ACT.Exp).then_inc(exp_done, 1)
                nc.scalar.activation(WD[:, 0, :, :], W2[:, :, :], ACT.Copy).then_inc(w_high, 1)

            @block.gpsimd
            def _(pool):
                tokens_low(pool, NTI, 0)
                weights_low(pool, nc.gpsimd.tensor_tensor, 0)

            @block.vector
            def _(v):
                expert_masks(c, v, SEL, SELF, P)
                v.wait_ge(lg_made, 1)
                dve.link(v, nc.vector.tensor_tensor(LG[:, :, :],
                                                    PS[0][:, 0:NT_TILES * E8].rearrange("p (t e) -> p t e", e=E8),
                                                    rep(w("gb"), NT_TILES), ALU.add))
                softmax_top2(c, v, LG, T, (exp_wanted, exp_done))
                weights_low(v, nc.vector.tensor_tensor, 1)

        sums = [[sem(f"{n}{r}") for n in ("oh_turned", "oh_copied", "b_made", "b_copied")] for r in range(2)]
        start_sums(c, "m0", T.OH1, ACC[0], c.W2S[:, 0:D], MT, sums[0], False)
        expert_round(c, "m0", NS, WU, WD, MT, SEL, ACC[0])

        def sum_inputs(v):
            for g in range(G):
                gs = slice(GW * g, GW * g + GW)
                nc.vector.scalar_tensor_tensor(BT[:, gs], ACC[0][:, gs], 0.5, NTI[:, gs], ALU.mult, ALU.add)\
                    .then_inc(b_ready, 1)

        start_sums(c, "m1", T.OH2, ACC[1], c.W2S[:, 0:D], MT, sums[1], False, first=False,
                   beside=(sum_inputs, lambda act: tokens_high(act, BT, b_ready), lambda pool: tokens_low(pool, BT, G)))
        expert_round(c, "m1", NS, WU, WD, MT, SEL, ACC[1])

        base, nv0 = c.n_front, c.n_var
        Y = BT[:, :].rearrange("p (t d) -> p t d", d=D)
        turned, y_ready = sem("turned"), sem("y_ready")
        with nc.Block() as block:
            @block.tensor
            def _(pe):
                for g in range(G):
                    for r in range(2):
                        i = 2 * g + r
                        if i >= 6:
                            pe.wait_ge(y_ready, i - 5)
                        for j in range(GT):
                            t = GT * g + j
                            last = nc.tensor.transpose(PS[i % 6][:, P * j:P * j + P], ACC[r][:, P * t:P * t + P],
                                                       w("ident"))
                        last.then_inc(turned, 1)
                for g in range(G):
                    transpose_xn(c, pe, base, g, PS[7])

            @block.scalar
            def _(act):
                act_tails(c, act, 3, nv0, base, lambda g: Y[:, GT * g:GT * g + GT, :], c.NT[0], PS[7])

            @block.gpsimd
            def _(pool):
                pool_tails(c, pool, 3, nv0, base)

            @block.vector
            def _(v):

                def make(g):
                    for r, (m, src) in enumerate(((T.M1, c.XN), (T.M2, Y))):
                        v.wait_ge(turned, 2 * g + r + 1)
                        for j in range(GT):
                            t = GT * g + j
                            last = nc.vector.scalar_tensor_tensor(Y[:, t, :], PS[(2 * g + r) % 6][:, P * j:P * j + P],
                                                                  m[:, t:t + 1], src[:, t, :], ALU.mult, ALU.add)
                        last.then_inc(y_ready, 1)
                        v.wait_ge(y_ready, 2 * g + r + 1)
                    return Y[:, GT * g:GT * g + GT, :]

                def own(YG):
                    dve.link(v, nc.vector.tensor_tensor(YG, YG, rep(w("lng"), GT), ALU.mult))
                    dve.link(v, nc.vector.tensor_tensor(YG, YG, rep(w("lnb"), GT), ALU.add))
                tails(c, v, make, own)


def expert_round(c, tag, NS, WU, WD, MT, SEL, ACC):
    nc, w, PS = c.nc, c.w, c.PS
    n = E8 * G
    with ExitStack() as ctx:
        sb = lambda s, shape, d=F32: ctx.enter_context(nc.sbuf_tensor(tag + s, shape, d))
        sem = lambda s: ctx.enter_context(nc.semaphore(tag + s))
        HS = [sb(f"_HS{i}", [P, 2, 2, GW], F32R) for i in range(3)]
        HF = [sb(f"_HF{i}", [P, 2, GW]) for i in range(3)]
        MB = [sb(f"_MB{i}", [P, GW]) for i in range(3)]
        Z = sb("_Z", [P, GW])
        (h_made, high_ready, full0, full1, low_ready, mb_made, mb_ready, y_made, z_ready, summed) = (sem(s) for s in (
            "_h_made", "_high_ready", "_full0", "_full1", "_low_ready", "_mb_made", "_mb_ready", "_y_made", "_z_ready",
            "_summed"))
        with nc.Block() as block:
            @block.tensor
            def _(pe):
                for i in range(n + 2):
                    if i < n:
                        e, g = divmod(i, G)
                        gs = slice(GW * g, GW * g + GW)
                        if i >= 2:
                            pe.wait_ge(mb_ready, i - 1)
                        nc.tensor.matmul(PS[6 + i % 2][:, :], SEL[:, e, :], MT[:, gs], start=True, stop=True)\
                            .then_inc(mb_made, 1)
                        for k in range(2):
                            if i >= 2:
                                pe.wait_ge(high_ready, 2 * (i - 2) + k + 1)
                                pe.wait_ge((full0, full1)[k], i - 1)
                            for a, b in HL:
                                last = nc.tensor.matmul(PS[2 * (i % 2) + k][:, :], WU[:, a, e, P * k:P * k + P],
                                                        NS[:, b, gs], start=((a, b) == HL[0]), stop=((a, b) == HL[-1]))
                            last.then_inc(h_made, 1)
                    if i >= 2:
                        q = i - 2
                        e = q // G
                        pe.wait_ge(high_ready, 2 * q + 2)
                        pe.wait_ge(low_ready, 2 * q + 2)
                        if q >= 2:
                            pe.wait_ge(z_ready, q - 1)
                        for k in range(2):
                            for a, b in HL:
                                last = nc.tensor.matmul(PS[4 + q % 2][:, :], WD[:, b, e, D * k:D * k + D],
                                                        HS[q % 3][:, a, k, :], start=(k == 0 and (a, b) == HL[0]),
                                                        stop=(k == 1 and (a, b) == HL[-1]))
                        last.then_inc(y_made, 1)

            @block.scalar
            def _(act):
                for i in range(n):
                    e = i // G
                    act.wait_ge(mb_made, i + 1)
                    if i >= 3:
                        act.wait_ge(z_ready, i - 2)
                    nc.scalar.activation(MB[i % 3][:, :], PS[6 + i % 2][:, :], ACT.Copy).then_inc(mb_ready, 1)
                    if i >= 3:
                        act.wait_ge(y_made, i - 2)
                        act.wait_ge(low_ready, 2 * (i - 3) + 2)
                    for k in range(2):
                        act.wait_ge(h_made, 2 * i + k + 1)
                        bias = w("b1m", 2 * e + k, 1)
                        nc.scalar.activation(HS[i % 3][:, 0, k, :], PS[2 * (i % 2) + k][:, :], ACT.Relu, bias=bias)\
                            .then_inc(high_ready, 1)
                    nc.scalar.activation(HF[i % 3][:, 1, :], PS[2 * (i % 2) + 1][:, :], ACT.Relu, bias=bias)\
                        .then_inc(full1, 1)

            @block.gpsimd
            def _(pool):
                for i in range(n):
                    for k in range(2):
                        pool.wait_ge(high_ready, 2 * i + k + 1)
                        pool.wait_ge((full0, full1)[k], i + 1)
                        nc.gpsimd.tensor_tensor(HS[i % 3][:, 1, k, :], HF[i % 3][:, k, :],
                                                HS[i % 3][:, 0, k, :].bitcast(F32), ALU.subtract).then_inc(low_ready, 1)

            @block.vector
            def _(v):
                for i in range(n + 2):
                    if i < n:
                        e = i // G
                        v.wait_ge(high_ready, 2 * i + 1)
                        if i >= 3:
                            v.wait_ge(low_ready, 2 * (i - 3) + 1)
                        nc.vector.tensor_scalar(HF[i % 3][:, 0, :], PS[2 * (i % 2)][:, :], w("b1m", 2 * e, 1), 0.0,
                                                ALU.add, ALU.max).then_inc(full0, 1)
                    if i >= 2:
                        q = i - 2
                        gs = slice(GW * (q % G), GW * (q % G) + GW)
                        v.wait_ge(y_made, q + 1)
                        v.wait_ge(mb_ready, q + 1)
                        if q:
                            v.wait_ge(summed, q)
                        nc.vector.tensor_tensor(Z[:, :], PS[4 + q % 2][:, :], MB[q % 3][:, :], ALU.mult)\
                            .then_inc(z_ready, 1)
                        v.wait_ge(z_ready, q + 1)
                        nc.vector.tensor_tensor(ACC[:, gs], ACC[:, gs], Z[:, :], ALU.add).then_inc(summed, 1)


def l2_attn(c):
    nc, w, PS = c.nc, c.w, c.PS
    dve = c.dve
    NTI = c.NT[0]
    FMAX = float(np.finfo(np.float32).max)
    with ExitStack() as ctx:
        sb = lambda n, s, d=F32: ctx.enter_context(nc.sbuf_tensor(n, s, d))
        sem = lambda n: ctx.enter_context(nc.semaphore(n))
        OT = sb("r_OT", [P, TOK])
        with ExitStack() as ctx1:
            sb1 = lambda n, s, d=F32: ctx1.enter_context(nc.sbuf_tensor(n, s, d))
            sem1 = lambda n: ctx1.enter_context(nc.semaphore("r_" + n))
            WM = sb1("r_WM", [P, 3, 2, D])
            OM = sb1("r_OM", [P, 3])
            LA, EU, EW = sb1("r_LA", [P, 1]), sb1("r_EU", [P, 1]), sb1("r_EW", [P, 1])
            AP, RN = sb1("r_AP", [P, S]), sb1("r_RN", [P, S])
            ONE = sb1("r_ONE", [P, S])
            EK, EKV, SK, RR = (sb1("r_" + n, [P, TOK]) for n in ("EK", "EKV", "SK", "RR"))
            F_, CSUM = sb1("r_F", [P, S]), sb1("r_CS", [P, S + 1])
            SKR = sb1("r_SKR", [P, TOK])
            ST, STN, MK, DEN = sb1("r_ST", [P, S]), sb1("r_STN", [P, 2 * B, S]), sb1("r_MK", [P, S], U32), sb1("r_DEN", [P, S])
            (wm_ready, kvr_made, ek_ready, ekv_ready, er_ready, sk_made, sk_ready, td_ready, la_ready, ap_ready,
             const_ready, rn_ready, skr_ready) = (sem1(n) for n in (
                 "wm_ready", "kvr_made", "ek_ready", "ekv_ready", "er_ready", "sk_made", "sk_ready",
                 "td_ready", "la_ready", "ap_ready", "const_ready", "rn_ready",
                 "skr_ready"))
            with nc.Block() as block:
                @block.tensor
                def _(pe):
                    mm = nc.tensor.matmul
                    pe.wait_ge(wm_ready, 1)
                    for g in range(G + 1):
                        if g < G:
                            at, head = GW * g, int(g % (G // B) == 0)
                            if g >= 2:
                                pe.wait_ge(ek_ready, g - 1)
                                pe.wait_ge(ekv_ready, g - 1)
                                pe.wait_ge(er_ready, g - 1)
                            for k in range(3):
                                bank = PS[3 * (g % 2) + k]
                                mm(bank[:, :], WM[:, k, 0, :], NTI[:, at:at + GW], start=True, stop=False)
                                mm(bank[:, head:GW], WM[:, k, 1, :], NTI[:, at + head - 1:at + GW - 1], start=False,
                                   stop=True).then_inc(kvr_made, 1)
                        if g:
                            q = g - 1
                            pe.wait_ge(ek_ready, q + 1)
                            if q >= 2:
                                pe.wait_ge(sk_ready, q - 1)
                            mm(PS[6 + q % 2][:, :], w("blocks"), EK[:, GW * q:GW * q + GW], start=True, stop=True)\
                                .then_inc(sk_made, 1)

                @block.scalar
                def _(act):
                    av = nc.scalar.activation
                    av(LA[:, :], w("td"), ACT.Exp)
                    av(EU[:, :], w("tf"), ACT.Exp).then_inc(td_ready, 1)
                    act.wait_ge(la_ready, 1)
                    av(EW[:, :], LA[:, :], ACT.Exp)
                    av(AP[:, :], w("time"), ACT.Exp, scale=LA[:, 0:1]).then_inc(ap_ready, 1)
                    for g in range(G):
                        gs = slice(GW * g, GW * g + GW)
                        act.wait_ge(kvr_made, 3 * g + 1)
                        av(EK[:, gs], PS[3 * (g % 2)][:, :], ACT.Exp).then_inc(ek_ready, 1)
                        act.wait_ge(kvr_made, 3 * g + 3)
                        av(RR[:, gs], PS[3 * (g % 2) + 2][:, :], ACT.Tanh, scale=0.5).then_inc(er_ready, 1)
                        act.wait_ge(sk_made, g + 1)
                        av(SK[:, gs], PS[6 + g % 2][:, :], ACT.Copy).then_inc(sk_ready, 1)

                @block.gpsimd
                def _(pool):
                    nc.gpsimd.memset(ONE[:, :], 1.0)
                    nc.gpsimd.memset(STN[:, :, :], 0.0)
                    nc.gpsimd.memset(CSUM[:, 0:1], 0.0).then_inc(const_ready, 1)
                    pool.wait_ge(rn_ready, 1)
                    for b in range(B):
                        bs = slice(S * b, S * b + S)
                        pool.wait_ge(sk_ready, (b + 1) * (G // B))
                        nc.gpsimd.tensor_tensor(SKR[:, bs], SK[:, bs], RN[:, :], ALU.mult).then_inc(skr_ready, 1)

                @block.vector
                def _(v):
                    tt, ts, stt = nc.vector.tensor_tensor, nc.vector.tensor_scalar, nc.vector.scalar_tensor_tensor
                    dve.link(v, ts(OM[:, :], w("mk", 0, 3), -1.0, 1.0, ALU.mult, ALU.add))
                    for k, (m, wn) in enumerate((("mk", "wkey"), ("mv", "wval"), ("mr", "wrec"))):
                        ts(WM[:, k, 0, :], w(wn), w(m), None, ALU.mult)
                        last = ts(WM[:, k, 1, :], w(wn), OM[:, k:k + 1], None, ALU.mult)
                    last.then_inc(wm_ready, 1)
                    v.wait_ge(td_ready, 1)
                    ts(LA[:, :], LA[:, :], -1.0, None, ALU.mult).then_inc(la_ready, 1)
                    def source(g):
                        gs = slice(GW * g, GW * g + GW)
                        v.wait_ge(kvr_made, 3 * g + 2)
                        v.wait_ge(ek_ready, g + 1)
                        tt(EKV[:, gs], PS[3 * (g % 2) + 1][:, :], EK[:, gs], ALU.mult).then_inc(ekv_ready, 1)

                    source(0)
                    v.wait_ge(ap_ready, 1)
                    dve.link(v, ts(RN[:, :], AP[:, :], EW[:, 0:1], None, ALU.mult))
                    nc.vector.reciprocal(RN[:, :], RN[:, :]).then_inc(rn_ready, 1)
                    v.wait_ge(rn_ready, 1)
                    source(1)
                    v.wait_ge(const_ready, 1)
                    for b in range(B):
                        bs = slice(S * b, S * b + S)
                        v.wait_ge(ekv_ready, (b + 1) * (G // B))
                        for k, state in enumerate("ab"):
                            if state == "a":
                                src = F_[:, :]
                                dve.link(v, tt(src, EKV[:, bs], RN[:, :], ALU.mult))
                            else:
                                src = SKR[:, bs]
                                v.wait_ge(skr_ready, b + 1)
                            dve.link(v, nc.vector.tensor_tensor_scan(CSUM[:, 1:1 + S], ONE[:, :], src, 0.0,
                                                                     ALU.mult, ALU.add))
                            dve.link(v, tt(ST[:, :], AP[:, :], CSUM[:, 0:S], ALU.mult))
                            ts(MK[:, :], ST[:, :], FMAX, None, ALU.is_le)
                            dve.link(v, ts(F_[:, :], ST[:, :], -FMAX, None, ALU.max))
                            kept = STN[:, 2 * b + k, :]
                            dve.link(v, nc.vector.copy_predicated(kept, MK[:, :], F_[:, :]))
                            if state == "a":
                                dve.link(v, stt(EKV[:, bs], EKV[:, bs], EU[:, 0:1], kept, ALU.mult, ALU.add))
                            else:
                                dve.link(v, stt(DEN[:, :], SK[:, bs], EU[:, 0:1], kept, ALU.mult, ALU.add))
                            if b == 0:
                                source(2 + k)
                        dve.link(v, ts(DEN[:, :], DEN[:, :], 1e-6, 2.0, ALU.max, ALU.mult))
                        dve.link(v, nc.vector.reciprocal(DEN[:, :], DEN[:, :]))
                        dve.link(v, tt(EKV[:, bs], EKV[:, bs], DEN[:, :], ALU.mult))
                        v.wait_ge(er_ready, (b + 1) * (G // B))
                        dve.link(v, stt(OT[:, bs], RR[:, bs], 1.0, EKV[:, bs], ALU.add, ALU.mult))

        def products(pe, g, bank):
            for j in range(GT):
                t = GT * g + j
                last = nc.tensor.matmul(bank[:, P * j:P * j + P], OT[:, P * t:P * t + P], w("wo2"),
                                        start=True, stop=True)
            return last
        project_tail(c, "r1", products, None, c.NT[1])


def l2_ffn(c):
    nc, w, PS = c.nc, c.w, c.PS
    NTI = c.NT[1]
    KC = HID2 // P
    with ExitStack() as ctx:
        HT = ctx.enter_context(nc.sbuf_tensor("g_HT", [P, KC, TOK], F32))
        h_made, h_ready = ctx.enter_context(nc.semaphore("g_h_made")), ctx.enter_context(nc.semaphore("g_h_ready"))
        with nc.Block() as block:
            @block.tensor
            def _(pe):
                for i in range(G * KC):
                    g, k = divmod(i, KC)
                    if i >= 4:
                        pe.wait_ge(h_ready, i - 3)
                    nc.tensor.matmul(PS[i % 4][:, :], w("w1f", P * k, P), NTI[:, GW * g:GW * g + GW],
                                     start=True, stop=True).then_inc(h_made, 1)

            @block.scalar
            def _(act):
                for i in range(G * KC):
                    g, k = divmod(i, KC)
                    act.wait_ge(h_made, i + 1)
                    nc.scalar.activation(HT[:, k, GW * g:GW * g + GW], PS[i % 4][:, :], ACT.Relu,
                                         bias=w("b1f", k, 1)).then_inc(h_ready, 1)

        def products(pe, g, bank):
            for j in range(GT):
                t = GT * g + j
                for k in range(KC):
                    last = nc.tensor.matmul(bank[:, P * j:P * j + P], HT[:, k, P * t:P * t + P], w("w2f", D * k, D),
                                            start=(k == 0), stop=(k == KC - 1))
            return last
        project_tail(c, "g1", products, "b2f", c.NT[0])


def l3_attn(c):
    nc, w, PS = c.nc, c.w, c.PS
    dve = c.dve
    NH, HD = NH3, HD3
    M = D // HD
    R = S // M
    NTM = c.NT[0][:, :].rearrange("c (b r m) -> c m b r", b=B, m=M)
    OT = c.NT[0]
    with ExitStack() as ctx:
        sb = lambda n_, s, d=F32: ctx.enter_context(nc.sbuf_tensor("h_" + n_, s, d))
        sem = lambda n_: ctx.enter_context(nc.semaphore("h_" + n_))
        two = lambda n_, s: [sb(f"{n_}{i}", s) for i in range(2)]
        OUT = sb("OUT", [P, NH, M, HD])
        QKV, PR = [sb(f"QKV{i}", [P, 3, NH, HD]) for i in range(3)], two("PR", [P, NH, NH, HD])
        SCR, E, PV = two("SCR", [P, NH, NH]), two("E", [P, NH, NH]), two("PV", [P, NH, HD, NH])
        VH = NH // 2

        def weighted(engine, q, a, b):
            return engine.tensor_tensor(PV[q % 2][:, a:b, :, :],
                                        E[q % 2][:, a:b, :].unsqueeze(2).to_broadcast([P, b - a, HD, NH]),
                                        QKV[q % 3][:, 2, :, :].rearrange("p k d -> p d k").unsqueeze(1)
                                        .to_broadcast([P, b - a, HD, NH]), ALU.mult)

        MX, SM = sb("MX", [P, NH]), sb("SM", [P, NH])
        (made, copied, prod_ready, prod_read, scr_ready, e_ready, e_read, done, turned, ot_copied,
         pv_ready) = (
            sem(n_) for n_ in ("made", "copied", "prod_ready", "prod_read", "scr_ready", "e_ready", "e_read", "done",
                               "turned", "ot_copied", "pv_ready"))
        over = lambda a: a.unsqueeze(2).to_broadcast([P, NH, NH])
        with nc.Block() as block:
            @block.tensor
            def _(pe):
                for m in range(M):
                    if m >= 2:
                        pe.wait_ge(copied, m - 1)
                    nc.tensor.matmul(PS[m % 2][:, 0:3 * D], NTM[:, m, :, :], w("wq3", 0, 3 * D),
                                     start=True, stop=True).then_inc(made, 1)
                pe.wait_ge(done, M)
                for h in range(NH):
                    if h >= 4:
                        pe.wait_ge(ot_copied, h - 3)
                    nc.tensor.transpose(PS[2 + h % 4][:, 0:P], OUT[:, h, :, :].rearrange("p m d -> p (m d)"), w("ident"))\
                        .then_inc(turned, 1)

            @block.scalar
            def _(act):
                for m in range(M + 1):
                    if m < M:
                        act.wait_ge(made, m + 1)
                        if m >= 3:
                            act.wait_ge(prod_ready, m - 2)
                            act.wait_ge(e_read, m - 2)
                        nc.scalar.activation(QKV[m % 3][:, :, :, :].rearrange("p k h d -> p (k h d)"),
                                             PS[m % 2][:, 0:3 * D], ACT.Copy).then_inc(copied, 1)
                    if m:
                        q = m - 1
                        act.wait_ge(scr_ready, q + 1)
                        if q >= 2:
                            act.wait_ge(e_read, q - 1)
                        nc.scalar.activation(E[q % 2][:, :, :], SCR[q % 2][:, :, :], ACT.Exp, scale=HD ** -0.5)\
                            .then_inc(e_ready, 1)
                for h in range(NH):
                    act.wait_ge(turned, h + 1)
                    nc.scalar.activation(OT[:, :].rearrange("c (b x) -> c b x", b=B)[:, :, R * h:R * h + R],
                                         PS[2 + h % 4][:, 0:P].rearrange("c (b r) -> c b r", b=B), ACT.Copy)\
                        .then_inc(ot_copied, 1)

            @block.gpsimd
            def _(pool):
                for m in range(M + 1):
                    if m < M:
                        qkv = QKV[m % 3]
                        pool.wait_ge(copied, m + 1)
                        if m >= 2:
                            pool.wait_ge(prod_read, m - 1)
                        nc.gpsimd.tensor_tensor(PR[m % 2][:, :, :, :],
                                                qkv[:, 0, :, :].unsqueeze(2).to_broadcast([P, NH, NH, HD]),
                                                qkv[:, 1, :, :].unsqueeze(1).to_broadcast([P, NH, NH, HD]), ALU.mult)\
                            .then_inc(prod_ready, 1)
                    if m:
                        q = m - 1
                        pool.wait_ge(e_ready, q + 1)
                        if q >= 2:
                            pool.wait_ge(e_read, q - 1)
                        weighted(nc.gpsimd, q, VH, NH).then_inc(pv_ready, 1)

            @block.vector
            def _(v):
                tt = nc.vector.tensor_tensor
                for m in range(M + 1):
                    if m < M:
                        s = m % 2
                        v.wait_ge(prod_ready, m + 1)
                        if m >= 2:
                            v.wait_ge(e_ready, m - 1)
                        nc.vector.reduce_sum(SCR[s][:, :, :], PR[s][:, :, :, :], axis=AX.X).then_inc(prod_read, 1)
                        v.wait_ge(prod_read, m + 1)
                        dve.link(v, nc.vector.reduce_max(MX[:, :], SCR[s][:, :, :], axis=AX.X))
                        tt(SCR[s][:, :, :], SCR[s][:, :, :], over(MX[:, :]), ALU.subtract).then_inc(scr_ready, 1)
                    if m:
                        q, s = m - 1, (m - 1) % 2
                        v.wait_ge(e_ready, q + 1)
                        if q:
                            v.wait_ge(done, q)
                        dve.link(v, nc.vector.reduce_sum(SM[:, :], E[s][:, :, :], axis=AX.X))
                        dve.link(v, weighted(nc.vector, q, 0, VH))
                        v.wait_ge(pv_ready, q + 1)
                        nc.vector.reduce_sum(OUT[:, :, q, :], PV[s][:, :, :, :], axis=AX.X).then_inc(e_read, 1)
                        dve.link(v, nc.vector.reciprocal(SM[:, :], SM[:, :]))
                        v.wait_ge(e_read, q + 1)
                        tt(OUT[:, :, q, :], OUT[:, :, q, :], SM[:, :].unsqueeze(2).to_broadcast([P, NH, HD]),
                           ALU.mult).then_inc(done, 1)

        def products(pe, g, bank):
            for j in range(GT):
                t = GT * g + j
                last = nc.tensor.matmul(bank[:, P * j:P * j + P], OT[:, P * t:P * t + P], w("wo3"),
                                        start=True, stop=True)
            return last
        project_tail(c, "h1", products, "bo3", c.NT[1])


def l3_ffn(c, w1_dram, w2_dram):
    nc, w, PS = c.nc, c.w, c.PS
    dve = c.dve
    NTI = c.NT[1]
    KC = F3 // P
    n = E8 * G
    with ExitStack() as ctx:
        sb = lambda n_, s, d=F32: ctx.enter_context(nc.sbuf_tensor(n_, s, d))
        sem = lambda n_: ctx.enter_context(nc.semaphore("x_" + n_))
        W1, W2 = sb("x_W1", [P, 2, 2 * F3]), sb("x_W2", [P, 2, KC * D])
        WU = [sb(f"x_WU{i}", [P, 2, 2 * F3], F32R) for i in range(2)]
        WD = [sb(f"x_WD{i}", [P, 2, KC * D], F32R) for i in range(2)]
        NS = sb("x_NS", [P, 2, TOK], F32R)
        T, LG = choice_tiles(sb, "x"), sb("x_LG", [P, NT_TILES, E8])
        HR, HRT = sb("x_HR", [P, NT_TILES, KR]), c.NT[0][0:KR, :]
        ACC = c.XN[:, :, :].rearrange("p t d -> p (t d)")
        MROWS = 64 + E8
        MT, SEL, SELF = sb("x_MT", [MROWS, TOK], BF16), sb("x_SEL", [MROWS, E8, P], BF16), sb("x_SELF", [MROWS, E8])
        MB = [sb(f"x_MB{i}", [P, GW]) for i in range(2)]
        Z = [sb(f"x_Z{i}", [P, GW]) for i in range(2)]
        RST, RMV, RV, RRS = (sb("x_RST", [P, NT_TILES, 6]), sb("x_RMV", [P, NT_TILES, 2]),
                             sb("x_RV", [P, NT_TILES]), sb("x_RRS", [P, NT_TILES]))
        GE = [sb(f"x_GE{i}", [P, GW]) for i in range(4)]
        GF = [sb(f"x_GF{i}", [P, GW]) for i in range(4)]
        GS = [sb(f"x_GS{i}", [P, 2, KC, GW], F32R) for i in range(2)]
        loaded = [sem(f"loaded{e}") for e in range(E8)]
        w_high, w_low, n_high, n_low = sem("w_high"), sem("w_low"), sem("n_high"), sem("n_low")

        def load(sp, e):
            sp.dma_start(W1[:, e % 2, :], w1_dram[e]).then_inc(loaded[e], 16)
            sp.dma_start(W2[:, e % 2, :], w2_dram[e].rearrange("p k d -> p (k d)")).then_inc(loaded[e], 16)

        def weights_high(act, e):
            act.wait_ge(loaded[e], 32)
            for raw, part in ((W1, WU), (W2, WD)):
                nc.scalar.activation(part[e % 2][:, 0, :], raw[:, e % 2, :], ACT.Copy).then_inc(w_high, 1)

        def weights_low(eng, tensor_tensor, e):
            for k, (raw, part) in enumerate(((W1, WU), (W2, WD))):
                eng.wait_ge(w_high, 2 * e + k + 1)
                tensor_tensor(part[e % 2][:, 1, :], raw[:, e % 2, :], part[e % 2][:, 0, :].bitcast(F32),
                                        ALU.subtract).then_inc(w_low, 1)
        (r_made, rv_ready, rr_ready, hr_ready, gelu_ready, r_turned, r_copied, lg_made, exp_wanted, exp_done) = (
            sem(n_) for n_ in ("r_made", "rv_ready", "rr_ready", "hr_ready", "gelu_ready", "r_turned", "r_copied",
                               "lg_made", "exp_wanted", "exp_done"))
        with nc.Block() as block:
            @block.sync
            def _(sp):
                for e in range(2):
                    load(sp, e)

            @block.tensor
            def _(pe):
                for t in range(NT_TILES):
                    last = nc.tensor.matmul(PS[t // 8][:, KR * (t % 8):KR * (t % 8) + KR], NTI[:, P * t:P * t + P],
                                            w("wr1"), start=True, stop=True)
                last.then_inc(r_made, 1)
                pe.wait_ge(gelu_ready, 1)
                for g in range(G):
                    for j in range(GT):
                        last = nc.tensor.transpose(PS[2 + g][0:KR, P * j:P * j + P], HR[:, GT * g + j, :], w("ident"))
                    last.then_inc(r_turned, 1)
                pe.wait_ge(r_copied, G)
                for t in range(NT_TILES):
                    last = nc.tensor.matmul(PS[6][:, E8 * t:E8 * t + E8], HRT[:, P * t:P * t + P], w("wr2", rows=KR),
                                            start=True, stop=True)
                last.then_inc(lg_made, 1)

            @block.scalar
            def _(act):
                for g in range(G):
                    nc.scalar.activation(NS[:, 0, GW * g:GW * g + GW], NTI[:, GW * g:GW * g + GW], ACT.Copy)\
                        .then_inc(n_high, 1)
                act.wait_ge(hr_ready, 1)
                nc.scalar.activation(HR[:, :, :], HR[:, :, :], ACT.Gelu_apprx_tanh).then_inc(gelu_ready, 1)
                for g in range(G):
                    act.wait_ge(r_turned, g + 1)
                    nc.scalar.activation(HRT[:, GW * g:GW * g + GW], PS[2 + g][0:KR, :], ACT.Copy).then_inc(r_copied, 1)
                for e in range(2):
                    weights_high(act, e)
                act.wait_ge(exp_wanted, 1)
                nc.scalar.activation(T.PB[:, :, :], T.A[:, :, :], ACT.Exp).then_inc(exp_done, 1)

            @block.gpsimd
            def _(pool):
                pool.wait_ge(rv_ready, 1)
                nc.gpsimd.tensor_tensor(RRS[:, :], RV[:, :], c.MHALF[:, 0:NT_TILES], ALU.pow).then_inc(rr_ready, 1)
                for g in range(G):
                    gs = slice(GW * g, GW * g + GW)
                    pool.wait_ge(n_high, g + 1)
                    nc.gpsimd.tensor_tensor(NS[:, 1, gs], NTI[:, gs], NS[:, 0, gs].bitcast(F32), ALU.subtract)\
                        .then_inc(n_low, 1)
                for e in range(2):
                    weights_low(pool, nc.gpsimd.tensor_tensor, e)

            @block.vector
            def _(v):
                tt, ts = nc.vector.tensor_tensor, nc.vector.tensor_scalar
                v.wait_ge(r_made, 1)
                for k in range(2):
                    last = tt(HR[:, 8 * k:8 * k + 8, :], PS[k][:, :].rearrange("p (t r) -> p t r", r=KR),
                              rep(w("br1"), 8), ALU.add)
                dve.link(v, last)
                for t in range(NT_TILES):
                    last = nc.vector.bn_stats(RST[:, t, :], HR[:, t, :])
                dve.link(v, last)
                for t in range(NT_TILES):
                    last = nc.vector.bn_aggr(RMV[:, t, :], RST[:, t, :])
                dve.link(v, last)
                ts(RV[:, :], RMV[:, :, 1], 1e-6, None, ALU.add).then_inc(rv_ready, 1)
                v.wait_ge(rr_ready, 1)
                for t in range(NT_TILES):
                    last = ts(HR[:, t, :], HR[:, t, :], RMV[:, t, 0:1], RRS[:, t:t + 1], ALU.subtract, ALU.mult)
                dve.link(v, last)
                dve.link(v, tt(HR[:, :, :], HR[:, :, :], rep(w("lns"), NT_TILES), ALU.mult))
                tt(HR[:, :, :], HR[:, :, :], rep(w("lnbi"), NT_TILES), ALU.add).then_inc(hr_ready, 1)
                expert_masks(c, v, SEL, SELF, MROWS)
                v.wait_ge(lg_made, 1)
                dve.link(v, tt(LG[:, :, :], PS[6][:, 0:NT_TILES * E8].rearrange("p (t e) -> p t e", e=E8),
                               rep(w("br2"), NT_TILES), ALU.add))
                softmax_top2(c, v, LG, T, (exp_wanted, exp_done))
                bc = lambda a: a[:, :].unsqueeze(2).to_broadcast([P, NT_TILES, E8])
                dve.link(v, tt(T.MX[:, :], T.M1[:, :], T.M2[:, :], ALU.add))
                dve.link(v, nc.vector.reciprocal(T.MX[:, :], T.MX[:, :]))
                tt(T.OH1[:, :, :], T.OH1[:, :, :], bc(T.M1), ALU.mult)
                dve.link(v, tt(T.OH2[:, :, :], T.OH2[:, :, :], bc(T.M2), ALU.mult))
                dve.link(v, tt(LG[:, :, :], T.OH1[:, :, :], T.OH2[:, :, :], ALU.add))
                dve.link(v, tt(LG[:, :, :], LG[:, :, :], bc(T.MX), ALU.mult))

        start_sums(c, "x", LG, ACC, c.W2S[:, D:2 * D], MT,
                   [sem(n_) for n_ in ("oh_turned", "oh_copied", "b_made", "b_copied")], True)
        x_made, ge_ready, g_ready, gh_ready, gl_ready, y_made, z_ready, mb_made, mb_ready, summed = (
            sem(n_) for n_ in ("x_made", "ge_ready", "g_ready", "gh_ready", "gl_ready", "y_made", "z_ready", "mb_made",
                               "mb_ready", "summed"))
        XB = (0, 2, 6)
        with nc.Block() as block:
            @block.sync
            def _(sp):
                for e in range(2, E8):
                    sp.wait_ge(w_low, 2 * (e - 1))
                    load(sp, e)

            @block.tensor
            def _(pe):
                for i in range(n + 1):
                    if i < n:
                        e, g = divmod(i, G)
                        if g == 0:
                            pe.wait_ge(w_low, 2 * (e + 1))
                        if i:
                            pe.wait_ge(mb_ready, i)
                        nc.tensor.matmul(PS[5][:, :], SEL[:, e, :], MT[:, GW * g:GW * g + GW],
                                         start=True, stop=True).then_inc(mb_made, 1)
                        for k in range(KC):
                            q = KC * i + k
                            if q >= 3:
                                pe.wait_ge(g_ready, q - 2)
                            for half in range(2):
                                for a, b in HL:
                                    last = nc.tensor.matmul(PS[XB[q % 3] + half][:, :],
                                                            WU[e % 2][:, a, F3 * half + P * k:F3 * half + P * k + P],
                                                            NS[:, b, GW * g:GW * g + GW],
                                                            start=((a, b) == HL[0]), stop=((a, b) == HL[-1]))
                            last.then_inc(x_made, 1)
                    if i:
                        e = (i - 1) // G
                        pe.wait_ge(gh_ready, KC * i)
                        pe.wait_ge(gl_ready, KC * i)
                        if i >= 2:
                            pe.wait_ge(z_ready, i - 1)
                        for k in range(KC):
                            for a, b in HL:
                                last = nc.tensor.matmul(PS[4][:, :], WD[e % 2][:, b, D * k:D * k + D],
                                                        GS[(i - 1) % 2][:, a, k, :],
                                                        start=(k == 0 and (a, b) == HL[0]),
                                                        stop=(k == KC - 1 and (a, b) == HL[-1]))
                        last.then_inc(y_made, 1)

            @block.scalar
            def _(act):
                for q in range(KC * n + 1):
                    if q < KC * n and q % KC == 0:
                        i = q // KC
                        act.wait_ge(mb_made, i + 1)
                        if i >= 2:
                            act.wait_ge(z_ready, i - 1)
                        nc.scalar.activation(MB[i % 2][:, :], PS[5][:, :], ACT.Copy).then_inc(mb_ready, 1)
                    if q < KC * n:
                        e, k = q // (KC * G), q % KC
                        act.wait_ge(x_made, q + 1)
                        if q >= 4:
                            act.wait_ge(g_ready, q - 3)
                        nc.scalar.activation(GE[q % 4][:, :], PS[XB[q % 3] + 1][:, :], ACT.Gelu_apprx_tanh,
                                             bias=w("b1g", 8 * e + KC + k, 1)).then_inc(ge_ready, 1)
                    if q:
                        p = q - 1
                        i, k = divmod(p, KC)
                        act.wait_ge(g_ready, q)
                        if i >= 2 and k == 0:
                            act.wait_ge(y_made, i - 1)
                        nc.scalar.activation(GS[i % 2][:, 0, k, :], GF[p % 4][:, :], ACT.Copy).then_inc(gh_ready, 1)
                    if q % (KC * G) == 2 * KC and 2 <= q // (KC * G) + 1 < E8:
                        e = q // (KC * G) + 1
                        act.wait_ge(y_made, G * (e - 1))
                        weights_high(act, e)

            @block.gpsimd
            def _(pool):
                def add(i):
                    gs = slice(GW * (i % G), GW * (i % G) + GW)
                    pool.wait_ge(z_ready, i + 1)
                    if i >= G:
                        pool.wait_ge(summed, i - G + 1)
                    nc.gpsimd.tensor_tensor(ACC[:, gs], ACC[:, gs], Z[i % 2][:, :], ALU.add).then_inc(summed, 1)

                for p in range(KC * n):
                    i, k = divmod(p, KC)
                    if i >= 2 and k == 2:
                        add(i - 2)
                    pool.wait_ge(gh_ready, p + 1)
                    nc.gpsimd.tensor_tensor(GS[i % 2][:, 1, k, :], GF[p % 4][:, :], GS[i % 2][:, 0, k, :].bitcast(F32),
                                            ALU.subtract).then_inc(gl_ready, 1)
                add(n - 2)
                add(n - 1)

            @block.vector
            def _(v):
                for i in range(n + 1):
                    if i < n:
                        e = i // G
                        for k in range(KC):
                            q = KC * i + k
                            v.wait_ge(ge_ready, q + 1)
                            if q >= 4:
                                v.wait_ge(gh_ready, q - 3)
                                v.wait_ge(gl_ready, q - 3)
                            nc.vector.scalar_tensor_tensor(GF[q % 4][:, :], PS[XB[q % 3]][:, :],
                                                           w("b1g", 8 * e + k, 1), GE[q % 4][:, :],
                                                           ALU.add, ALU.mult).then_inc(g_ready, 1)
                    if i:
                        v.wait_ge(y_made, i)
                        v.wait_ge(mb_ready, i)
                        if i >= 3:
                            v.wait_ge(summed, i - 2)
                        nc.vector.tensor_tensor(Z[(i - 1) % 2][:, :], PS[4][:, :], MB[(i - 1) % 2][:, :], ALU.mult)\
                            .then_inc(z_ready, 1)
                    if i % G == 2 and 2 <= i // G + 1 < E8:
                        weights_low(v, nc.vector.tensor_tensor, i // G + 1)

        nv0 = c.n_var
        acc_turned, acc_copied, x_final = sem("acc_turned"), sem("acc_copied"), sem("x_final")
        YF = W1[:, :, :].rearrange("p a (t d) -> p (a t) d", d=D)
        with nc.Block() as block:
            @block.sync
            def _(sp):
                for g in range(G):
                    sp.wait_ge(x_final, g + 1)
                    sp.dma_start(c.out[GT * g:GT * g + GT].rearrange("t p d -> p t d"),
                                 c.X[:, GT * g:GT * g + GT, :]).then_inc(c.out_stored, 16)
                sp.wait_ge(c.out_stored, 16 * G)

            @block.tensor
            def _(pe):
                for g in range(G):
                    for j in range(GT):
                        t = GT * g + j
                        last = nc.tensor.transpose(PS[g][:, P * j:P * j + P], ACC[:, P * t:P * t + P], w("ident"))
                    last.then_inc(acc_turned, 1)

            @block.scalar
            def _(act):
                for g in range(G):
                    act.wait_ge(acc_turned, g + 1)
                    nc.scalar.activation(YF[:, GT * g:GT * g + GT, :],
                                         PS[g][:, :].rearrange("p (t d) -> p t d", d=D), ACT.Copy)\
                        .then_inc(acc_copied, 1)
                act_tails(c, act, 2, nv0, c.n_front, lambda g: YF[:, GT * g:GT * g + GT, :])

            @block.gpsimd
            def _(pool):
                pool_tails(c, pool, 2, nv0, c.n_front, finish=True)

            @block.vector
            def _(v):
                def make(g):
                    v.wait_ge(acc_copied, g + 1)
                    return YF[:, GT * g:GT * g + GT, :]
                tails(c, v, make, finish=lambda g: v.sem_inc(x_final, 1))


def kernel(**inputs):
    import numpy as np
    import concourse.bacc as bacc
    from concourse.bass_utils import run_bass_kernel_spmd as run

    nc = bacc.Bacc("TRN2", target_bir_lowering=False, num_devices=1)
    arrays = host_layout(inputs)
    args = {}
    for name, a in arrays.items():
        args[name] = nc.dram_tensor(f"in_{name}", a.shape, mybir.dt.from_np(a.dtype), kind="ExternalInput").ap()
    out = nc.dram_tensor("out", (NT_TILES, P, D), F32, kind="ExternalOutput").ap()
    program(nc, args["x"], args["pack"], args["b2s"], args["l1w1"], args["l1w2"], args["l3w1"], args["l3w2"],
            out)
    r = run(nc, [{f"in_{k}": a for k, a in arrays.items()}], core_ids=[0])
    return r.results[0]["out"].reshape(B, S, D)


def host_layout(i):
    f = np.float32
    i = {k: np.asarray(a) for k, a in i.items()}
    rows = lambda a: np.broadcast_to(a.reshape(1, -1), (P, a.size))
    ar = np.arange(P)
    angle = 2 * np.pi * (np.outer(ar, ar) % P) / P
    chan = lambda a: np.repeat(a, D // a.size).reshape(P, 1)
    win = i["L1_attn_W_in"]
    bc = win[:, 512:1024].reshape(D, 2, H1, 32, 2).transpose(0, 1, 2, 4, 3).reshape(D, 512)
    cols = {
        "ident": np.eye(P), "ones": np.ones((P, P)),
        "wq0": i["L0_attn_w_qkv"][0:128].T, "wk0": i["L0_attn_w_qkv"][128:256].T,
        "wv0": i["L0_attn_w_qkv"][256:384].T, "wfc": i["L0_attn_w_fc"].T,
        "bfc": rows(i["L0_attn_b_fc"]), "gam0": rows(i["L0_attn_gamma"]), "bet0": rows(i["L0_attn_beta"]),
        "wr": i["L0_ffn_w_freq_real"], "wi": i["L0_ffn_w_freq_imag"],
        "cos": np.cos(angle), "sin": np.sin(angle), "nsin": -np.sin(angle), "fbias": rows(i["L0_ffn_bias"]),
        "win": np.concatenate([win[:, 0:512], bc, win[:, 1024:]], 1),
        "nw": i["L1_attn_norm_weight"].reshape(2, P).T,
        "wout": i["L1_attn_W_out"].reshape(2, P, D).transpose(1, 0, 2).reshape(P, 2 * D),
        "dtb": rows(i["L1_attn_dt_bias"]), "alog": rows(i["L1_attn_A_log"]),
        "freq": rows((1.0 / 10000.0 ** (np.arange(32, dtype=f) / f(32))).astype(f)),
        "upper": (ar[:, None] <= ar[None, :]), "below": (ar[:, None] > ar[None, :]),
        "shift": (ar[:, None] == ar[None, :] + 1), "first": (ar[:, None] == 0) & (ar[None, :] == P - 1),
        "mask": np.where(ar[:, None] > ar[None, :], f(-1e30), f(0.0)),
        "gw": i["L1_ffn_gate_W"], "gb": rows(i["L1_ffn_gate_b"]), "rank": rows(E8 - np.arange(E8, dtype=f)),
        "b1m": i["L1_ffn_b1"].reshape(E8, 2, P).transpose(2, 0, 1).reshape(P, 16),
        "lng": rows(i["L1_ffn_ln_gamma"]), "lnb": rows(i["L1_ffn_ln_beta"]),
        "mk": chan(i["L2_attn_mix_k"]), "mv": chan(i["L2_attn_mix_v"]), "mr": chan(i["L2_attn_mix_r"]),
        "wkey": i["L2_attn_W_key"].T, "wval": i["L2_attn_W_value"].T, "wrec": i["L2_attn_W_receptance"].T,
        "wo2": i["L2_attn_W_output"].T, "td": chan(i["L2_attn_time_decay"]), "tf": chan(i["L2_attn_time_first"]),
        "blocks": (ar[:, None] // 8 == ar[None, :] // 8), "time": rows(np.arange(S, dtype=f)),
        "w1f": i["L2_ffn_W1"], "b1f": i["L2_ffn_b1"].reshape(4, P).T,
        "w2f": i["L2_ffn_W2"].reshape(4, P, D).transpose(1, 0, 2).reshape(P, 4 * D), "b2f": rows(i["L2_ffn_b2"]),
        "wq3": i["L3_attn_Wq"].T, "wk3": i["L3_attn_Wk"].T, "wv3": i["L3_attn_Wv"].T, "wo3": i["L3_attn_Wo"].T,
        "bo3": rows(i["L3_attn_bo"]),
        "wr1": i["L3_ffn_Wr1"], "br1": rows(i["L3_ffn_br1"]), "lns": rows(i["L3_ffn_ln_scale"]),
        "lnbi": rows(i["L3_ffn_ln_bias"]),
        "wr2": np.concatenate([i["L3_ffn_Wr2"], i["L3_ffn_Wr2"]], 0), "br2": rows(i["L3_ffn_br2"]),
        "b1g": i["L3_ffn_b1"].reshape(E8, 8, P).transpose(2, 0, 1).reshape(P, 64),
    }
    pack = np.concatenate([np.asarray(cols[k]).astype(f).reshape(P, wd) for k, (_, wd) in PACK.items()], 1)
    return {
        "x": np.ascontiguousarray(i["L0_attn_x"].reshape(NT_TILES, P, D)),
        "pack": np.ascontiguousarray(pack),
        "b2s": np.ascontiguousarray(np.concatenate([i["L1_ffn_b2"], i["L3_ffn_b2"]], 1)),
        "l1w1": np.ascontiguousarray(i["L1_ffn_W1"]),
        "l1w2": np.ascontiguousarray(i["L1_ffn_W2"].reshape(E8, 2, P, D).transpose(0, 2, 1, 3)),
        "l3w1": np.ascontiguousarray(i["L3_ffn_W1"]),
        "l3w2": np.ascontiguousarray(i["L3_ffn_W2"].reshape(E8, 4, P, D).transpose(0, 2, 1, 3)),
    }
```
